# Optimizing a Trainium2 kernel written in Bass

```python
import numpy as np
import jax
import jax.numpy as jnp

def _softmax(x, axis=-1):
    return jax.nn.softmax(x, axis=axis)

def _gelu(x):
    return jax.nn.gelu(x, approximate=True)

def _silu(x):
    return jax.nn.silu(x)

def _sigmoid(x):
    return jax.nn.sigmoid(x)

def _layernorm(x, axis=-1, eps=1e-05):
    m = jnp.mean(x, axis=axis, keepdims=True)
    v = jnp.var(x, axis=axis, keepdims=True)
    return (x - m) / jnp.sqrt(v + eps)

def _scatter_add(tgt, idx, src, axis=0):
    return tgt.at[idx].add(src)

def _segment_sum(src, seg, n):
    return jax.ops.segment_sum(src, seg, n)
kernel_name = 'mk_gnn_preln_d2_gnn_r8_2cf044'

def setup_inputs(seed: int=0):
    np.random.seed(seed)
    _w = jnp.asarray

    def _rec_inputs():
        import jax
        import jax.numpy as jnp
        _gk = jax.random.key(seed)
        x = -0.0003713 + 1 * jax.random.normal(jax.random.fold_in(_gk, 1), (12500, 128), jnp.float32)
        src = jax.random.randint(jax.random.fold_in(_gk, 2), (200000,), 0, 12500, jnp.int32)
        dst = jnp.minimum((12500 * jax.random.uniform(jax.random.fold_in(_gk, 3), (200000,)) ** 2.0).astype(jnp.int32), 99999)
        _o = jnp.argsort(dst, stable=True)
        src = src[_o]
        dst = dst[_o]
        edge_attr_64 = 0.000149146 + 1.0001 * jax.random.normal(jax.random.fold_in(_gk, 11), (200000, 64), jnp.float32)
        edge_weight = jax.random.uniform(jax.random.fold_in(_gk, 13), (200000,), jnp.float32, 0.0, 999.998)
        node_vec = jax.random.uniform(jax.random.fold_in(_gk, 14), (12500,), jnp.float32, 0.0, 999.994)
        return (x, src, dst, edge_attr_64, edge_weight, node_vec)
    x, src, dst, edge_attr_64, edge_weight, node_vec = _rec_inputs()

    def _L0_gnn_setup():
        import jax, jax.numpy as jnp
        import numpy as np
        N = 12500
        E = 80000
        IN_CH = 128
        OUT_CH = 128
        MSG_DIM = 64
        TIME_DIM = 64
        EDGE_DIM = MSG_DIM + TIME_DIM
        HEADS = 4

        def _linear_params(key, fan_in, fan_out, bias=True, scale=0.02):
            k1, k2 = jax.random.split(key)
            W = jax.random.normal(k1, (fan_in, fan_out), jnp.float32) * scale
            if bias:
                b = jax.random.normal(k2, (fan_out,), jnp.float32) * scale
                return (W, b)
            return W

        def transformer_conv(x, src, dst, edge_attr, Wq, bq, Wk, bk, Wv, bv, We, Wskip, bskip):
            n = x.shape[0]
            HC = Wq.shape[1]
            C = HC // HEADS
            q = (x @ Wq + bq).reshape(n, HEADS, C)
            k = (x @ Wk + bk).reshape(n, HEADS, C)
            v = (x @ Wv + bv).reshape(n, HEADS, C)
            e = (edge_attr @ We).reshape(-1, HEADS, C)
            k_j = k[src] + e
            v_j = v[src] + e
            alpha = jnp.einsum('ehc,ehc->eh', q[dst], k_j) / jnp.sqrt(jnp.float32(C))
            amax = jax.ops.segment_max(alpha, dst, num_segments=n)
            expa = jnp.exp(alpha - amax[dst])
            denom = jax.ops.segment_sum(expa, dst, num_segments=n)
            attn = expa / (denom[dst] + 1e-16)
            out = jax.ops.segment_sum(attn[:, :, None] * v_j, dst, num_segments=n)
            out = out.reshape(n, HC)
            return out + x @ Wskip + bskip
        key = jax.random.key(seed)
        ks = jax.random.split(key, 16)
        inp = {'x': jax.random.normal(ks[0], (N, IN_CH), jnp.float32), 'last_update': jax.random.uniform(ks[1], (N,), jnp.float32) * 1000.0, 't': jax.random.uniform(ks[2], (E,), jnp.float32) * 1000.0, 'msg': jax.random.normal(ks[3], (E, MSG_DIM), jnp.float32), 'edge_index': jax.random.randint(ks[4], (2, E), 0, N, jnp.int64)}
        inp['Wt'], inp['bt'] = _linear_params(ks[5], 1, TIME_DIM)
        HC1 = HEADS * (IN_CH // 4)
        inp['Wq1'], inp['bq1'] = _linear_params(ks[6], IN_CH, HC1)
        inp['Wk1'], inp['bk1'] = _linear_params(ks[7], IN_CH, HC1)
        inp['Wv1'], inp['bv1'] = _linear_params(ks[8], IN_CH, HC1)
        inp['We1'] = _linear_params(ks[9], EDGE_DIM, HC1, bias=False)
        inp['Wskip1'], inp['bskip1'] = _linear_params(ks[10], IN_CH, HC1)
        HC2 = HEADS * (OUT_CH // 4)
        inp['Wq2'], inp['bq2'] = _linear_params(ks[11], IN_CH, HC2)
        inp['Wk2'], inp['bk2'] = _linear_params(ks[12], IN_CH, HC2)
        inp['Wv2'], inp['bv2'] = _linear_params(ks[13], IN_CH, HC2)
        inp['We2'] = _linear_params(ks[14], EDGE_DIM, HC2, bias=False)
        inp['Wskip2'], inp['bskip2'] = _linear_params(ks[15], IN_CH, HC2)
        return inp
    _L0_gnn_all = _L0_gnn_setup()
    _L0_gnn_in = {k: v for k, v in _L0_gnn_all.items() if k in ('Wt', 'bt', 'Wq1', 'bq1', 'Wk1', 'bk1', 'Wv1', 'bv1', 'We1', 'Wskip1', 'bskip1', 'Wq2', 'bq2', 'Wk2', 'bk2', 'Wv2', 'bv2', 'We2', 'Wskip2', 'bskip2')}
    del _L0_gnn_all

    def _L1_gnn_setup():
        import jax, jax.numpy as jnp
        import numpy as np
        NUM_LAYERS = 3
        HIDDEN = 128
        N_NODES = 6250
        N_EDGES = 75000
        key = jax.random.key(seed)
        ks = jax.random.split(key, 5)
        x = jax.random.normal(ks[0], (N_NODES, HIDDEN), dtype=jnp.float32)
        edge_index = jax.random.randint(ks[1], (2, N_EDGES), 0, N_NODES, dtype=jnp.int32)
        scale = 1.0 / np.sqrt(HIDDEN)
        Wl = jax.random.uniform(ks[2], (NUM_LAYERS, HIDDEN, HIDDEN), jnp.float32, -scale, scale)
        bl = jnp.zeros((NUM_LAYERS, HIDDEN), dtype=jnp.float32)
        Wr = jax.random.uniform(ks[3], (NUM_LAYERS, HIDDEN, HIDDEN), jnp.float32, -scale, scale)
        return {'x': x, 'edge_index': edge_index, 'Wl': Wl, 'bl': bl, 'Wr': Wr}
    _L1_gnn_all = _L1_gnn_setup()
    _L1_gnn_in = {k: v for k, v in _L1_gnn_all.items() if k in ('Wl', 'bl', 'Wr')}
    del _L1_gnn_all
    return {'x': x, 'src': src, 'dst': dst, 'edge_attr_64': edge_attr_64, 'edge_weight': edge_weight, 'node_vec': node_vec, 'L0_gnn_Wt': _L0_gnn_in['Wt'], 'L0_gnn_bt': _L0_gnn_in['bt'], 'L0_gnn_Wq1': _L0_gnn_in['Wq1'], 'L0_gnn_bq1': _L0_gnn_in['bq1'], 'L0_gnn_Wk1': _L0_gnn_in['Wk1'], 'L0_gnn_bk1': _L0_gnn_in['bk1'], 'L0_gnn_Wv1': _L0_gnn_in['Wv1'], 'L0_gnn_bv1': _L0_gnn_in['bv1'], 'L0_gnn_We1': _L0_gnn_in['We1'], 'L0_gnn_Wskip1': _L0_gnn_in['Wskip1'], 'L0_gnn_bskip1': _L0_gnn_in['bskip1'], 'L0_gnn_Wq2': _L0_gnn_in['Wq2'], 'L0_gnn_bq2': _L0_gnn_in['bq2'], 'L0_gnn_Wk2': _L0_gnn_in['Wk2'], 'L0_gnn_bk2': _L0_gnn_in['bk2'], 'L0_gnn_Wv2': _L0_gnn_in['Wv2'], 'L0_gnn_bv2': _L0_gnn_in['bv2'], 'L0_gnn_We2': _L0_gnn_in['We2'], 'L0_gnn_Wskip2': _L0_gnn_in['Wskip2'], 'L0_gnn_bskip2': _L0_gnn_in['bskip2'], 'L1_gnn_Wl': _L1_gnn_in['Wl'], 'L1_gnn_bl': _L1_gnn_in['bl'], 'L1_gnn_Wr': _L1_gnn_in['Wr']}

def reference(x, src, dst, edge_attr_64, edge_weight, node_vec, L0_gnn_Wt, L0_gnn_bt, L0_gnn_Wq1, L0_gnn_bq1, L0_gnn_Wk1, L0_gnn_bk1, L0_gnn_Wv1, L0_gnn_bv1, L0_gnn_We1, L0_gnn_Wskip1, L0_gnn_bskip1, L0_gnn_Wq2, L0_gnn_bq2, L0_gnn_Wk2, L0_gnn_bk2, L0_gnn_Wv2, L0_gnn_bv2, L0_gnn_We2, L0_gnn_Wskip2, L0_gnn_bskip2, L1_gnn_Wl, L1_gnn_bl, L1_gnn_Wr):
    import jax
    import jax.numpy as jnp

    def _L0_gnn_ref(x, last_update, t, msg, edge_index, Wt, bt, Wq1, bq1, Wk1, bk1, Wv1, bv1, We1, Wskip1, bskip1, Wq2, bq2, Wk2, bk2, Wv2, bv2, We2, Wskip2, bskip2):
        import jax, jax.numpy as jnp
        import numpy as np
        N = 12500
        E = 80000
        IN_CH = 128
        OUT_CH = 128
        MSG_DIM = 64
        TIME_DIM = 64
        EDGE_DIM = MSG_DIM + TIME_DIM
        HEADS = 4

        def _linear_params(key, fan_in, fan_out, bias=True, scale=0.02):
            k1, k2 = jax.random.split(key)
            W = jax.random.normal(k1, (fan_in, fan_out), jnp.float32) * scale
            if bias:
                b = jax.random.normal(k2, (fan_out,), jnp.float32) * scale
                return (W, b)
            return W

        def transformer_conv(x, src, dst, edge_attr, Wq, bq, Wk, bk, Wv, bv, We, Wskip, bskip):
            n = x.shape[0]
            HC = Wq.shape[1]
            C = HC // HEADS
            q = (x @ Wq + bq).reshape(n, HEADS, C)
            k = (x @ Wk + bk).reshape(n, HEADS, C)
            v = (x @ Wv + bv).reshape(n, HEADS, C)
            e = (edge_attr @ We).reshape(-1, HEADS, C)
            k_j = k[src] + e
            v_j = v[src] + e
            alpha = jnp.einsum('ehc,ehc->eh', q[dst], k_j) / jnp.sqrt(jnp.float32(C))
            amax = jax.ops.segment_max(alpha, dst, num_segments=n)
            expa = jnp.exp(alpha - amax[dst])
            denom = jax.ops.segment_sum(expa, dst, num_segments=n)
            attn = expa / (denom[dst] + 1e-16)
            out = jax.ops.segment_sum(attn[:, :, None] * v_j, dst, num_segments=n)
            out = out.reshape(n, HC)
            return out + x @ Wskip + bskip
        src, dst = (edge_index[0], edge_index[1])
        rel_t = last_update[src] - t
        rel_t_enc = jnp.cos(rel_t[:, None] * Wt[0][None, :] + bt)
        edge_attr = jnp.concatenate([rel_t_enc, msg], axis=-1)
        h = transformer_conv(x, src, dst, edge_attr, Wq1, bq1, Wk1, bk1, Wv1, bv1, We1, Wskip1, bskip1)
        return transformer_conv(h, src, dst, edge_attr, Wq2, bq2, Wk2, bk2, Wv2, bv2, We2, Wskip2, bskip2)

    def _L1_gnn_ref(x, edge_index, Wl, bl, Wr):
        import jax, jax.numpy as jnp
        import numpy as np
        NUM_LAYERS = 3
        HIDDEN = 128
        N_NODES = 6250
        N_EDGES = 75000
        src = edge_index[0]
        dst = edge_index[1]
        n = x.shape[0]
        deg = jax.ops.segment_sum(jnp.ones(src.shape[0], dtype=x.dtype), dst, num_segments=n)
        inv_deg = (1.0 / jnp.maximum(deg, 1.0))[:, None]
        h = x
        for i in range(NUM_LAYERS):
            agg = jax.ops.segment_sum(h[src], dst, num_segments=n) * inv_deg
            h = agg @ Wl[i].T + bl[i] + h @ Wr[i].T
            if i < NUM_LAYERS - 1:
                h = jax.nn.relu(h)
        return h
    edge_index = jnp.stack([src, dst])
    h = jnp.maximum(_layernorm(x, axis=-1), 0.0)
    x = x + _L0_gnn_ref(h, node_vec, edge_weight, edge_attr_64, edge_index, L0_gnn_Wt, L0_gnn_bt, L0_gnn_Wq1, L0_gnn_bq1, L0_gnn_Wk1, L0_gnn_bk1, L0_gnn_Wv1, L0_gnn_bv1, L0_gnn_We1, L0_gnn_Wskip1, L0_gnn_bskip1, L0_gnn_Wq2, L0_gnn_bq2, L0_gnn_Wk2, L0_gnn_bk2, L0_gnn_Wv2, L0_gnn_bv2, L0_gnn_We2, L0_gnn_Wskip2, L0_gnn_bskip2)
    h = jnp.maximum(_layernorm(x, axis=-1), 0.0)
    x = x + _L1_gnn_ref(h, edge_index, L1_gnn_Wl, L1_gnn_bl, L1_gnn_Wr)
    return x

_drawn_inputs = setup_inputs


def setup_inputs(seed=0):
    import zlib

    import numpy as np

    out = dict(_drawn_inputs(seed))
    spreads = {'L1_gnn_bl': (0.0, 0.1)}
    factors = {'L0_gnn_bt': 64.0,
     'L0_gnn_Wq1': 8.0,
     'L0_gnn_bq1': 64.0,
     'L0_gnn_Wk1': 8.0,
     'L0_gnn_bk1': 64.0,
     'L0_gnn_bv1': 8.0,
     'L0_gnn_bskip1': 8.0,
     'L0_gnn_Wq2': 37.357,
     'L0_gnn_bq2': 64.0,
     'L0_gnn_Wk2': 42.146,
     'L0_gnn_bk2': 64.0,
     'L0_gnn_bv2': 2.781,
     'L0_gnn_bskip2': 3.132}
    for name, (base, spread) in spreads.items():
        noise = np.random.default_rng([zlib.crc32(name.encode()), seed]).standard_normal(out[name].shape)
        drawn = base * np.exp(spread * noise) if base else spread * noise
        out[name] = jnp.asarray(drawn.astype(out[name].dtype))
    for name, factor in factors.items():
        out[name] = (out[name] * factor).astype(out[name].dtype)
    return out
```

```python
from contextlib import ExitStack, contextmanager

import concourse.bass as bass
from concourse import mybir

F32 = mybir.dt.float32
BF16 = mybir.dt.bfloat16
I32 = mybir.dt.int32
ALU = mybir.AluOpType
ACT = mybir.ActivationFunctionType
AX = mybir.AxisListType

D = 128
HEADS = 4
C = D // HEADS
MSG = 64
EP = 128
NP = 125
GR = 4
NG = 16
RING = 4
KVW = 2 * D + 4
ACW = D + HEADS
BIG = 1.0e30
ROUND = 12582912.0
TWO_PI_HI = 6.28125
TWO_PI_LO = 0.0019353071795864769
INV_TWO_PI = 0.15915494309189535
HALF_PI = 1.5707963267948966


class Shapes:

    def __init__(self, x, src):
        self.N = x.shape[0]
        self.NB = self.N // NP
        self.T = src.shape[0]
        self.NQ = -(-(self.T + self.NB) // NG)
        self.I = NG * self.NQ
        self.G = self.I // GR
        assert self.N % NP == 0 and self.NB % 4 == 0 and self.NQ <= 128


class Store:
    pass


class Chain:

    def __init__(self, engine, sem):
        self.engine, self.sem, self.n = engine, sem, 0

    def link(self, instruction):
        self.n += 1
        instruction.then_inc(self.sem, 1)
        self.engine.wait_ge(self.sem, self.n)


def at_least(engine, sem, value):
    if not isinstance(value, int) or value > 0:
        engine.wait_ge(sem, value)


def reached(n, back=0):
    return not isinstance(n, int) or n - back >= 0


def pipeline(engine, count, lag, step):
    for n in range(RING):
        step(n, n)
    if count // RING > 1:
        with engine.Fori(1, count // RING) as it:
            for u in range(RING):
                step(it * RING + u, u)
    for n in range(count, count + lag):
        step(n, n % RING)


@contextmanager
def phase(nc, k):
    made = []

    def sem(name):
        made.append(nc.alloc_semaphore(name=k.tag + name))
        return made[-1]

    with ExitStack() as c:
        yield c, sem
    nc.clear_and_free_semaphores(made)
    nc.all_engine_barrier()


def constants(nc, k):
    with phase(nc, k) as (c, sem):
        made, cast = sem("const_made"), sem("const_cast")
        block = c.enter_context(nc.Block())


        @block.gpsimd
        def _(pool):
            pool.memset(k.ident[:, :], 0.0).then_inc(made, 1)
            pool.wait_ge(made, 1)
            pool.affine_select(out=k.ident[:, :], in_=k.ident[:, :], compare_op=ALU.not_equal, fill=1.0,
                               base=0, pattern=[[-1, 128]], channel_multiplier=1).then_inc(made, 1)
            pool.iota(k.node_iota_i[:, :], pattern=[[1, NP]], base=0, channel_multiplier=0).then_inc(made, 1)
            pool.memset(k.half_pi[:, :], HALF_PI)
            pool.memset(k.quarter[:, :], 0.25)
            pool.memset(k.plus_round[:, :], ROUND)
            pool.memset(k.minus_round[:, :], -ROUND)
            pool.memset(k.zero[:, :], 0.0)
            pool.memset(k.ones[:, :], 1.0)
            pool.memset(k.eps[:, :], 1e-5).then_inc(made, 1)

        @block.vector
        def _(dve):
            dve.wait_ge(made, 4)
            dve.tensor_copy(k.ident_b[:, :], k.ident[:, :])
            dve.tensor_copy(k.node_iota[:, :], k.node_iota_i[:, :]).then_inc(cast, 1)
            dve.wait_ge(cast, 1)
            dve.tensor_copy(k.node_iota_b[:, :], k.node_iota[:, :]).then_inc(cast, 1)
            dve.wait_ge(cast, 2)


def item_tables(nc, k, s, a):
    NQ, T, I = s.NQ, s.T, s.I
    SL = NG * EP
    with phase(nc, k) as (c, sem):
        def sb(name, shape, dt=F32):
            return c.enter_context(nc.sbuf_tensor(k.tag + name, shape, dt))

        last_i = sb("last_i", [1, T], I32)
        tile_i = sb("tile_i", [1, T], I32)
        last_f = sb("last_f", [1, T])
        tile_f = sb("tile_f", [1, T])
        leave = sb("leave", [1, T])
        leave_all = sb("leave_all", [128, T])
        junk = sb("junk", [128, T])
        item_i = sb("item_i", [128, NG], I32)
        item_f = sb("item_f", [128, NG])
        tile_of = sb("tile_of", [128, NG])
        block_of = sb("block_of", [128, NG])
        tile_of_i = sb("tile_of_i", [128, NG], I32)
        block_of_i = sb("block_of_i", [128, NG], I32)
        base = sb("base", [128, NG])
        src_q = sb("src_q", [128, NG, EP], I32)
        dst_q = sb("dst_q", [128, NG, EP], I32)
        weight_q = sb("weight_q", [128, NG, EP])
        src_f = sb("src_f", [128, NG, EP])
        dst_f = sb("dst_f", [128, NG, EP])
        local = sb("local", [128, NG, EP])
        valid = sb("valid", [128, NG, EP])
        ps_row = c.enter_context(nc.psum_tensor("ps_row", [128, 4, 512], F32))
        ps_t = [c.enter_context(nc.psum_tensor(k.tag + f"ps_t{i}", [128, 4, 128], F32)) for i in range(2)]

        loaded, iotas, leave_done, row_ready, row_copied = map(sem, ["loaded", "iotas", "leave_done", "row_ready", "row_copied"])
        tiles_known, tiles_stored, tiles_back = map(sem, ["tiles_known", "tiles_stored", "tiles_back"])
        src_in, dst_in, weight_in = map(sem, ["src_in", "dst_in", "weight_in"])
        cast_done, local_done, own, turned, placed = map(sem, ["cast_done", "local_done", "own", "turned", "placed"])
        block = c.enter_context(nc.Block())

        @block.sync
        def _(sp):
            sp.dma_start(last_i[:, :], a.dst[:, EP - 1:EP].rearrange("t o -> o t"),
                         allow_slow_non_contiguous=True).then_inc(loaded, 16)
            sp.wait_ge(tiles_known, 1)
            sp.dma_start(k.d_tile_of.rearrange("(q g) -> q g", g=NG), tile_of_i[0:NQ, :]).then_inc(tiles_stored, 16)
            sp.dma_start(k.d_block_of.rearrange("(q g) -> q g", g=NG), block_of_i[0:NQ, :]).then_inc(tiles_stored, 16)
            sp.wait_ge(tiles_stored, 32)
            sp.dma_start(k.tile_row[:, :], k.d_tile_of.rearrange("(o i) -> o i", o=1)).then_inc(tiles_back, 16)
            sp.dma_start(k.block_row[:, :], k.d_block_of.rearrange("(o i) -> o i", o=1)).then_inc(tiles_back, 16)
            sp.wait_ge(tiles_back, 32)

        @block.gpsimd
        def _(pool):
            pool.memset(k.src[:, I:I + RING * GR], 0)
            pool.iota(tile_i[:, :], pattern=[[1, T]], base=0, channel_multiplier=0)
            pool.iota(item_i[:, :], pattern=[[1, NG]], base=0, channel_multiplier=NG).then_inc(iotas, 1)
            pool.wait_ge(tiles_known, 1)
            for g in range(NG):
                for table, out, done in ((a.dst, dst_q, dst_in), (a.src, src_q, src_in), (a.weight, weight_q, weight_in)):
                    pool.indirect_dma_start(out[0:NQ, g, :], None, table,
                                            bass.IndirectOffsetOnAxis(ap=tile_of_i[0:NQ, g:g + 1], axis=0)).then_inc(done, 16)

        @block.vector
        def _(dve):
            ch = Chain(dve, own)
            dve.wait_ge(iotas, 1)
            dve.tensor_copy(tile_f[:, :], tile_i[:, :])
            dve.tensor_copy(item_f[:, :], item_i[:, :])
            dve.wait_ge(loaded, 16)
            ch.link(dve.tensor_copy(last_f[:, :], last_i[:, :]))
            ch.link(dve.tensor_scalar(last_f[:, :], last_f[:, :], 1.0 / NP, 0.5 / NP - 0.5, ALU.mult, ALU.add))
            ch.link(dve.tensor_scalar(last_f[:, :], last_f[:, :], ROUND, ROUND, ALU.add, ALU.subtract))
            dve.tensor_tensor(leave[:, :], last_f[:, :], tile_f[:, :], ALU.add).then_inc(leave_done, 1)
            dve.wait_ge(row_copied, 1)
            for g in range(NG):
                last = dve.tensor_scalar(junk[0:NQ, :], leave_all[0:NQ, :], item_f[0:NQ, g:g + 1], 0.0,
                                         ALU.is_lt, ALU.add, accum_out=tile_of[0:NQ, g:g + 1])
                ch.link(last)
            ch.link(dve.tensor_scalar(tile_of[0:NQ, :], tile_of[0:NQ, :], float(T - 1), None, ALU.min))
            ch.link(dve.tensor_tensor(block_of[0:NQ, :], item_f[0:NQ, :], tile_of[0:NQ, :], ALU.subtract))
            ch.link(dve.tensor_scalar(block_of[0:NQ, :], block_of[0:NQ, :], float(s.NB), None, ALU.min))
            dve.tensor_copy(tile_of_i[0:NQ, :], tile_of[0:NQ, :])
            dve.tensor_copy(block_of_i[0:NQ, :], block_of[0:NQ, :]).then_inc(tiles_known, 1)
            ch.link(dve.tensor_scalar(base[0:NQ, :], block_of[0:NQ, :], float(NP), None, ALU.mult))
            dve.wait_ge(dst_in, 16 * NG)
            ch.link(dve.tensor_copy(dst_f[0:NQ, :, :], dst_q[0:NQ, :, :]))
            ch.link(dve.tensor_tensor(local[0:NQ, :, :], dst_f[0:NQ, :, :],
                                      base[0:NQ, :].unsqueeze(2).broadcast_to([NQ, NG, EP]), ALU.subtract))
            dve.wait_ge(src_in, 16 * NG)
            dve.tensor_copy(src_f[0:NQ, :, :], src_q[0:NQ, :, :]).then_inc(local_done, 1)
            ch.link(dve.tensor_scalar(valid[0:NQ, :, :], local[0:NQ, :, :], 0.0, None, ALU.is_ge))
            ch.link(dve.scalar_tensor_tensor(valid[0:NQ, :, :], local[0:NQ, :, :], float(NP), valid[0:NQ, :, :],
                                             ALU.is_lt, ALU.mult))
            ch.link(dve.scalar_tensor_tensor(dst_f[0:NQ, :, :], dst_f[0:NQ, :, :], 1.0, valid[0:NQ, :, :],
                                             ALU.add, ALU.mult))
            ch.link(dve.tensor_scalar(k.key[0:NQ, :], dst_f[0:NQ, :, :].rearrange("q g e -> q (g e)"), -1.0, None, ALU.add))

        order = [(t, g4) for t in range(3) for g4 in range(NG // 4)]

        @block.tensor
        def _(pe):
            pe.wait_ge(leave_done, 1)
            for i in range(-(-T // 512)):
                w = min(512, T - 512 * i)
                last = pe.matmul(ps_row[0:NQ, i, 0:w], k.ones[0:1, 0:NQ], leave[:, 512 * i:512 * i + w], start=True, stop=True)
            last.then_inc(row_ready, 1)
            pe.wait_ge(local_done, 1)
            pe.wait_ge(weight_in, 16 * NG)
            for j, (t, g4) in enumerate(order):
                table = (local, src_f, weight_q)[t]
                at_least(pe, placed, j - 1)
                for g in range(4):
                    last = pe.transpose(ps_t[j % 2][:, g, 0:NQ], table[0:NQ, 4 * g4 + g, :], k.ident[0:NQ, 0:NQ])
                last.then_inc(turned, 1)

        @block.scalar
        def _(act):
            act.wait_ge(row_ready, 1)
            for i in range(-(-T // 512)):
                w = min(512, T - 512 * i)
                last = act.copy(leave_all[0:NQ, 512 * i:512 * i + w], ps_row[0:NQ, i, 0:w])
            last.then_inc(row_copied, 1)
            for j, (t, g4) in enumerate(order):
                table = (k.local, k.src, k.weight)[t]
                act.wait_ge(turned, j + 1)
                act.copy(table[:, 0:I].rearrange("p (q g) -> p g q", g=NG)[:, 4 * g4:4 * g4 + 4, :],
                         ps_t[j % 2][:, :, 0:NQ]).then_inc(placed, 1)
            act.wait_ge(placed, len(order))


def layer_norm(nc, k, s):
    NB = s.NB
    with phase(nc, k) as (c, sem):
        def sb(name, shape, dt=F32):
            return c.enter_context(nc.sbuf_tensor(k.tag + name, shape, dt))

        stats = sb("ln_stats", [128, NB, 6])
        moments = sb("ln_moments", [128, NB, 2])
        std = sb("ln_std", [128, NB])
        rstd = sb("ln_rstd", [128, NB])
        shift = sb("ln_shift", [128, NB])
        own = sem("ln_own")
        var_done = sem("ln_var_done")
        std_done = sem("ln_std_done")
        scale_done = sem("ln_scale_done")
        applied = sem("ln_applied")
        block = c.enter_context(nc.Block())

        @block.vector
        def _(dve):
            with dve.Fori(0, NB // 2) as it:
                for u in range(2):
                    b = it * 2 + u
                    dve.bn_stats(stats[0:NP, bass.ds(b, 1), :].rearrange("p a d -> p (a d)"),
                                 k.nodes[0:NP, bass.ds(b, 1), 0:D].rearrange("p a d -> p (a d)")).then_inc(own, 1)
            dve.wait_ge(own, NB)
            for b in range(NB):
                last = dve.bn_aggr(moments[0:NP, b, :], stats[0:NP, b, :])
            last.then_inc(var_done, 1)
            dve.wait_ge(std_done, 1)
            dve.reciprocal(rstd[0:NP, :], std[0:NP, :]).then_inc(own, 1)
            dve.wait_ge(own, NB + 1)
            dve.scalar_tensor_tensor(shift[0:NP, :], moments[0:NP, :, 0], -1.0, rstd[0:NP, :],
                                     ALU.mult, ALU.mult).then_inc(scale_done, 1)

        @block.scalar
        def _(act):
            act.wait_ge(var_done, 1)
            act.activation(std[0:NP, :], moments[0:NP, :, 1], ACT.Sqrt, bias=k.eps[0:NP, :]).then_inc(std_done, 1)
            act.wait_ge(scale_done, 1)
            with act.Fori(0, NB // 2) as it:
                for u in range(2):
                    b = it * 2 + u
                    row = k.nodes[0:NP, bass.ds(b, 1), 0:D].rearrange("p a d -> p (a d)")
                    act.activation(row, row, ACT.Relu, bias=shift[0:NP, bass.ds(b, 1)],
                                   scale=rstd[0:NP, bass.ds(b, 1)]).then_inc(applied, 1)
            act.wait_ge(applied, NB)


def load_nodes(nc, k, s, a):
    with phase(nc, k) as (c, sem):
        vec_rows = c.enter_context(nc.sbuf_tensor("vec_rows", [128, NP], F32))
        ps = c.enter_context(nc.psum_tensor("ps_vec", [128, 128], F32))
        x_in, vec_in, turned, copied = [sem(n) for n in ("x_in", "vec_in", "vec_turned", "vec_copied")]
        block = c.enter_context(nc.Block())

        @block.sync
        def _(sp):
            sp.dma_start(vec_rows[0:s.NB, :], a.vec.rearrange("(b p) -> b p", p=NP)).then_inc(vec_in, 16)
            sp.dma_start(k.nodes[0:NP, 0:s.NB, 0:D], a.x.rearrange("(b p) d -> p b d", p=NP)).then_inc(x_in, 16)
            sp.wait_ge(x_in, 16)

        @block.tensor
        def _(pe):
            pe.wait_ge(vec_in, 16)
            pe.transpose(ps[0:NP, 0:s.NB], vec_rows[0:s.NB, :], k.ident[0:s.NB, 0:s.NB]).then_inc(turned, 1)

        @block.vector
        def _(dve):
            dve.wait_ge(turned, 1)
            dve.tensor_copy(k.vec[0:NP, :], ps[0:NP, 0:s.NB]).then_inc(copied, 1)
            dve.wait_ge(copied, 1)


def project_nodes(nc, k, s, w):
    NB = s.NB
    with phase(nc, k) as (c, sem):
        def sb(name, shape, dt=F32):
            return c.enter_context(nc.sbuf_tensor(k.tag + name, shape, dt))

        weights = sb("pr_weights", [128, 4 * D])
        bias = sb("pr_bias", [128, 4 * D])
        turned_sb = sb("pr_turned", [128, 2, NP])
        still = sb("pr_still", [128, 2, D])
        kv = sb("pr_kv", [128, 2, KVW])
        skip = sb("pr_skip", [128, 2, D])
        ps_t = [c.enter_context(nc.psum_tensor(k.tag + f"pr_ps_t{i}", [128, 512], F32)) for i in range(2)]
        ps_p = [c.enter_context(nc.psum_tensor(k.tag + f"pr_ps_p{i}", [128, 512], F32)) for i in range(2)]
        loaded, stilled, turned, copied, projected, added, vec_put, zeroed = map(
            sem, ["pr_loaded", "pr_stilled", "pr_turned_s", "pr_copied", "pr_projected", "pr_added", "pr_vec_put", "pr_zeroed"])
        kv_out = [sem(f"pr_kv_out{i}") for i in range(2)]
        skip_out = [sem(f"pr_skip_out{i}") for i in range(2)]
        block = c.enter_context(nc.Block())

        def steps(engine, step):
            for b in range(2):
                step(b, b)
            with engine.Fori(1, NB // 2) as it:
                for u in range(2):
                    step(it * 2 + u, u)

        @block.sync
        def _(sp):
            for i in range(4):
                sp.dma_start(weights[:, D * i:D * i + D], w.weights[i]).then_inc(loaded, 16)
                sp.dma_start(bias[:, D * i:D * i + D], w.biases[i].rearrange("(o d) -> o d", o=1).broadcast_to([128, D])).then_inc(loaded, 16)

            def step(b, u):
                sp.wait_ge(added, b + 1)
                sp.wait_ge(vec_put, b + 1)
                sp.dma_start(k.d_kv.rearrange("(b p) d -> p b d", p=NP)[:, bass.ds(b, 1), :].rearrange("p a d -> p (a d)"),
                             kv[0:NP, u, :]).then_inc(kv_out[u], 16)
                sp.dma_start(k.d_skip.rearrange("(b p) d -> p b d", p=NP)[:, bass.ds(b, 1), :].rearrange("p a d -> p (a d)"),
                             skip[0:NP, u, :]).then_inc(skip_out[u], 16)

            steps(sp, step)
            for u in range(2):
                sp.wait_ge(kv_out[u], 16 * (NB // 2))
                sp.wait_ge(skip_out[u], 16 * (NB // 2))

        @block.tensor
        def _(pe):
            pe.wait_ge(loaded, 128)

            def step(b, u):
                pe.wait_ge(stilled, b + 1)
                if reached(b, 2):
                    pe.wait_ge(copied, b - 1)
                pe.transpose(ps_t[u][:, 0:NP], still[0:NP, u, :],
                             k.ident[0:NP, 0:NP]).then_inc(turned, 1)
                pe.wait_ge(copied, b + 1)
                if reached(b, 2):
                    pe.wait_ge(added, b - 1)
                pe.matmul(ps_p[u][0:NP, :], turned_sb[:, u, :], weights[:, :], start=True, stop=True).then_inc(projected, 1)

            steps(pe, step)

        @block.gpsimd
        def _(pool):
            def step(b, u):
                if reached(b, 2):
                    pool.wait_ge(turned, b - 1)
                pool.tensor_copy(still[0:NP, u, :], k.nodes[0:NP, bass.ds(b, 1), 0:D].rearrange("p a d -> p (a d)")).then_inc(stilled, 1)

            steps(pool, step)

        @block.scalar
        def _(act):
            def step(b, u):
                act.wait_ge(turned, b + 1)
                if reached(b, 2):
                    act.wait_ge(projected, b - 1)
                act.copy(turned_sb[:, u, :], ps_t[u][:, 0:NP]).then_inc(copied, 1)
                if reached(b, 2):
                    act.wait_ge(kv_out[u], (b // 2) * 16 if isinstance(b, int) else (b - u) * 8)
                act.copy(kv[0:NP, u, 2 * D:2 * D + 1], k.vec[0:NP, bass.ds(b, 1)]).then_inc(vec_put, 1)

            act.wait_ge(zeroed, 1)
            steps(act, step)

        @block.vector
        def _(dve):
            dve.memset(kv[:, :, :], 0.0)
            dve.memset(k.query[:, NB, :], 0.0).then_inc(zeroed, 1)
            dve.wait_ge(loaded, 128)
            dve.wait_ge(zeroed, 1)

            def step(b, u):
                dve.wait_ge(projected, b + 1)
                if reached(b, 2):
                    dve.wait_ge(kv_out[u], (b // 2) * 16 if isinstance(b, int) else (b - u) * 8)
                    dve.wait_ge(skip_out[u], (b // 2) * 16 if isinstance(b, int) else (b - u) * 8)
                dve.tensor_tensor(k.query[0:NP, bass.ds(b, 1), 0:D].rearrange("p a d -> p (a d)"), ps_p[u][0:NP, 0:D], bias[0:NP, 0:D], ALU.add)
                dve.tensor_tensor(kv[0:NP, u, 0:2 * D], ps_p[u][0:NP, D:3 * D], bias[0:NP, D:3 * D], ALU.add)
                dve.tensor_tensor(skip[0:NP, u, :], ps_p[u][0:NP, 3 * D:4 * D], bias[0:NP, 3 * D:4 * D],
                                  ALU.add).then_inc(added, 1)

            steps(dve, step)


def edge_scores(nc, k, s, a, w, first):
    NGR = s.G
    with phase(nc, k) as (c, sem):
        def sb(name, shape, dt=F32):
            return c.enter_context(nc.sbuf_tensor(k.tag + name, shape, dt))

        def psums(name, shape, dt=F32):
            return [c.enter_context(nc.psum_tensor(k.tag + f"{name}{i}", shape, dt)) for i in range(2)]

        idx = sb("es_idx", [128, RING, GR], I32)
        taken = [0]

        def carve(width):
            part = k.big2[:, taken[0]:taken[0] + RING * GR * width]
            taken[0] += RING * GR * width
            return part.rearrange("p (r i d) -> p r i d", r=RING, i=GR)

        kv = carve(KVW)
        onehot = sb("es_onehot", [128, 2, GR, 128], BF16)
        onehot_t = sb("es_onehot_t", [128, 2, GR, EP])
        attr_t = carve(EP)
        both = carve(D)
        key_e = sb("es_key", [128, 2, GR, D])
        prod = sb("es_prod", [128, 2, GR, D])
        we = sb("es_we", [128, D])
        ps_oh = psums("es_ps_oh", [128, GR, 256], BF16)
        ps_at = psums("es_ps_at", [128, GR, EP])
        ps_e = psums("es_ps_e", [128, GR, D])
        ps_q = psums("es_ps_q", [128, GR, D])
        if first:
            attr = carve(D)
            rel = sb("es_rel", [128, 2, GR])
            arg = sb("es_arg", [128, 2, GR, MSG])
            turns = sb("es_turns", [128, 2, GR, MSG])
            wt = sb("es_wt", [128, MSG])
            bt = sb("es_bt", [128, MSG])

        loaded = sem("es_loaded")
        idx_put, turns_begun = sem("es_idx_put"), sem("es_turns_begun")
        gathered = [sem(f"es_gathered{i}") for i in range(RING)]
        onehot_made, onehot_turned, onehot_copied = map(sem, ["es_oh_made", "es_oh_turned", "es_oh_copied"])
        rel_made, mul_made, arg_made, turn_raw, turn_rounded, turn_made, red_a, red_b, angle_made, code_made = map(
            sem, ["es_rel", "es_mul", "es_arg", "es_turn_raw", "es_turn_rounded", "es_turn", "es_red_a", "es_red_b", "es_angle", "es_code"])
        attr_turned, attr_copied = map(sem, ["es_at_turned", "es_at_copied"])
        e_done, q_done, key_made, value_made, prod_made, score_made = map(
            sem, ["es_e", "es_q", "es_keyadd", "es_valadd", "es_prod", "es_score"])
        message_in = [sem(f"es_msg{i}") for i in range(RING)]
        attr_in = [sem(f"es_attr_in{i}") for i in range(RING)]
        attr_out = [sem(f"es_attr_out{i}") for i in range(RING)]
        value_out = [sem(f"es_value_out{i}") for i in range(RING)]
        block = c.enter_context(nc.Block())

        def uses(n, u, per):
            return (n // RING + 1) * per if isinstance(n, int) else (n - u + RING) * (per // RING)

        def live(n):
            return not isinstance(n, int) or n < NGR

        @block.gpsimd
        def _(pool):
            def step(n, u):
                pool.wait_ge(idx_put, n + 1)
                if reached(n, RING):
                    pool.wait_ge(value_made, n - RING + 1)
                pool.sem_inc(turns_begun, 1)
                for i in range(GR):
                    pool.indirect_dma_start(kv[:, u, i, :], None, k.d_kv,
                                            bass.IndirectOffsetOnAxis(ap=idx[:, u, i:i + 1], axis=0)).then_inc(gathered[u], 16)

            pipeline(pool, NGR, 0, step)

        @block.sync
        def _(sp):
            sp.dma_start(we[:, :], w.edge).then_inc(loaded, 16)
            if first:
                sp.dma_start(wt[:, :], a.wt.broadcast_to([128, MSG])).then_inc(loaded, 16)
                sp.dma_start(bt[:, :], a.bt.rearrange("(o d) -> o d", o=1).broadcast_to([128, MSG])).then_inc(loaded, 16)

            def step(n, u):
                if live(n):
                    if first:
                        if reached(n, RING):
                            sp.wait_ge(attr_turned, n - RING + 1)
                        _, tiles = nc.values_load_multi_w_load_instructions(
                            k.tile_row[0:1, bass.ds(n * GR, GR)], engines=[mybir.EngineType.SP], min_val=0, max_val=s.T - 1,
                            skip_runtime_bounds_check_because="item_tables holds the tiles in 0 .. T - 1")
                        for i in range(GR):
                            sp.dma_start(attr[:, u, i, MSG:D],
                                         a.message[bass.ds(tiles[i], 1), :, :].rearrange("a p d -> (a p) d")).then_inc(message_in[u], 16)
                    else:
                        if reached(n, RING):
                            sp.wait_ge(e_done, n - RING + 1)
                        sp.dma_start(attr_t[:, u, :, :].rearrange("p a e -> p (a e)"),
                                     k.d_attr[bass.ds(n, 1), :, :].rearrange("a p d -> (a p) d")).then_inc(attr_in[u], 16)
                if reached(n, 3):
                    m, v = n - 3, (u - 3) % RING
                    if first:
                        sp.wait_ge(attr_copied, m + 1)
                        sp.dma_start(k.d_attr[bass.ds(m, 1), :, :].rearrange("a p d -> (a p) d"),
                                     attr_t[:, v, :, :].rearrange("p a e -> p (a e)")).then_inc(attr_out[v], 16)
                    sp.wait_ge(value_made, m + 1)
                    sp.dma_start(k.d_value[bass.ds(m, 1), :, :].rearrange("a p d -> (a p) d"),
                                 both[:, v, :, :].rearrange("p a d -> p (a d)")).then_inc(value_out[v], 16)

            pipeline(sp, NGR, 3, step)
            for u in range(RING):
                if first:
                    sp.wait_ge(attr_out[u], 16 * (NGR // RING))
                sp.wait_ge(value_out[u], 16 * (NGR // RING))

        @block.vector
        def _(dve):
            dve.wait_ge(loaded, 48 if first else 16)

            def step(n, u):
                h = u % 2
                if live(n):
                    if reached(n, 2):
                        dve.wait_ge(onehot_turned, n - 1)
                    for i in range(GR):
                        last = dve.tensor_scalar(onehot[:, h, i, 0:NP], k.node_iota_b[:, :], k.local[:, bass.ds(n * GR + i, 1)],
                                                 None, ALU.is_equal)
                    last.then_inc(onehot_made, 1)
                    if first:
                        dve.wait_ge(gathered[u], uses(n, u, 16 * GR))
                        dve.tensor_tensor(rel[:, h, :], kv[:, u, :, 2 * D], k.weight[:, bass.ds(n * GR, GR)],
                                          ALU.subtract).then_inc(rel_made, 1)
                        dve.wait_ge(rel_made, n + 1)
                        dve.tensor_tensor(turns[:, h, :, :], rel[:, h, :].unsqueeze(2).broadcast_to([128, GR, MSG]),
                                          wt[:, :].unsqueeze(1).broadcast_to([128, GR, MSG]), ALU.mult).then_inc(mul_made, 1)
                        dve.wait_ge(mul_made, n + 1)
                        dve.tensor_tensor(arg[:, h, :, :], turns[:, h, :, :],
                                          bt[:, :].unsqueeze(1).broadcast_to([128, GR, MSG]), ALU.add).then_inc(arg_made, 1)
                if reached(n, 2):
                    m, v, g = n - 2, (u - 2) % RING, h
                    if not first:
                        dve.wait_ge(gathered[v], uses(m, v, 16 * GR))
                    dve.wait_ge(e_done, m + 1)
                    if reached(m, RING):
                        dve.wait_ge(value_out[v], uses(m - RING, v, 16))
                    dve.tensor_tensor(key_e[:, g, :, :], kv[:, v, :, 0:D], ps_e[g][:, :, :], ALU.add).then_inc(key_made, 1)
                    dve.tensor_tensor(both[:, v, :, :], kv[:, v, :, D:2 * D], ps_e[g][:, :, :], ALU.add).then_inc(value_made, 1)
                    dve.wait_ge(q_done, m + 1)
                    dve.wait_ge(key_made, m + 1)
                    dve.tensor_tensor(prod[:, g, :, :], key_e[:, g, :, :], ps_q[g][:, :, :], ALU.mult).then_inc(prod_made, 1)
                    dve.wait_ge(prod_made, m + 1)
                    dve.tensor_reduce(k.score[:, bass.ds(m * (GR * HEADS), GR * HEADS)],
                                      prod[:, g, :, :].rearrange("p i (h c) -> p (i h) c", c=C), AX.X, ALU.add).then_inc(score_made, 1)
                if live(n) and first:
                    dve.wait_ge(turn_made, n + 1)
                    dve.scalar_tensor_tensor(arg[:, h, :, :], turns[:, h, :, :], -TWO_PI_HI, arg[:, h, :, :],
                                             ALU.mult, ALU.add).then_inc(red_a, 1)
                    dve.wait_ge(red_a, n + 1)
                    dve.scalar_tensor_tensor(arg[:, h, :, :], turns[:, h, :, :], -TWO_PI_LO, arg[:, h, :, :],
                                             ALU.mult, ALU.add).then_inc(red_b, 1)
                    dve.wait_ge(red_b, n + 1)
                    dve.tensor_scalar(arg[:, h, :, :], arg[:, h, :, :], 1.570796, -4.712388, ALU.min, ALU.max).then_inc(angle_made, 1)

            pipeline(dve, NGR, 2, step)
            dve.wait_ge(score_made, NGR)

        @block.scalar
        def _(act):
            act.copy(idx[:, :, :], k.src[:, 0:RING * GR].rearrange("p (r i) -> p r i", i=GR)).then_inc(idx_put, RING)

            def step(n, u):
                h = u % 2
                if live(n):
                    if first:
                        act.wait_ge(arg_made, n + 1)
                        act.activation(turns[:, h, :, :], arg[:, h, :, :], ACT.Identity, bias=k.quarter[:, :],
                                       scale=INV_TWO_PI).then_inc(turn_raw, 1)
                        act.wait_ge(turn_raw, n + 1)
                        act.activation(turns[:, h, :, :], turns[:, h, :, :], ACT.Identity, bias=k.plus_round[:, :]).then_inc(turn_rounded, 1)
                        act.wait_ge(turn_rounded, n + 1)
                        act.activation(turns[:, h, :, :], turns[:, h, :, :], ACT.Identity, bias=k.minus_round[:, :]).then_inc(turn_made, 1)
                if first and reached(n, 1):
                    m, v, g = n - 1, (u - 1) % RING, 1 - h
                    act.wait_ge(attr_turned, m + 1)
                    if reached(m, RING):
                        act.wait_ge(attr_out[v], uses(m - RING, v, 16))
                        act.wait_ge(e_done, m - RING + 1)
                    act.copy(attr_t[:, v, :, :], ps_at[g][:, :, :]).then_inc(attr_copied, 1)
                if live(n):
                    act.wait_ge(onehot_turned, n + 1)
                    if reached(n, 2):
                        act.wait_ge(q_done, n - 1)
                    act.copy(onehot_t[0:NP, h, :, :], ps_oh[h][0:NP, :, 0:EP]).then_inc(onehot_copied, 1)
                    if first:
                        act.wait_ge(angle_made, n + 1)
                        if reached(n, RING):
                            act.wait_ge(attr_turned, n - RING + 1)
                        act.activation(attr[:, u, :, 0:MSG], arg[:, h, :, :], ACT.Sin, bias=k.half_pi[:, :]).then_inc(code_made, 1)
                    act.wait_ge(gathered[u], uses(n, u, 16 * GR))
                    act.copy(idx[:, u, :], k.src[:, bass.ds((n + RING) * GR, GR)]).then_inc(idx_put, 1)

            pipeline(act, NGR, 1, step)

        @block.tensor
        def _(pe):
            pe.wait_ge(loaded, 48 if first else 16)

            def step(n, u):
                h = u % 2
                if live(n):
                    pe.wait_ge(onehot_made, n + 1)
                    if reached(n, 2):
                        pe.wait_ge(onehot_copied, n - 1)
                    for i in range(GR):
                        last = pe.transpose(ps_oh[h][0:NP, i, 0:EP], onehot[:, h, i, 0:NP], k.ident_b[:, :])
                    last.then_inc(onehot_turned, 1)
                if reached(n, 1):
                    m, v, g = n - 1, (u - 1) % RING, 1 - h
                    if first:
                        pe.wait_ge(attr_copied, m + 1)
                    else:
                        pe.wait_ge(attr_in[v], uses(m, v, 16))
                    if reached(m, 2):
                        pe.wait_ge(value_made, m - 1)
                        pe.wait_ge(key_made, m - 1)
                    for i in range(GR):
                        last = pe.matmul(ps_e[g][:, i, :], attr_t[:, v, i, :], we[:, :], start=True, stop=True)
                    last.then_inc(e_done, 1)
                    _, blocks = nc.values_load_multi_w_load_instructions(
                        k.block_row[0:1, bass.ds(m * GR, GR)], engines=[mybir.EngineType.PE], min_val=0, max_val=s.NB,
                        skip_runtime_bounds_check_because="item_tables holds the blocks in 0 .. NB")
                    pe.wait_ge(onehot_copied, m + 1)
                    if reached(m, 2):
                        pe.wait_ge(prod_made, m - 1)
                    for i in range(GR):
                        last = pe.matmul(ps_q[g][:, i, :], onehot_t[0:NP, g, i, :],
                                         k.query[0:NP, bass.ds(blocks[i], 1), 0:D].rearrange("p a d -> p (a d)"),
                                         start=True, stop=True)
                    last.then_inc(q_done, 1)
                if live(n) and first:
                    pe.wait_ge(message_in[u], uses(n, u, 16 * GR))
                    pe.wait_ge(code_made, n + 1)
                    if reached(n, 2):
                        pe.wait_ge(attr_copied, n - 1)
                    for i in range(GR):
                        last = pe.transpose(ps_at[h][:, i, :], attr[:, u, i, :], k.ident[:, :])
                    last.then_inc(attr_turned, 1)

            pipeline(pe, NGR, 1, step)


def softmax_weights(nc, k, s):
    NQ, SL = s.NQ, NG * EP
    with phase(nc, k) as (c, sem):
        def sb(name, shape, dt=F32):
            return c.enter_context(nc.sbuf_tensor(k.tag + name, shape, dt))

        alpha = k.big1[:, 0:HEADS * SL].rearrange("p (h s) -> p h s", h=HEADS)
        peak = k.big2[:, 0:HEADS * SL].rearrange("p (h s) -> p h s", h=HEADS)
        cut = k.big1[:, HEADS * SL:HEADS * SL + SL + 1]
        other = k.big2[:, HEADS * SL:HEADS * SL + 2 * SL].rearrange("p (a s) -> p a s", a=2)
        edge = sb("sm_edge", [128, 10])
        diag = sb("sm_diag", [128, 10, 128])
        rows = sb("sm_rows", [128, 10, 128])
        apart = sb("sm_apart", [128, 2, 2, 128])
        cand = sb("sm_cand", [128, 2, 128])
        joined = sb("sm_joined", [128, 2, HEADS])
        ps_f = [c.enter_context(nc.psum_tensor(k.tag + f"sm_ps_f{i}", [128, HEADS, 128], F32)) for i in range(2)]
        ps_r = [c.enter_context(nc.psum_tensor(k.tag + f"sm_ps_r{i}", [128, 4, 128], F32)) for i in range(3)]
        turned, put, own, peaks, ran, seam, seam_rows, diff, expd, back, done = map(
            sem, ["sm_turned", "sm_put", "sm_own", "sm_peaks", "sm_ran", "sm_seam", "sm_seam_rows", "sm_diff", "sm_expd",
                  "sm_back", "sm_done"])
        block = c.enter_context(nc.Block())

        @block.tensor
        def _(pe):
            for g in range(NG):
                at_least(pe, put, g - 1)
                for h in range(HEADS):
                    v = k.score[:, :].rearrange("p (q g h) -> p g h q", g=NG, h=HEADS)[:, g, h, :]
                    last = pe.transpose(ps_f[g % 2][0:NQ, h, :], v, k.ident[:, :])
                last.then_inc(turned, 1)
            pe.wait_ge(seam, 1)
            for i in range(3):
                w = min(4, 10 - 4 * i)
                last = pe.matmul(ps_r[i][0:NQ, 0:w, :], k.ones[0:NQ, 0:NQ], diag[0:NQ, 4 * i:4 * i + w, :], start=True, stop=True)
            last.then_inc(seam_rows, 1)
            pe.wait_ge(expd, HEADS)
            for g in range(NG):
                at_least(pe, back, g - 1)
                for h in range(HEADS):
                    last = pe.transpose(ps_f[g % 2][:, h, 0:NQ], peak[0:NQ, h, EP * g:EP * g + EP], k.ident[0:NQ, 0:NQ])
                last.then_inc(done, 1)

        @block.scalar
        def _(act):
            for g in range(NG):
                act.wait_ge(turned, g + 1)
                act.copy(alpha[0:NQ, :, EP * g:EP * g + EP], ps_f[g % 2][0:NQ, :, :]).then_inc(put, 1)
            for h in range(HEADS):
                act.wait_ge(diff, h + 1)
                act.activation(peak[0:NQ, h, :], peak[0:NQ, h, :], ACT.Exp, scale=float(C) ** -0.5).then_inc(expd, 1)
            for g in range(NG):
                act.wait_ge(done, g + 1)
                act.copy(k.score[:, :].rearrange("p (q g h) -> p g h q", g=NG, h=HEADS)[:, g, :, :],
                         ps_f[g % 2][:, :, 0:NQ]).then_inc(back, 1)
            act.wait_ge(back, NG)

        @block.vector
        def _(dve):
            ch = Chain(dve, own)
            dve.memset(cut[0:NQ, 0:1], -BIG)
            dve.memset(cut[0:NQ, SL:SL + 1], -BIG)
            dve.memset(diag[:, :, :], 0.0)
            ch.link(dve.scalar_tensor_tensor(cut[0:NQ, 1:SL], k.key[0:NQ, 1:SL], 0.0, k.key[0:NQ, 0:SL - 1],
                                             ALU.add, ALU.not_equal))
            ch.link(dve.tensor_scalar(cut[0:NQ, 1:SL], cut[0:NQ, 1:SL], -BIG, None, ALU.mult))
            dve.wait_ge(put, NG)
            for h in range(HEADS):
                dve.tensor_tensor_scan(peak[0:NQ, h, :], cut[0:NQ, 0:SL], alpha[0:NQ, h, :], 0.0, ALU.add, ALU.max).then_inc(peaks, 1)
            for h in range(HEADS):
                dve.wait_ge(peaks, h + 1)
                last = dve.tensor_tensor_scan(other[0:NQ, 0, ::-1], cut[0:NQ, SL:0:-1], peak[0:NQ, h, ::-1], 0.0, ALU.add, ALU.max)
                ch.link(last)
                ch.link(dve.tensor_copy(peak[0:NQ, h, :], other[0:NQ, 0, :]))
            for end, slot in ((0, 0), (1, SL - 1)):
                dve.tensor_copy(edge[0:NQ, end:end + 1], k.key[0:NQ, slot:slot + 1])
                last = dve.tensor_copy(edge[0:NQ, 2 + HEADS * end:2 + HEADS * end + HEADS], peak[0:NQ, :, slot])
            ch.link(last)
            dve.tensor_tensor(diag[0:NQ, :, 0:NQ], edge[0:NQ, :].unsqueeze(2).broadcast_to([NQ, 10, NQ]),
                              k.ident[0:NQ, 0:NQ].unsqueeze(1).broadcast_to([NQ, 10, NQ]), ALU.mult).then_inc(seam, 1)
            for end in range(2):
                slot = (0, SL - 1)[end]
                last = dve.tensor_scalar(other[0:NQ, end, :], k.key[0:NQ, :], k.key[0:NQ, slot:slot + 1], -BIG,
                                         ALU.not_equal, ALU.mult)
            ch.link(last)
            dve.wait_ge(seam_rows, 1)
            for i in range(3):
                w = min(4, 10 - 4 * i)
                last = dve.tensor_copy(rows[0:NQ, 4 * i:4 * i + w, :], ps_r[i][0:NQ, 0:w, :])
            ch.link(last)
            for end in range(2):
                last = dve.tensor_scalar(apart[0:NQ, end, :, 0:NQ], rows[0:NQ, 0:2, 0:NQ], edge[0:NQ, end:end + 1], -BIG,
                                         ALU.not_equal, ALU.mult)
            ch.link(last)
            for end in range(2):
                for h in range(HEADS):
                    ch.link(dve.tensor_tensor(cand[0:NQ, :, 0:NQ], rows[0:NQ, 2 + h:7 + h:HEADS, 0:NQ], apart[0:NQ, end, :, 0:NQ], ALU.add))
                    ch.link(dve.tensor_reduce(joined[0:NQ, end, h:h + 1], cand[0:NQ, :, 0:NQ], AX.XY, ALU.max))
            for h in range(HEADS):
                for end in range(2):
                    ch.link(dve.scalar_tensor_tensor(peak[0:NQ, h, :], other[0:NQ, end, :], joined[0:NQ, end, h:h + 1],
                                                     peak[0:NQ, h, :], ALU.add, ALU.max))
                dve.tensor_tensor(peak[0:NQ, h, :], alpha[0:NQ, h, :], peak[0:NQ, h, :], ALU.subtract).then_inc(diff, 1)


def add_up(nc, k, s, weighted):
    NGR = s.G
    W = ACW if weighted else D + 1
    with phase(nc, k) as (c, sem):
        def sb(name, shape, dt=F32):
            return c.enter_context(nc.sbuf_tensor(k.tag + name, shape, dt))

        rows = sb("au_rows", [128, RING, GR, ACW])
        onehot = sb("au_onehot", [128, 2, GR, 128])
        if weighted:
            value = sb("au_value", [128, RING, GR, D])
        else:
            idx = sb("au_idx", [128, RING, GR], I32)
        ps = [[c.enter_context(nc.psum_tensor(k.tag + f"au_ps{i}{j}", [128, 2, 256], F32)) for j in range(2)] for i in range(2)]
        arrived = [sem(f"au_arrived{i}") for i in range(RING)]
        turns_begun = sem("au_turns_begun")
        ones_put, zeroed, idx_put, onehot_made, scaled, weight_put, summed, added = map(
            sem, ["au_ones_put", "au_zeroed", "au_idx_put", "au_onehot_made", "au_scaled", "au_weight_put", "au_summed", "au_added"])
        block = c.enter_context(nc.Block())

        def uses(n, u, per):
            return (n // RING + 1) * per if isinstance(n, int) else (n - u + RING) * (per // RING)

        def live(n):
            return not isinstance(n, int) or n < NGR

        @block.sync
        def _(sp):
            if weighted:
                def step(n, u):
                    if reached(n, RING):
                        sp.wait_ge(scaled, n - RING + 1)
                    sp.dma_start(value[:, u, :, :].rearrange("p a d -> p (a d)"),
                                 k.d_value[bass.ds(n, 1), :, :].rearrange("a p d -> (a p) d")).then_inc(arrived[u], 16)

                pipeline(sp, NGR, 0, step)

        @block.gpsimd
        def _(pool):
            if not weighted:
                pool.memset(rows[:, :, :, D:ACW], 1.0).then_inc(ones_put, 1)

            def step(n, u):
                if weighted:
                    pool.wait_ge(arrived[u], uses(n, u, 16))
                    if reached(n, RING):
                        pool.wait_ge(summed, n - RING + 1)
                    pool.tensor_tensor(rows[:, u, :, 0:D].rearrange("p i (h c) -> p i h c", c=C),
                                       value[:, u, :, :].rearrange("p i (h c) -> p i h c", c=C),
                                       k.score[:, bass.ds(n * (GR * HEADS), GR * HEADS)].rearrange("p (i h) -> p i h", h=HEADS)
                                       .unsqueeze(3).broadcast_to([128, GR, HEADS, C]), ALU.mult).then_inc(scaled, 1)
                else:
                    pool.wait_ge(idx_put, n + 1)
                    if reached(n, RING):
                        pool.wait_ge(summed, n - RING + 1)
                    pool.sem_inc(turns_begun, 1)
                    for i in range(GR):
                        pool.indirect_dma_start(rows[:, u, i, 0:D], None, k.d_node,
                                                bass.IndirectOffsetOnAxis(ap=idx[:, u, i:i + 1], axis=0)).then_inc(arrived[u], 16)

            pipeline(pool, NGR, 0, step)

        @block.scalar
        def _(act):
            if weighted:
                def step(n, u):
                    if reached(n, RING):
                        act.wait_ge(summed, n - RING + 1)
                    act.copy(rows[:, u, :, D:ACW],
                             k.score[:, bass.ds(n * (GR * HEADS), GR * HEADS)].rearrange("p (i h) -> p i h", h=HEADS)).then_inc(weight_put, 1)

                pipeline(act, NGR, 0, step)
            else:
                act.copy(idx[:, :, :], k.src[:, 0:RING * GR].rearrange("p (r i) -> p r i", i=GR)).then_inc(idx_put, RING)

                def step(n, u):
                    act.wait_ge(arrived[u], uses(n, u, 16 * GR))
                    act.copy(idx[:, u, :], k.src[:, bass.ds((n + RING) * GR, GR)]).then_inc(idx_put, 1)

                pipeline(act, NGR, 0, step)

        @block.vector
        def _(dve):
            dve.memset(k.big_acc(weighted)[:, :], 0.0).then_inc(zeroed, 1)
            acc = k.acc(weighted)
            dve.wait_ge(zeroed, 1)

            def step(n, u):
                if live(n):
                    if reached(n, 2):
                        dve.wait_ge(summed, n - 1)
                    for i in range(GR):
                        last = dve.tensor_scalar(onehot[:, u % 2, i, 0:NP], k.node_iota[:, :],
                                                 k.local[:, bass.ds(n * GR + i, 1)], None, ALU.is_equal)
                    last.then_inc(onehot_made, 1)
                if reached(n, 1):
                    m, g = n - 1, (u - 1) % 2
                    _, blocks = nc.values_load_multi_w_load_instructions(
                        k.block_row[0:1, bass.ds(m * GR, GR)], engines=[mybir.EngineType.DVE], min_val=0, max_val=s.NB,
                        skip_runtime_bounds_check_because="item_tables holds the blocks in 0 .. NB")
                    dve.wait_ge(summed, m + 1)
                    for i in range(GR):
                        row = acc[0:NP, bass.ds(blocks[i], 1), 0:W].rearrange("p a d -> p (a d)")
                        at_least(dve, added, m * GR + i)
                        dve.tensor_tensor(row, row, ps[g][i // 2][0:NP, i % 2, 0:W], ALU.add).then_inc(added, 1)

            pipeline(dve, NGR, 1, step)
            dve.wait_ge(added, NGR * GR)

        @block.tensor
        def _(pe):
            if not weighted:
                pe.wait_ge(ones_put, 1)

            def step(n, u):
                pe.wait_ge(onehot_made, n + 1)
                if weighted:
                    pe.wait_ge(scaled, n + 1)
                    pe.wait_ge(weight_put, n + 1)
                else:
                    pe.wait_ge(arrived[u], uses(n, u, 16 * GR))
                if reached(n, 2):
                    pe.wait_ge(added, (n - 1) * GR)
                for i in range(GR):
                    last = pe.matmul(ps[u % 2][i // 2][0:NP, i % 2, 0:W], onehot[:, u % 2, i, 0:NP], rows[:, u, i, 0:W],
                                     start=True, stop=True)
                last.then_inc(summed, 1)

            pipeline(pe, NGR, 0, step)


def finish_conv(nc, k, s, a, residual):
    NB = s.NB
    with phase(nc, k) as (c, sem):
        def sb(name, shape, dt=F32):
            return c.enter_context(nc.sbuf_tensor(k.tag + name, shape, dt))

        share = sb("fc_share", [128, NB, HEADS])
        skip = sb("fc_skip", [128, 4, D])
        x = sb("fc_x", [128, 4, D])
        norm = sb("fc_norm", [128, 2, D])
        own, normed, out_made, x_made, final = map(sem, ["fc_own", "fc_normed", "fc_out", "fc_xm", "fc_final"])
        skip_in = [sem(f"fc_skip_in{i}") for i in range(4)]
        x_in = [sem(f"fc_x_in{i}") for i in range(4)]
        stored = sem("fc_stored")
        block = c.enter_context(nc.Block())

        def steps(engine, step):
            for b in range(4):
                step(b, b)
            if NB > 4:
                with engine.Fori(1, NB // 4) as it:
                    for u in range(4):
                        step(it * 4 + u, u)

        def uses(b, u):
            return (b // 4 + 1) * 16 if isinstance(b, int) else (b - u + 4) * 4

        @block.sync
        def _(sp):
            def step(b, u):
                if reached(b, 4):
                    sp.wait_ge(final, b - 3)
                sp.dma_start(skip[0:NP, u, :], k.d_skip[bass.ds(b * NP, NP), :]).then_inc(skip_in[u], 16)
                if residual:
                    sp.dma_start(x[0:NP, u, :], a.x[bass.ds(b * NP, NP), :]).then_inc(x_in[u], 16)

            steps(sp, step)
            if residual:
                sp.wait_ge(final, NB)
                sp.dma_start(k.d_x1.rearrange("(b p) d -> p b d", p=NP), k.nodes[0:NP, 0:NB, 0:D]).then_inc(stored, 16)
                sp.wait_ge(stored, 16)

        @block.vector
        def _(dve):
            ch = Chain(dve, own)
            ch.link(dve.tensor_scalar(share[0:NP, :, :], k.nodes[0:NP, 0:NB, D:ACW], 1e-16, None, ALU.add))
            ch.link(dve.reciprocal(share[0:NP, :, :], share[0:NP, :, :]))

            def step(b, u):
                row = k.nodes[0:NP, bass.ds(b, 1), 0:D].rearrange("p a d -> p (a d)")
                dve.tensor_tensor(norm[0:NP, u % 2, :].rearrange("p (h c) -> p h c", c=C),
                                  row.rearrange("p (h c) -> p h c", c=C),
                                  share[0:NP, bass.ds(b, 1), :].rearrange("p a h -> p (a h)").unsqueeze(2).broadcast_to([NP, HEADS, C]),
                                  ALU.mult).then_inc(normed, 1)
                if residual:
                    dve.wait_ge(x_in[u], uses(b, u))
                    dve.wait_ge(skip_in[u], uses(b, u))
                    dve.tensor_tensor(skip[0:NP, u, :], skip[0:NP, u, :], x[0:NP, u, :], ALU.add).then_inc(x_made, 1)
                    dve.wait_ge(x_made, b + 1)
                dve.wait_ge(skip_in[u], uses(b, u))
                dve.wait_ge(normed, b + 1)
                dve.tensor_tensor(row, norm[0:NP, u % 2, :], skip[0:NP, u, :], ALU.add).then_inc(final, 1)

            steps(dve, step)
            dve.wait_ge(final, NB)


def store_node_table(nc, k, s):
    with phase(nc, k) as (c, sem):
        stored = sem("st_stored")
        block = c.enter_context(nc.Block())


        @block.sync
        def _(sp):
            sp.dma_start(k.d_node.rearrange("(b p) d -> p b d", p=NP), k.nodes[0:NP, 0:s.NB, 0:D]).then_inc(stored, 16)
            sp.wait_ge(stored, 16)


def finish_mean_layer(nc, k, s, a, layer, layers, out):
    NB = s.NB
    last_layer = layer == layers - 1
    with phase(nc, k) as (c, sem):
        def sb(name, shape, dt=F32):
            return c.enter_context(nc.sbuf_tensor(k.tag + name, shape, dt))

        wl = sb("fm_wl", [128, D])
        wr = sb("fm_wr", [128, D])
        bl = sb("fm_bl", [128, D])
        inv = sb("fm_inv", [128, NB])
        mean = sb("fm_mean", [128, 2, D])
        still = sb("fm_still", [128, 2, D])
        turned_sb = sb("fm_turned", [128, 2, 2, NP])
        raw = sb("fm_raw", [128, 2, D])
        x1 = sb("fm_x1", [128, 2, D])
        res = sb("fm_res", [128, 2, D])
        ps_t = [c.enter_context(nc.psum_tensor(k.tag + f"fm_ps_t{i}", [128, 2, 128], F32)) for i in range(2)]
        ps_o = [c.enter_context(nc.psum_tensor(k.tag + f"fm_ps_o{i}", [128, D], F32)) for i in range(2)]
        loaded, own, meaned, stilled, turned, copied, multiplied, biased, made = map(
            sem, ["fm_loaded", "fm_own", "fm_meaned", "fm_stilled", "fm_turned_s", "fm_copied", "fm_multiplied", "fm_biased", "fm_made"])
        x1_in = [sem(f"fm_x1_in{i}") for i in range(2)]
        stored = [sem(f"fm_stored{i}") for i in range(2)]
        block = c.enter_context(nc.Block())
        acc = k.acc(False)

        def steps(engine, lag, step):
            for b in range(2):
                step(b, b)
            with engine.Fori(1, NB // 2) as it:
                for u in range(2):
                    step(it * 2 + u, u)
            for b in range(NB, NB + lag):
                step(b, b % 2)

        def uses(b, u):
            return (b // 2 + 1) * 16 if isinstance(b, int) else (b - u + 2) * 8

        def live(b):
            return not isinstance(b, int) or b < NB

        @block.sync
        def _(sp):
            sp.dma_start(wl[:, :], a.wl[layer]).then_inc(loaded, 16)
            sp.dma_start(wr[:, :], a.wr[layer]).then_inc(loaded, 16)
            sp.dma_start(bl[:, :], a.bl[layer:layer + 1, :].broadcast_to([128, D])).then_inc(loaded, 16)

            def step(b, u):
                if live(b) and last_layer:
                    if reached(b, 2):
                        sp.wait_ge(made, b - 1)
                    sp.dma_start(x1[0:NP, u, :], k.d_x1[bass.ds(b * NP, NP), :]).then_inc(x1_in[u], 16)
                if reached(b, 1):
                    m, v = b - 1, 1 - u
                    sp.wait_ge(made, m + 1)
                    target = out if last_layer else k.d_node
                    source = res[0:NP, v, :] if last_layer else k.nodes[0:NP, bass.ds(m, 1), 0:D].rearrange("p a d -> p (a d)")
                    sp.dma_start(target[bass.ds(m * NP, NP), :], source).then_inc(stored[v], 16)

            steps(sp, 1, step)
            for u in range(2):
                sp.wait_ge(stored[u], 16 * (NB // 2))

        @block.vector
        def _(dve):
            ch = Chain(dve, own)
            ch.link(dve.tensor_scalar(inv[0:NP, :], acc[0:NP, 0:NB, D], 1.0, None, ALU.max))
            ch.link(dve.reciprocal(inv[0:NP, :], inv[0:NP, :]))
            dve.wait_ge(loaded, 48)

            def step(b, u):
                if live(b):
                    if reached(b, 2):
                        dve.wait_ge(turned, b - 1)
                    dve.tensor_scalar(mean[0:NP, u, :], acc[0:NP, bass.ds(b, 1), 0:D].rearrange("p a d -> p (a d)"),
                                      inv[0:NP, bass.ds(b, 1)], None, ALU.mult).then_inc(meaned, 1)
                if reached(b, 1):
                    m, v = b - 1, 1 - u
                    dve.wait_ge(multiplied, m + 1)
                    if reached(m, 2):
                        dve.wait_ge(made, m - 1)
                    dve.tensor_tensor(raw[0:NP, v, :], ps_o[v][0:NP, :], bl[0:NP, :], ALU.add).then_inc(biased, 1)
                    if last_layer:
                        dve.wait_ge(x1_in[v], uses(m, v))
                        dve.wait_ge(biased, m + 1)
                        if reached(m, 2):
                            dve.wait_ge(stored[v], uses(m - 2, v))
                        dve.tensor_tensor(res[0:NP, v, :], raw[0:NP, v, :], x1[0:NP, v, :], ALU.add).then_inc(made, 1)

            steps(dve, 1, step)

        @block.tensor
        def _(pe):
            pe.wait_ge(loaded, 48)

            def step(b, u):
                pe.wait_ge(meaned, b + 1)
                pe.wait_ge(stilled, b + 1)
                if reached(b, 2):
                    pe.wait_ge(copied, b - 1)
                pe.transpose(ps_t[u][:, 0, 0:NP], mean[0:NP, u, :], k.ident[0:NP, 0:NP])
                pe.transpose(ps_t[u][:, 1, 0:NP], still[0:NP, u, :],
                             k.ident[0:NP, 0:NP]).then_inc(turned, 1)
                pe.wait_ge(copied, b + 1)
                if reached(b, 2):
                    pe.wait_ge(biased, b - 1)
                pe.matmul(ps_o[u][0:NP, :], turned_sb[:, u, 0, :], wl[:, :], start=True, stop=False)
                pe.matmul(ps_o[u][0:NP, :], turned_sb[:, u, 1, :], wr[:, :], start=False, stop=True).then_inc(multiplied, 1)

            steps(pe, 0, step)

        @block.gpsimd
        def _(pool):
            def step(b, u):
                if reached(b, 2):
                    pool.wait_ge(turned, b - 1)
                pool.tensor_copy(still[0:NP, u, :], k.nodes[0:NP, bass.ds(b, 1), 0:D].rearrange("p a d -> p (a d)")).then_inc(stilled, 1)

            steps(pool, 0, step)

        @block.scalar
        def _(act):
            def step(b, u):
                if live(b):
                    act.wait_ge(turned, b + 1)
                    if reached(b, 2):
                        act.wait_ge(multiplied, b - 1)
                    act.copy(turned_sb[:, u, :, :], ps_t[u][:, :, 0:NP]).then_inc(copied, 1)
                if reached(b, 1) and not last_layer:
                    m, v = b - 1, 1 - u
                    act.wait_ge(biased, m + 1)
                    act.activation(k.nodes[0:NP, bass.ds(m, 1), 0:D].rearrange("p a d -> p (a d)"), raw[0:NP, v, :],
                                   ACT.Relu).then_inc(made, 1)

            steps(act, 1, step)


def graph_kernel(nc, a, out):
    s = Shapes(a.x, a.src)
    k = Store()
    k.tag = "prepare_"

    def dram(name, shape, dt=F32):
        return nc.dram_tensor(name, shape, dt, kind="Internal").ap()

    k.d_tile_of = dram("d_tile_of", [s.I], I32)
    k.d_block_of = dram("d_block_of", [s.I], I32)
    k.d_kv = dram("d_kv", [s.N, KVW])
    k.d_skip = dram("d_skip", [s.N, D])
    k.d_attr = dram("d_attr", [s.G, 128, GR * EP])
    k.d_value = dram("d_value", [s.G, EP, GR * D])
    k.d_x1 = dram("d_x1", [s.N, D])
    k.d_node = dram("d_node", [s.N, D])
    with ExitStack() as c:
        def sb(name, shape, dt=F32):
            return c.enter_context(nc.sbuf_tensor(name, shape, dt))

        k.ident = sb("ident", [128, 128])
        k.ident_b = sb("ident_b", [128, 128], BF16)
        k.node_iota_i = sb("node_iota_i", [128, NP], I32)
        k.node_iota = sb("node_iota", [128, NP])
        k.node_iota_b = sb("node_iota_b", [128, NP], BF16)
        k.ones = sb("ones", [128, 128])
        k.half_pi = sb("half_pi", [128, 1])
        k.quarter = sb("quarter", [128, 1])
        k.plus_round = sb("plus_round", [128, 1])
        k.minus_round = sb("minus_round", [128, 1])
        k.zero = sb("zero", [128, 1])
        k.eps = sb("eps", [128, 1])
        k.tile_row = sb("tile_row", [1, s.I], I32)
        k.block_row = sb("block_row", [1, s.I], I32)
        k.local = sb("local_t", [128, s.I])
        k.src = sb("src_t", [128, s.I + RING * GR], I32)
        k.weight = sb("weight_t", [128, s.I])
        k.key = sb("key", [128, NG * EP])
        k.vec = sb("vec", [128, s.NB])
        constants(nc, k)
        item_tables(nc, k, s, a)

        k.score = sb("score", [128, s.I * HEADS])
        big = max((s.NB + 1) * ACW, (HEADS + 2) * NG * EP)
        k.big1 = sb("big1", [128, big])
        k.big2 = sb("big2", [128, big])
        k.query = k.big1[:, 0:(s.NB + 1) * ACW].rearrange("p (b d) -> p b d", d=ACW)
        k.nodes = k.big2[:, 0:(s.NB + 1) * ACW].rearrange("p (b d) -> p b d", d=ACW)
        k.acc = lambda weighted: k.nodes if weighted else k.query
        k.big_acc = lambda weighted: k.big2 if weighted else k.big1

        load_nodes(nc, k, s, a)
        layer_norm(nc, k, s)
        for n in range(2):
            k.tag = f"conv{n}_"
            project_nodes(nc, k, s, a.convs[n])
            edge_scores(nc, k, s, a, a.convs[n], first=n == 0)
            softmax_weights(nc, k, s)
            add_up(nc, k, s, weighted=True)
            finish_conv(nc, k, s, a, residual=n == 1)
        k.tag = "between_"
        layer_norm(nc, k, s)
        store_node_table(nc, k, s)
        layers = a.wl.shape[0]
        for n in range(layers):
            k.tag = f"mean{n}_"
            add_up(nc, k, s, weighted=False)
            finish_mean_layer(nc, k, s, a, n, layers, out)


def layout(inputs):
    import numpy as np

    N = inputs["x"].shape[0]
    pad = -inputs["src"].shape[0] % EP
    edge = lambda v, fill: np.concatenate([np.asarray(v), np.full((pad,) + v.shape[1:], fill, v.dtype)])
    arrays = {
        "x": inputs["x"], "vec": inputs["node_vec"],
        "src": edge(inputs["src"], 0).reshape(-1, EP),
        "dst": edge(inputs["dst"], N).reshape(-1, EP),
        "weight": edge(inputs["edge_weight"], 0).reshape(-1, EP),
        "message": edge(inputs["edge_attr_64"], 0).reshape(-1, EP, MSG),
        "wt": inputs["L0_gnn_Wt"], "bt": inputs["L0_gnn_bt"], "bl": inputs["L1_gnn_bl"],
        "wl": np.swapaxes(np.asarray(inputs["L1_gnn_Wl"]), 1, 2),
        "wr": np.swapaxes(np.asarray(inputs["L1_gnn_Wr"]), 1, 2),
    }
    for n in "12":
        arrays["we" + n] = inputs["L0_gnn_We" + n]
        for name in ("q", "k", "v", "skip"):
            arrays[f"w{name}{n}"] = inputs[f"L0_gnn_W{name}{n}"]
            arrays[f"b{name}{n}"] = inputs[f"L0_gnn_b{name}{n}"]
    return {name: np.ascontiguousarray(v) for name, v in arrays.items()}


def build(nc, arrays):
    def tensor(name):
        v = arrays[name]
        return nc.dram_tensor(f"in_{name}", v.shape, mybir.dt.from_np(v.dtype), kind="ExternalInput").ap()

    a = Store()
    a.x, a.vec = tensor("x"), tensor("vec")
    a.src, a.dst, a.weight, a.message = tensor("src"), tensor("dst"), tensor("weight"), tensor("message")
    a.wt, a.bt = tensor("wt"), tensor("bt")
    a.wl, a.wr, a.bl = tensor("wl"), tensor("wr"), tensor("bl")
    a.convs = []
    for n in "12":
        conv = Store()
        conv.edge = tensor("we" + n)
        conv.weights = [tensor(f"w{p}{n}") for p in ("q", "k", "v", "skip")]
        conv.biases = [tensor(f"b{p}{n}") for p in ("q", "k", "v", "skip")]
        a.convs.append(conv)
    out = nc.dram_tensor("out_0_dram", arrays["x"].shape, F32, kind="ExternalOutput").ap()
    graph_kernel(nc, a, out)


def kernel(**inputs):
    import concourse.bacc as _bacc
    from concourse.bass_utils import run_bass_kernel_spmd as _run

    nc = _bacc.Bacc("TRN2", target_bir_lowering=False, num_devices=1)
    arrays = layout(inputs)
    build(nc, arrays)
    r = _run(nc, [{f"in_{name}": v for name, v in arrays.items()}], core_ids=[0])
    return r.results[0]["out_0_dram"]
```

```python
from contextlib import ExitStack, contextmanager

import concourse.bass as bass
from concourse import mybir

F32 = mybir.dt.float32
BF16 = mybir.dt.bfloat16
I32 = mybir.dt.int32
ALU = mybir.AluOpType
ACT = mybir.ActivationFunctionType
AX = mybir.AxisListType

D = 128
HEADS = 4
C = D // HEADS
MSG = 64
EP = 128
NP = 125
GR = 4
NG = 16
UNROLL = 8
RING = 4
PR = 4
KVW = 2 * D + 4
ACW = D + HEADS
BIG = 1.0e30
ROUND = 12582912.0
TWO_PI = 6.283185
INV_TWO_PI = 0.15915494309189535


class Shapes:

    def __init__(self, x, src):
        self.N = x.shape[0]
        self.NB = self.N // NP
        self.T = src.shape[0]
        self.NQ = -(-(self.T + self.NB) // NG)
        self.NQ += self.NQ % 2
        self.I = NG * self.NQ
        self.G = self.I // GR
        assert self.N % NP == 0 and self.NB % 4 == 0 and self.NQ <= 128


class Store:
    pass


class Chain:

    def __init__(self, engine, sem):
        self.engine, self.sem, self.n = engine, sem, 0

    def link(self, instruction):
        self.n += 1
        instruction.then_inc(self.sem, 1)
        self.engine.wait_ge(self.sem, self.n)


def at_least(engine, sem, value):
    if not isinstance(value, int) or value > 0:
        engine.wait_ge(sem, value)


def reached(n, back=0):
    return not isinstance(n, int) or n - back >= 0


def pipeline(engine, count, lag, step):
    for n in range(UNROLL):
        step(n, n)
    with engine.Fori(1, count // UNROLL) as it:
        for u in range(UNROLL):
            step(it * UNROLL + u, u)
    for n in range(count, count + lag):
        step(n, n % UNROLL)


def uses(n, u, ring, per):
    return (n // ring + 1) * per if isinstance(n, int) else (n - u % ring + ring) * (per // ring)


@contextmanager
def phase(nc, k):
    made = []

    def sem(name):
        made.append(nc.alloc_semaphore(name=k.tag + name))
        return made[-1]

    with ExitStack() as c:
        yield c, sem
    nc.clear_and_free_semaphores(made)
    nc.all_engine_barrier()


def constants(nc, k):
    with phase(nc, k) as (c, sem):
        made, cast = sem("const_made"), sem("const_cast")
        block = c.enter_context(nc.Block())


        @block.gpsimd
        def _(pool):
            pool.memset(k.ident[:, :], 0.0).then_inc(made, 1)
            pool.wait_ge(made, 1)
            pool.affine_select(out=k.ident[:, :], in_=k.ident[:, :], compare_op=ALU.not_equal, fill=1.0,
                               base=0, pattern=[[-1, 128]], channel_multiplier=1).then_inc(made, 1)
            pool.iota(k.node_iota_i[:, :], pattern=[[1, NP]], base=0, channel_multiplier=0).then_inc(made, 1)
            pool.memset(k.zero[:, :], 0.0)
            pool.memset(k.ones[:, :], 1.0)
            pool.memset(k.eps[:, :], 1e-5).then_inc(made, 1)

        @block.vector
        def _(dve):
            dve.wait_ge(made, 4)
            dve.tensor_copy(k.ident_b[:, :], k.ident[:, :])
            dve.tensor_copy(k.node_iota[:, :], k.node_iota_i[:, :]).then_inc(cast, 1)
            dve.wait_ge(cast, 1)
            dve.tensor_copy(k.node_iota_b[:, :], k.node_iota[:, :]).then_inc(cast, 1)
            dve.wait_ge(cast, 2)


def item_tables(nc, k, s, a):
    NQ, T, I = s.NQ, s.T, s.I
    SL = NG * EP
    with phase(nc, k) as (c, sem):
        def sb(name, shape, dt=F32):
            return c.enter_context(nc.sbuf_tensor(k.tag + name, shape, dt))

        last_i = sb("last_i", [1, T], I32)
        tile_i = sb("tile_i", [1, T], I32)
        last_f = sb("last_f", [1, T])
        tile_f = sb("tile_f", [1, T])
        leave = sb("leave", [1, T])
        leave_all = sb("leave_all", [128, T])
        junk = sb("junk", [128, T])
        item_i = sb("item_i", [128, NG], I32)
        item_f = sb("item_f", [128, NG])
        tile_of = sb("tile_of", [128, NG])
        block_of = sb("block_of", [128, NG])
        tile_of_i = sb("tile_of_i", [128, NG], I32)
        block_of_i = sb("block_of_i", [128, NG], I32)
        base = sb("base", [128, NG])
        src_q = sb("src_q", [128, NG, EP], I32)
        dst_q = sb("dst_q", [128, NG, EP], I32)
        weight_q = sb("weight_q", [128, NG, EP])
        src_f = sb("src_f", [128, NG, EP])
        dst_f = sb("dst_f", [128, NG, EP])
        local = sb("local", [128, NG, EP])
        valid = sb("valid", [128, NG, EP])
        ps_row = c.enter_context(nc.psum_tensor("ps_row", [128, 4, 512], F32))
        ps_t = [c.enter_context(nc.psum_tensor(k.tag + f"ps_t{i}", [128, 4, 128], F32)) for i in range(2)]

        loaded, iotas, leave_done, row_ready, row_copied = map(sem, ["loaded", "iotas", "leave_done", "row_ready", "row_copied"])
        tiles_known, tiles_stored, tiles_back = map(sem, ["tiles_known", "tiles_stored", "tiles_back"])
        src_in, dst_in, weight_in = map(sem, ["src_in", "dst_in", "weight_in"])
        cast_done, local_done, own, turned, placed = map(sem, ["cast_done", "local_done", "own", "turned", "placed"])
        block = c.enter_context(nc.Block())

        @block.sync
        def _(sp):
            sp.dma_start(last_i[:, :], a.dst[:, EP - 1:EP].rearrange("t o -> o t"),
                         allow_slow_non_contiguous=True).then_inc(loaded, 16)
            sp.wait_ge(tiles_known, 1)
            sp.dma_start(k.d_tile_of.rearrange("(q g) -> q g", g=NG), tile_of_i[0:NQ, :]).then_inc(tiles_stored, 16)
            sp.dma_start(k.d_block_of.rearrange("(q g) -> q g", g=NG), block_of_i[0:NQ, :]).then_inc(tiles_stored, 16)
            sp.wait_ge(tiles_stored, 32)
            sp.dma_start(k.tile_row[:, :], k.d_tile_of.rearrange("(o i) -> o i", o=1)).then_inc(tiles_back, 16)
            sp.dma_start(k.block_row[:, :], k.d_block_of.rearrange("(o i) -> o i", o=1)).then_inc(tiles_back, 16)
            sp.wait_ge(tiles_back, 32)

        @block.gpsimd
        def _(pool):
            pool.memset(k.src[:, I:I + UNROLL * GR], 0)
            pool.iota(tile_i[:, :], pattern=[[1, T]], base=0, channel_multiplier=0)
            pool.iota(item_i[:, :], pattern=[[1, NG]], base=0, channel_multiplier=NG).then_inc(iotas, 1)
            pool.wait_ge(tiles_known, 1)
            for g in range(NG):
                for table, out, done in ((a.dst, dst_q, dst_in), (a.src, src_q, src_in), (a.weight, weight_q, weight_in)):
                    pool.indirect_dma_start(out[0:NQ, g, :], None, table,
                                            bass.IndirectOffsetOnAxis(ap=tile_of_i[0:NQ, g:g + 1], axis=0)).then_inc(done, 16)

        @block.vector
        def _(dve):
            ch = Chain(dve, own)
            dve.wait_ge(iotas, 1)
            dve.tensor_copy(tile_f[:, :], tile_i[:, :])
            dve.tensor_copy(item_f[:, :], item_i[:, :])
            dve.wait_ge(loaded, 16)
            ch.link(dve.tensor_copy(last_f[:, :], last_i[:, :]))
            ch.link(dve.tensor_scalar(last_f[:, :], last_f[:, :], 1.0 / NP, 0.5 / NP - 0.5, ALU.mult, ALU.add))
            ch.link(dve.tensor_scalar(last_f[:, :], last_f[:, :], ROUND, ROUND, ALU.add, ALU.subtract))
            dve.tensor_tensor(leave[:, :], last_f[:, :], tile_f[:, :], ALU.add).then_inc(leave_done, 1)
            dve.wait_ge(row_copied, 1)
            for g in range(NG):
                last = dve.tensor_scalar(junk[0:NQ, :], leave_all[0:NQ, :], item_f[0:NQ, g:g + 1], 0.0,
                                         ALU.is_lt, ALU.add, accum_out=tile_of[0:NQ, g:g + 1])
                ch.link(last)
            ch.link(dve.tensor_scalar(tile_of[0:NQ, :], tile_of[0:NQ, :], float(T - 1), None, ALU.min))
            ch.link(dve.tensor_tensor(block_of[0:NQ, :], item_f[0:NQ, :], tile_of[0:NQ, :], ALU.subtract))
            ch.link(dve.tensor_scalar(block_of[0:NQ, :], block_of[0:NQ, :], float(s.NB), None, ALU.min))
            dve.tensor_copy(tile_of_i[0:NQ, :], tile_of[0:NQ, :])
            dve.tensor_copy(block_of_i[0:NQ, :], block_of[0:NQ, :]).then_inc(tiles_known, 1)
            ch.link(dve.tensor_scalar(base[0:NQ, :], block_of[0:NQ, :], float(NP), None, ALU.mult))
            dve.wait_ge(dst_in, 16 * NG)
            ch.link(dve.tensor_copy(dst_f[0:NQ, :, :], dst_q[0:NQ, :, :]))
            ch.link(dve.tensor_tensor(local[0:NQ, :, :], dst_f[0:NQ, :, :],
                                      base[0:NQ, :].unsqueeze(2).broadcast_to([NQ, NG, EP]), ALU.subtract))
            dve.wait_ge(src_in, 16 * NG)
            dve.tensor_copy(src_f[0:NQ, :, :], src_q[0:NQ, :, :])
            ch.link(dve.tensor_scalar(valid[0:NQ, :, :], local[0:NQ, :, :], 0.0, None, ALU.is_ge))
            ch.link(dve.scalar_tensor_tensor(valid[0:NQ, :, :], local[0:NQ, :, :], float(NP), valid[0:NQ, :, :],
                                             ALU.is_lt, ALU.mult))
            ch.link(dve.scalar_tensor_tensor(local[0:NQ, :, :], local[0:NQ, :, :], 1.0, valid[0:NQ, :, :],
                                             ALU.add, ALU.mult))
            dve.tensor_scalar(local[0:NQ, :, :], local[0:NQ, :, :], -1.0, None, ALU.add).then_inc(local_done, 1)
            ch.link(dve.scalar_tensor_tensor(dst_f[0:NQ, :, :], dst_f[0:NQ, :, :], 1.0, valid[0:NQ, :, :],
                                             ALU.add, ALU.mult))
            ch.link(dve.tensor_scalar(k.key[0:NQ, :], dst_f[0:NQ, :, :].rearrange("q g e -> q (g e)"), -1.0, None, ALU.add))
            dve.wait_ge(placed, NG // 4)
            ch.link(dve.tensor_copy(k.local_b[:, :], k.local[:, :]))

        order = [(t, g4) for t in range(3) for g4 in range(NG // 4)]

        @block.tensor
        def _(pe):
            pe.wait_ge(leave_done, 1)
            for i in range(-(-T // 512)):
                w = min(512, T - 512 * i)
                last = pe.matmul(ps_row[0:NQ, i, 0:w], k.ones[0:1, 0:NQ], leave[:, 512 * i:512 * i + w], start=True, stop=True)
            last.then_inc(row_ready, 1)
            pe.wait_ge(local_done, 1)
            pe.wait_ge(weight_in, 16 * NG)
            for j, (t, g4) in enumerate(order):
                table = (local, src_f, weight_q)[t]
                at_least(pe, placed, j - 1)
                for g in range(4):
                    last = pe.transpose(ps_t[j % 2][:, g, 0:NQ], table[0:NQ, 4 * g4 + g, :], k.ident[0:NQ, 0:NQ])
                last.then_inc(turned, 1)

        @block.scalar
        def _(act):
            act.wait_ge(row_ready, 1)
            for i in range(-(-T // 512)):
                w = min(512, T - 512 * i)
                last = act.copy(leave_all[0:NQ, 512 * i:512 * i + w], ps_row[0:NQ, i, 0:w])
            last.then_inc(row_copied, 1)
            for j, (t, g4) in enumerate(order):
                table = (k.local, k.src, k.weight)[t]
                act.wait_ge(turned, j + 1)
                act.copy(table[:, 0:I].rearrange("p (q g) -> p g q", g=NG)[:, 4 * g4:4 * g4 + 4, :],
                         ps_t[j % 2][:, :, 0:NQ]).then_inc(placed, 1)
            act.wait_ge(placed, len(order))


def layer_norm(nc, k, s):
    NB = s.NB
    with phase(nc, k) as (c, sem):
        def sb(name, shape, dt=F32):
            return c.enter_context(nc.sbuf_tensor(k.tag + name, shape, dt))

        stats = sb("ln_stats", [128, NB, 6])
        moments = sb("ln_moments", [128, NB, 2])
        std = sb("ln_std", [128, NB])
        rstd = sb("ln_rstd", [128, NB])
        shift = sb("ln_shift", [128, NB])
        own = sem("ln_own")
        var_done = sem("ln_var_done")
        std_done = sem("ln_std_done")
        scale_done = sem("ln_scale_done")
        applied = sem("ln_applied")
        block = c.enter_context(nc.Block())

        @block.vector
        def _(dve):
            with dve.Fori(0, NB // 2) as it:
                for u in range(2):
                    b = it * 2 + u
                    dve.bn_stats(stats[0:NP, bass.ds(b, 1), :].rearrange("p a d -> p (a d)"),
                                 k.nodes[0:NP, bass.ds(b, 1), 0:D].rearrange("p a d -> p (a d)")).then_inc(own, 1)
            dve.wait_ge(own, NB)
            for b in range(NB):
                last = dve.bn_aggr(moments[0:NP, b, :], stats[0:NP, b, :])
            last.then_inc(var_done, 1)
            dve.wait_ge(std_done, 1)
            dve.reciprocal(rstd[0:NP, :], std[0:NP, :]).then_inc(own, 1)
            dve.wait_ge(own, NB + 1)
            dve.scalar_tensor_tensor(shift[0:NP, :], moments[0:NP, :, 0], -1.0, rstd[0:NP, :],
                                     ALU.mult, ALU.mult).then_inc(scale_done, 1)

        @block.scalar
        def _(act):
            act.wait_ge(var_done, 1)
            act.activation(std[0:NP, :], moments[0:NP, :, 1], ACT.Sqrt, bias=k.eps[0:NP, :]).then_inc(std_done, 1)
            act.wait_ge(scale_done, 1)
            with act.Fori(0, NB // 2) as it:
                for u in range(2):
                    b = it * 2 + u
                    row = k.nodes[0:NP, bass.ds(b, 1), 0:D].rearrange("p a d -> p (a d)")
                    act.activation(row, row, ACT.Relu, bias=shift[0:NP, bass.ds(b, 1)],
                                   scale=rstd[0:NP, bass.ds(b, 1)]).then_inc(applied, 1)
            act.wait_ge(applied, NB)


def load_nodes(nc, k, s, a):
    with phase(nc, k) as (c, sem):
        vec_rows = c.enter_context(nc.sbuf_tensor("vec_rows", [128, NP], F32))
        ps = c.enter_context(nc.psum_tensor("ps_vec", [128, 128], F32))
        x_in, vec_in, turned, copied = [sem(n) for n in ("x_in", "vec_in", "vec_turned", "vec_copied")]
        block = c.enter_context(nc.Block())

        @block.sync
        def _(sp):
            sp.dma_start(vec_rows[0:s.NB, :], a.vec.rearrange("(b p) -> b p", p=NP)).then_inc(vec_in, 16)
            sp.dma_start(k.nodes[0:NP, 0:s.NB, 0:D], a.x.rearrange("(b p) d -> p b d", p=NP)).then_inc(x_in, 16)
            sp.wait_ge(x_in, 16)

        @block.tensor
        def _(pe):
            pe.wait_ge(vec_in, 16)
            pe.transpose(ps[0:NP, 0:s.NB], vec_rows[0:s.NB, :], k.ident[0:s.NB, 0:s.NB]).then_inc(turned, 1)

        @block.vector
        def _(dve):
            dve.wait_ge(turned, 1)
            dve.tensor_copy(k.vec[0:NP, :], ps[0:NP, 0:s.NB]).then_inc(copied, 1)
            dve.wait_ge(copied, 1)


def project_nodes(nc, k, s, w):
    NB = s.NB
    with phase(nc, k) as (c, sem):
        def sb(name, shape, dt=F32):
            return c.enter_context(nc.sbuf_tensor(k.tag + name, shape, dt))

        weights = sb("pr_weights", [128, 4 * D])
        bias = sb("pr_bias", [128, 4 * D])
        turned_sb = sb("pr_turned", [128, PR, NP])
        still = sb("pr_still", [128, PR, D])
        kv = sb("pr_kv", [128, PR, KVW])
        skip = sb("pr_skip", [128, PR, D])
        ps_t = [c.enter_context(nc.psum_tensor(k.tag + f"pr_ps_t{i}", [128, 512], F32)) for i in range(PR)]
        ps_p = [c.enter_context(nc.psum_tensor(k.tag + f"pr_ps_p{i}", [128, 512], F32)) for i in range(PR)]
        loaded, stilled, turned, copied, projected, added, vec_put, zeroed = map(
            sem, ["pr_loaded", "pr_stilled", "pr_turned_s", "pr_copied", "pr_projected", "pr_added", "pr_vec_put", "pr_zeroed"])
        kv_out = [sem(f"pr_kv_out{i}") for i in range(PR)]
        skip_out = [sem(f"pr_skip_out{i}") for i in range(PR)]
        block = c.enter_context(nc.Block())

        def steps(engine, step):
            for b in range(2 * PR):
                step(b, b % PR)
            with engine.Fori(2, NB // PR) as it:
                for u in range(PR):
                    step(it * PR + u, u)

        def live(b):
            return not isinstance(b, int) or b < NB

        @block.sync
        def _(sp):
            for i in range(4):
                sp.dma_start(weights[:, D * i:D * i + D], w.weights[i]).then_inc(loaded, 16)
                sp.dma_start(bias[:, D * i:D * i + D], w.biases[i].rearrange("(o d) -> o d", o=1).broadcast_to([128, D])).then_inc(loaded, 16)

            def step(b, u):
                sp.wait_ge(added, b + 1)
                sp.wait_ge(vec_put, b + 1)
                sp.dma_start(k.d_kv.rearrange("(b p) d -> p b d", p=NP)[:, bass.ds(b, 1), :].rearrange("p a d -> p (a d)"),
                             kv[0:NP, u, :]).then_inc(kv_out[u], 16)
                sp.dma_start(k.d_skip.rearrange("(b p) d -> p b d", p=NP)[:, bass.ds(b, 1), :].rearrange("p a d -> p (a d)"),
                             skip[0:NP, u, :]).then_inc(skip_out[u], 16)

            steps(sp, step)
            for u in range(PR):
                sp.wait_ge(kv_out[u], 16 * (NB // PR))
                sp.wait_ge(skip_out[u], 16 * (NB // PR))

        @block.tensor
        def _(pe):
            pe.wait_ge(loaded, 128)

            def step(b, u):
                if live(b):
                    pe.wait_ge(stilled, b + 1)
                    if reached(b, PR):
                        pe.wait_ge(copied, b - PR + 1)
                    pe.transpose(ps_t[u][:, 0:NP], still[0:NP, u, :],
                                 k.ident[0:NP, 0:NP]).then_inc(turned, 1)
                if reached(b, 1):
                    m, v = b - 1, (u - 1) % PR
                    pe.wait_ge(copied, m + 1)
                    if reached(m, PR):
                        pe.wait_ge(added, m - PR + 1)
                    pe.matmul(ps_p[v][0:NP, :], turned_sb[:, v, :], weights[:, :], start=True, stop=True).then_inc(projected, 1)

            steps(pe, step)
            step(NB, NB % PR)

        @block.gpsimd
        def _(pool):
            def step(b, u):
                if reached(b, PR):
                    pool.wait_ge(turned, b - PR + 1)
                pool.tensor_copy(still[0:NP, u, :], k.nodes[0:NP, bass.ds(b, 1), 0:D].rearrange("p a d -> p (a d)")).then_inc(stilled, 1)

            steps(pool, step)

        @block.scalar
        def _(act):
            def step(b, u):
                act.wait_ge(turned, b + 1)
                if reached(b, PR):
                    act.wait_ge(projected, b - PR + 1)
                act.copy(turned_sb[:, u, :], ps_t[u][:, 0:NP]).then_inc(copied, 1)
                if reached(b, PR):
                    act.wait_ge(kv_out[u], uses(b - PR, u, PR, 16))
                act.copy(kv[0:NP, u, 2 * D:2 * D + 1], k.vec[0:NP, bass.ds(b, 1)]).then_inc(vec_put, 1)

            act.wait_ge(zeroed, 1)
            steps(act, step)

        @block.vector
        def _(dve):
            dve.memset(kv[:, :, :], 0.0)
            dve.memset(k.query[:, NB, :], 0.0).then_inc(zeroed, 1)
            dve.wait_ge(loaded, 128)
            dve.wait_ge(zeroed, 1)

            def step(b, u):
                dve.wait_ge(projected, b + 1)
                if reached(b, PR):
                    dve.wait_ge(kv_out[u], uses(b - PR, u, PR, 16))
                    dve.wait_ge(skip_out[u], uses(b - PR, u, PR, 16))
                dve.tensor_tensor(k.query[0:NP, bass.ds(b, 1), 0:D].rearrange("p a d -> p (a d)"), ps_p[u][0:NP, 0:D], bias[0:NP, 0:D], ALU.add)
                dve.tensor_tensor(kv[0:NP, u, 0:2 * D], ps_p[u][0:NP, D:3 * D], bias[0:NP, D:3 * D], ALU.add)
                dve.tensor_tensor(skip[0:NP, u, :], ps_p[u][0:NP, 3 * D:4 * D], bias[0:NP, 3 * D:4 * D],
                                  ALU.add).then_inc(added, 1)

            steps(dve, step)


def edge_scores(nc, k, s, a, w, first):
    NGR = s.G
    lag = 3 if first else 2
    with phase(nc, k) as (c, sem):
        def sb(name, shape, dt=F32):
            return c.enter_context(nc.sbuf_tensor(k.tag + name, shape, dt))

        def psums(name, shape, dt=F32):
            return [c.enter_context(nc.psum_tensor(k.tag + f"{name}{i}", shape, dt)) for i in range(2)]

        taken = [0]

        def carve(ring, width):
            part = k.big2[:, taken[0]:taken[0] + ring * GR * width]
            taken[0] += ring * GR * width
            return part.rearrange("p (r i d) -> p r i d", r=ring, i=GR)

        kv = carve(UNROLL, KVW)
        attr_t = carve(RING, EP)
        both = carve(RING, D)
        idx = sb("es_idx", [128, UNROLL, GR], I32)
        onehot = sb("es_onehot", [128, 2, GR, 128], BF16)
        onehot_t = sb("es_onehot_t", [128, RING, GR, EP])
        key_e = sb("es_key", [128, 2, GR, D])
        prod = sb("es_prod", [128, 2, GR, D])
        we = sb("es_we", [128, D])
        ps_oh = psums("es_ps_oh", [128, GR, 256], BF16)
        ps_at = psums("es_ps_at", [128, GR, EP])
        ps_e = psums("es_ps_e", [128, GR, D])
        ps_q = psums("es_ps_q", [128, GR, D])
        if first:
            attr = sb("es_attr", [128, RING, GR, D])
            rel = sb("es_rel", [128, 2, GR])
            arg = sb("es_arg", [128, 2, GR, MSG])
            part = sb("es_part", [128, 2, GR, MSG])
            wt = sb("es_wt", [128, MSG])
            bt = sb("es_bt", [128, MSG])

        loaded = sem("es_loaded")
        idx_put, gather_turn = sem("es_idx_put"), sem("es_gather_turn")
        gathered = [sem(f"es_gathered{i}") for i in range(UNROLL)]
        onehot_made, onehot_turned, onehot_copied = sem("es_oh_made"), sem("es_oh_turned"), sem("es_oh_copied")
        turns_ready = sem("es_turns_ready")
        rel_made, product_made, arg_made = sem("es_rel_made"), sem("es_product_made"), sem("es_arg_made")
        whole_made, angle_made, code_made = sem("es_whole_made"), sem("es_angle_made"), sem("es_code_made")
        attr_turned, attr_copied = sem("es_attr_turned"), sem("es_attr_copied")
        e_done, q_done, key_made = sem("es_e_done"), sem("es_q_done"), sem("es_key_made")
        value_made, prod_made, score_made = sem("es_value_made"), sem("es_prod_made"), sem("es_score_made")
        message_in = [sem(f"es_message_in{i}") for i in range(RING)]
        attr_in = [sem(f"es_attr_in{i}") for i in range(RING)]
        attr_out = [sem(f"es_attr_out{i}") for i in range(RING)]
        value_out = [sem(f"es_value_out{i}") for i in range(RING)]
        block = c.enter_context(nc.Block())

        def live(n):
            return not isinstance(n, int) or n < NGR

        def ended(n, back):
            return reached(n, back) and live(n - back)

        @block.gpsimd
        def _(pool):
            def step(n, u):
                pool.wait_ge(idx_put, n + 1)
                if reached(n, UNROLL):
                    pool.wait_ge(value_made, n - UNROLL + 1)
                pool.sem_inc(gather_turn, 1)
                for i in range(GR):
                    pool.indirect_dma_start(kv[:, u, i, :], None, k.d_kv,
                                            bass.IndirectOffsetOnAxis(ap=idx[:, u, i:i + 1], axis=0)).then_inc(gathered[u], 16)

            pipeline(pool, NGR, 0, step)

        @block.sync
        def _(sp):
            sp.dma_start(we[:, :], w.edge).then_inc(loaded, 16)
            if first:
                sp.dma_start(wt[:, :], a.wt.broadcast_to([128, MSG])).then_inc(loaded, 16)
                sp.dma_start(bt[:, :], a.bt.rearrange("(o d) -> o d", o=1).broadcast_to([128, MSG])).then_inc(loaded, 16)

            def step(n, u):
                if live(n):
                    v = u % RING
                    if first:
                        if reached(n, RING):
                            sp.wait_ge(attr_turned, n - RING + 1)
                        _, tiles = nc.values_load_multi_w_load_instructions(
                            k.tile_row[0:1, bass.ds(n * GR, GR)], engines=[mybir.EngineType.SP], min_val=0, max_val=s.T - 1,
                            skip_runtime_bounds_check_because="item_tables holds the tiles in 0 .. T - 1")
                        for i in range(GR):
                            sp.dma_start(attr[:, v, i, MSG:D],
                                         a.message[bass.ds(tiles[i], 1), :, :].rearrange("a p d -> (a p) d")).then_inc(message_in[v], 16)
                    else:
                        if reached(n, RING):
                            sp.wait_ge(e_done, n - RING + 1)
                        sp.dma_start(attr_t[:, v, :, :].rearrange("p a e -> p (a e)"),
                                     k.d_attr[bass.ds(n, 1), :, :].rearrange("a p d -> (a p) d")).then_inc(attr_in[v], 16)
                if ended(n, lag + 1):
                    m, v = n - lag - 1, (u - lag - 1) % RING
                    if first:
                        sp.wait_ge(attr_copied, m + 1)
                        sp.dma_start(k.d_attr[bass.ds(m, 1), :, :].rearrange("a p d -> (a p) d"),
                                     attr_t[:, v, :, :].rearrange("p a e -> p (a e)")).then_inc(attr_out[v], 16)
                    sp.wait_ge(value_made, m + 1)
                    sp.dma_start(k.d_value[bass.ds(m, 1), :, :].rearrange("a p d -> (a p) d"),
                                 both[:, v, :, :].rearrange("p a d -> p (a d)")).then_inc(value_out[v], 16)

            pipeline(sp, NGR, lag + 1, step)
            for v in range(RING):
                if first:
                    sp.wait_ge(attr_out[v], 16 * (NGR // RING))
                sp.wait_ge(value_out[v], 16 * (NGR // RING))

        @block.vector
        def _(dve):
            dve.wait_ge(loaded, 48 if first else 16)
            if first:
                dve.tensor_scalar(wt[:, :], wt[:, :], INV_TWO_PI, None, ALU.mult).then_inc(turns_ready, 1)
                dve.tensor_scalar(bt[:, :], bt[:, :], INV_TWO_PI, 0.25, ALU.mult, ALU.add).then_inc(turns_ready, 1)
                dve.wait_ge(turns_ready, 2)

            def step(n, u):
                h = u % 2
                if live(n):
                    if reached(n, 2):
                        dve.wait_ge(onehot_turned, n - 1)
                    dve.tensor_tensor(onehot[:, h, :, 0:NP], k.node_iota_b[:, :].unsqueeze(1).broadcast_to([128, GR, NP]),
                                      k.local_b[:, bass.ds(n * GR, GR)].unsqueeze(2).broadcast_to([128, GR, NP]),
                                      ALU.is_equal).then_inc(onehot_made, 1)
                    if first:
                        dve.wait_ge(gathered[u], uses(n, u, UNROLL, 16 * GR))
                        if reached(n, 2):
                            dve.wait_ge(product_made, n - 1)
                        dve.tensor_tensor(rel[:, h, :], kv[:, u, :, 2 * D], k.weight[:, bass.ds(n * GR, GR)],
                                          ALU.subtract).then_inc(rel_made, 1)
                m, v, g = n - lag, (u - lag) % UNROLL, (u - lag) % 2
                r, o = n - 1, 1 - h
                score, reduce = ended(n, lag), first and ended(n, 1)
                if score:
                    if not first:
                        dve.wait_ge(gathered[v], uses(m, v, UNROLL, 16 * GR))
                    dve.wait_ge(e_done, m + 1)
                    dve.tensor_tensor(key_e[:, g, :, :], kv[:, v, :, 0:D], ps_e[g][:, :, :], ALU.add).then_inc(key_made, 1)
                if reduce:
                    dve.wait_ge(arg_made, r + 1)
                    dve.tensor_scalar(part[:, o, :, :], arg[:, o, :, :], ROUND, ROUND, ALU.add, ALU.subtract).then_inc(whole_made, 1)
                if score:
                    if reached(m, RING):
                        dve.wait_ge(value_out[v % RING], uses(m - RING, v, RING, 16))
                    dve.tensor_tensor(both[:, v % RING, :, :], kv[:, v, :, D:2 * D], ps_e[g][:, :, :], ALU.add).then_inc(value_made, 1)
                if reduce:
                    dve.wait_ge(whole_made, r + 1)
                    dve.tensor_tensor(arg[:, o, :, :], arg[:, o, :, :], part[:, o, :, :], ALU.subtract).then_inc(angle_made, 1)
                if score:
                    dve.wait_ge(q_done, m + 1)
                    dve.wait_ge(key_made, m + 1)
                    dve.tensor_tensor(prod[:, g, :, :], key_e[:, g, :, :], ps_q[g][:, :, :], ALU.mult).then_inc(prod_made, 1)
                if first and live(n):
                    dve.wait_ge(product_made, n + 1)
                    if reached(n, 2):
                        dve.wait_ge(code_made, n - 1)
                    dve.tensor_tensor(arg[:, h, :, :], part[:, h, :, :],
                                      bt[:, :].unsqueeze(1).broadcast_to([128, GR, MSG]), ALU.add).then_inc(arg_made, 1)
                if score:
                    dve.wait_ge(prod_made, m + 1)
                    dve.tensor_reduce(k.score[:, bass.ds(m * (GR * HEADS), GR * HEADS)],
                                      prod[:, g, :, :].rearrange("p i (h c) -> p (i h) c", c=C), AX.X, ALU.add).then_inc(score_made, 1)

            pipeline(dve, NGR, lag, step)
            dve.wait_ge(score_made, NGR)

        @block.scalar
        def _(act):
            if first:
                act.wait_ge(turns_ready, 2)
            act.copy(idx[:, :, :], k.src[:, 0:UNROLL * GR].rearrange("p (r i) -> p r i", i=GR)).then_inc(idx_put, UNROLL)

            def step(n, u):
                h = u % 2
                if first and ended(n, 2):
                    m, v, g = n - 2, (u - 2) % RING, h
                    act.wait_ge(attr_turned, m + 1)
                    if reached(m, RING):
                        act.wait_ge(attr_out[v], uses(m - RING, v, RING, 16))
                        act.wait_ge(e_done, m - RING + 1)
                    act.copy(attr_t[:, v, :, :], ps_at[g][:, :, :]).then_inc(attr_copied, 1)
                if first and live(n):
                    act.wait_ge(rel_made, n + 1)
                    if reached(n, 2):
                        act.wait_ge(angle_made, n - 1)
                    for i in range(GR):
                        last = act.activation(part[:, h, i, :], wt[:, :], ACT.Identity, bias=k.zero[:, :], scale=rel[:, h, i:i + 1])
                    last.then_inc(product_made, 1)
                if live(n):
                    act.wait_ge(onehot_turned, n + 1)
                    if reached(n, RING):
                        act.wait_ge(q_done, n - RING + 1)
                    act.copy(onehot_t[0:NP, u % RING, :, :], ps_oh[h][0:NP, :, 0:EP]).then_inc(onehot_copied, 1)
                if first and ended(n, 1):
                    m, v, g = n - 1, (u - 1) % RING, 1 - h
                    act.wait_ge(angle_made, m + 1)
                    if reached(m, RING):
                        act.wait_ge(attr_turned, m - RING + 1)
                    act.activation(attr[:, v, :, 0:MSG], arg[:, g, :, :], ACT.Sin, bias=k.zero[:, :], scale=TWO_PI).then_inc(code_made, 1)
                if live(n):
                    act.wait_ge(gathered[u], uses(n, u, UNROLL, 16 * GR))
                    act.copy(idx[:, u, :], k.src[:, bass.ds((n + UNROLL) * GR, GR)]).then_inc(idx_put, 1)

            pipeline(act, NGR, 2 if first else 0, step)

        @block.tensor
        def _(pe):
            pe.wait_ge(loaded, 48 if first else 16)

            def step(n, u):
                h = u % 2
                if live(n):
                    pe.wait_ge(onehot_made, n + 1)
                    if reached(n, 2):
                        pe.wait_ge(onehot_copied, n - 1)
                    for i in range(GR):
                        last = pe.transpose(ps_oh[h][0:NP, i, 0:EP], onehot[:, h, i, 0:NP], k.ident_b[:, :])
                    last.then_inc(onehot_turned, 1)
                if ended(n, lag - 1):
                    m, v, g = n - lag + 1, (u - lag + 1) % RING, (u - lag + 1) % 2
                    if first:
                        pe.wait_ge(attr_copied, m + 1)
                    else:
                        pe.wait_ge(attr_in[v], uses(m, v, RING, 16))
                    if reached(m, 2):
                        pe.wait_ge(value_made, m - 1)
                        pe.wait_ge(key_made, m - 1)
                    for i in range(GR):
                        last = pe.matmul(ps_e[g][:, i, :], attr_t[:, v, i, :], we[:, :], start=True, stop=True)
                    last.then_inc(e_done, 1)
                    _, blocks = nc.values_load_multi_w_load_instructions(
                        k.block_row[0:1, bass.ds(m * GR, GR)], engines=[mybir.EngineType.PE], min_val=0, max_val=s.NB,
                        skip_runtime_bounds_check_because="item_tables holds the blocks in 0 .. NB")
                    pe.wait_ge(onehot_copied, m + 1)
                    if reached(m, 2):
                        pe.wait_ge(prod_made, m - 1)
                    for i in range(GR):
                        last = pe.matmul(ps_q[g][:, i, :], onehot_t[0:NP, v, i, :],
                                         k.query[0:NP, bass.ds(blocks[i], 1), 0:D].rearrange("p a d -> p (a d)"),
                                         start=True, stop=True)
                    last.then_inc(q_done, 1)
                if first and ended(n, 1):
                    m, v, g = n - 1, (u - 1) % RING, 1 - h
                    pe.wait_ge(message_in[v], uses(m, v, RING, 16 * GR))
                    pe.wait_ge(code_made, m + 1)
                    if reached(m, 2):
                        pe.wait_ge(attr_copied, m - 1)
                    for i in range(GR):
                        last = pe.transpose(ps_at[g][:, i, :], attr[:, v, i, :], k.ident[:, :])
                    last.then_inc(attr_turned, 1)

            pipeline(pe, NGR, lag - 1, step)


def softmax_weights(nc, k, s):
    NQ, SL = s.NQ, NG * EP
    with phase(nc, k) as (c, sem):
        def sb(name, shape, dt=F32):
            return c.enter_context(nc.sbuf_tensor(k.tag + name, shape, dt))

        alpha = k.big1[:, 0:HEADS * SL].rearrange("p (h s) -> p h s", h=HEADS)
        peak = k.big2[:, 0:HEADS * SL].rearrange("p (h s) -> p h s", h=HEADS)
        cut = k.big1[:, HEADS * SL:HEADS * SL + SL + 1]
        other = k.big2[:, HEADS * SL:HEADS * SL + 2 * SL].rearrange("p (a s) -> p a s", a=2)
        edge = sb("sm_edge", [128, 10])
        diag = sb("sm_diag", [128, 10, 128])
        rows = sb("sm_rows", [128, 10, 128])
        apart = sb("sm_apart", [128, 2, 2, 128])
        cand = sb("sm_cand", [128, 2, 128])
        joined = sb("sm_joined", [128, 2, HEADS])
        ps_f = [c.enter_context(nc.psum_tensor(k.tag + f"sm_ps_f{i}", [128, HEADS, 128], F32)) for i in range(2)]
        ps_r = [c.enter_context(nc.psum_tensor(k.tag + f"sm_ps_r{i}", [128, 4, 128], F32)) for i in range(3)]
        turned, put, own, peaks, ran, seam, seam_rows, diff, expd, back, done = map(
            sem, ["sm_turned", "sm_put", "sm_own", "sm_peaks", "sm_ran", "sm_seam", "sm_seam_rows", "sm_diff", "sm_expd",
                  "sm_back", "sm_done"])
        block = c.enter_context(nc.Block())

        @block.tensor
        def _(pe):
            for g in range(NG):
                at_least(pe, put, g - 1)
                for h in range(HEADS):
                    v = k.score[:, :].rearrange("p (q g h) -> p g h q", g=NG, h=HEADS)[:, g, h, :]
                    last = pe.transpose(ps_f[g % 2][0:NQ, h, :], v, k.ident[:, :])
                last.then_inc(turned, 1)
            pe.wait_ge(seam, 1)
            for i in range(3):
                w = min(4, 10 - 4 * i)
                last = pe.matmul(ps_r[i][0:NQ, 0:w, :], k.ones[0:NQ, 0:NQ], diag[0:NQ, 4 * i:4 * i + w, :], start=True, stop=True)
            last.then_inc(seam_rows, 1)
            pe.wait_ge(expd, HEADS)
            for g in range(NG):
                at_least(pe, back, g - 1)
                for h in range(HEADS):
                    last = pe.transpose(ps_f[g % 2][:, h, 0:NQ], peak[0:NQ, h, EP * g:EP * g + EP], k.ident[0:NQ, 0:NQ])
                last.then_inc(done, 1)

        @block.scalar
        def _(act):
            for g in range(NG):
                act.wait_ge(turned, g + 1)
                act.copy(alpha[0:NQ, :, EP * g:EP * g + EP], ps_f[g % 2][0:NQ, :, :]).then_inc(put, 1)
            for h in range(HEADS):
                act.wait_ge(diff, h + 1)
                act.activation(peak[0:NQ, h, :], peak[0:NQ, h, :], ACT.Exp, scale=float(C) ** -0.5).then_inc(expd, 1)
            for g in range(NG):
                act.wait_ge(done, g + 1)
                act.copy(k.score[:, :].rearrange("p (q g h) -> p g h q", g=NG, h=HEADS)[:, g, :, :],
                         ps_f[g % 2][:, :, 0:NQ]).then_inc(back, 1)
            act.wait_ge(back, NG)

        @block.vector
        def _(dve):
            ch = Chain(dve, own)
            dve.memset(cut[0:NQ, 0:1], -BIG)
            dve.memset(cut[0:NQ, SL:SL + 1], -BIG)
            dve.memset(diag[:, :, :], 0.0)
            ch.link(dve.scalar_tensor_tensor(cut[0:NQ, 1:SL], k.key[0:NQ, 1:SL], 0.0, k.key[0:NQ, 0:SL - 1],
                                             ALU.add, ALU.not_equal))
            ch.link(dve.tensor_scalar(cut[0:NQ, 1:SL], cut[0:NQ, 1:SL], -BIG, None, ALU.mult))
            dve.wait_ge(put, NG)
            for h in range(HEADS):
                dve.tensor_tensor_scan(peak[0:NQ, h, :], cut[0:NQ, 0:SL], alpha[0:NQ, h, :], 0.0, ALU.add, ALU.max).then_inc(peaks, 1)
            for h in range(HEADS):
                dve.wait_ge(peaks, h + 1)
                last = dve.tensor_tensor_scan(other[0:NQ, 0, ::-1], cut[0:NQ, SL:0:-1], peak[0:NQ, h, ::-1], 0.0, ALU.add, ALU.max)
                ch.link(last)
                ch.link(dve.tensor_copy(peak[0:NQ, h, :], other[0:NQ, 0, :]))
            for end, slot in ((0, 0), (1, SL - 1)):
                dve.tensor_copy(edge[0:NQ, end:end + 1], k.key[0:NQ, slot:slot + 1])
                last = dve.tensor_copy(edge[0:NQ, 2 + HEADS * end:2 + HEADS * end + HEADS], peak[0:NQ, :, slot])
            ch.link(last)
            dve.tensor_tensor(diag[0:NQ, :, 0:NQ], edge[0:NQ, :].unsqueeze(2).broadcast_to([NQ, 10, NQ]),
                              k.ident[0:NQ, 0:NQ].unsqueeze(1).broadcast_to([NQ, 10, NQ]), ALU.mult).then_inc(seam, 1)
            for end in range(2):
                slot = (0, SL - 1)[end]
                last = dve.tensor_scalar(other[0:NQ, end, :], k.key[0:NQ, :], k.key[0:NQ, slot:slot + 1], -BIG,
                                         ALU.not_equal, ALU.mult)
            ch.link(last)
            dve.wait_ge(seam_rows, 1)
            for i in range(3):
                w = min(4, 10 - 4 * i)
                last = dve.tensor_copy(rows[0:NQ, 4 * i:4 * i + w, :], ps_r[i][0:NQ, 0:w, :])
            ch.link(last)
            for end in range(2):
                last = dve.tensor_scalar(apart[0:NQ, end, :, 0:NQ], rows[0:NQ, 0:2, 0:NQ], edge[0:NQ, end:end + 1], -BIG,
                                         ALU.not_equal, ALU.mult)
            ch.link(last)
            for end in range(2):
                for h in range(HEADS):
                    ch.link(dve.tensor_tensor(cand[0:NQ, :, 0:NQ], rows[0:NQ, 2 + h:7 + h:HEADS, 0:NQ], apart[0:NQ, end, :, 0:NQ], ALU.add))
                    ch.link(dve.tensor_reduce(joined[0:NQ, end, h:h + 1], cand[0:NQ, :, 0:NQ], AX.XY, ALU.max))
            for h in range(HEADS):
                for end in range(2):
                    ch.link(dve.scalar_tensor_tensor(peak[0:NQ, h, :], other[0:NQ, end, :], joined[0:NQ, end, h:h + 1],
                                                     peak[0:NQ, h, :], ALU.add, ALU.max))
                dve.tensor_tensor(peak[0:NQ, h, :], alpha[0:NQ, h, :], peak[0:NQ, h, :], ALU.subtract).then_inc(diff, 1)


def add_up(nc, k, s, weighted):
    NGR = s.G
    W = ACW if weighted else D + 1
    ring = RING if weighted else UNROLL
    with phase(nc, k) as (c, sem):
        def sb(name, shape, dt=F32):
            return c.enter_context(nc.sbuf_tensor(k.tag + name, shape, dt))

        rows = sb("au_rows", [128, ring, GR, ACW])
        onehot = sb("au_onehot", [128, 2, GR, 128])
        if weighted:
            value = sb("au_value", [128, ring, GR, D])
        else:
            idx = sb("au_idx", [128, UNROLL, GR], I32)
        ps = [[c.enter_context(nc.psum_tensor(k.tag + f"au_ps{i}{j}", [128, 2, 256], F32)) for j in range(2)] for i in range(4)]
        arrived = [sem(f"au_arrived{i}") for i in range(ring)]
        ones_put, zeroed, idx_put, gather_turn = sem("au_ones_put"), sem("au_zeroed"), sem("au_idx_put"), sem("au_gather_turn")
        onehot_made, scaled, weight_put = sem("au_onehot_made"), sem("au_scaled"), sem("au_weight_put")
        summed, added = sem("au_summed"), sem("au_added")
        block = c.enter_context(nc.Block())

        def live(n):
            return not isinstance(n, int) or n < NGR

        @block.sync
        def _(sp):
            if weighted:
                def step(n, u):
                    if reached(n, ring):
                        sp.wait_ge(scaled, n - ring + 1)
                    sp.dma_start(value[:, u % ring, :, :].rearrange("p a d -> p (a d)"),
                                 k.d_value[bass.ds(n, 1), :, :].rearrange("a p d -> (a p) d")).then_inc(arrived[u % ring], 16)

                pipeline(sp, NGR, 0, step)

        @block.gpsimd
        def _(pool):
            if not weighted:
                pool.memset(rows[:, :, :, D:ACW], 1.0).then_inc(ones_put, 1)

            def step(n, u):
                if weighted:
                    pool.wait_ge(arrived[u % ring], uses(n, u, ring, 16))
                    if reached(n, ring):
                        pool.wait_ge(summed, n - ring + 1)
                    pool.tensor_tensor(rows[:, u % ring, :, 0:D].rearrange("p i (h c) -> p i h c", c=C),
                                       value[:, u % ring, :, :].rearrange("p i (h c) -> p i h c", c=C),
                                       k.score[:, bass.ds(n * (GR * HEADS), GR * HEADS)].rearrange("p (i h) -> p i h", h=HEADS)
                                       .unsqueeze(3).broadcast_to([128, GR, HEADS, C]), ALU.mult).then_inc(scaled, 1)
                else:
                    pool.wait_ge(idx_put, n + 1)
                    if reached(n, ring):
                        pool.wait_ge(summed, n - ring + 1)
                    pool.sem_inc(gather_turn, 1)
                    for i in range(GR):
                        pool.indirect_dma_start(rows[:, u, i, 0:D], None, k.d_node,
                                                bass.IndirectOffsetOnAxis(ap=idx[:, u, i:i + 1], axis=0)).then_inc(arrived[u], 16)

            pipeline(pool, NGR, 0, step)

        @block.scalar
        def _(act):
            half = (s.NB + 1) * ACW // 2
            if weighted:
                for big in (k.big1, k.big2):
                    act.activation(big[:, half:2 * half], k.zero[:, 0:1].broadcast_to([128, half]), ACT.Copy).then_inc(zeroed, 1)

                def step(n, u):
                    if reached(n, ring):
                        act.wait_ge(summed, n - ring + 1)
                    act.copy(rows[:, u % ring, :, D:ACW],
                             k.score[:, bass.ds(n * (GR * HEADS), GR * HEADS)].rearrange("p (i h) -> p i h", h=HEADS)).then_inc(weight_put, 1)

                pipeline(act, NGR, 0, step)
            else:
                act.copy(idx[:, :, :], k.src[:, 0:UNROLL * GR].rearrange("p (r i) -> p r i", i=GR)).then_inc(idx_put, UNROLL)
                act.activation(k.big_acc(weighted)[:, half:2 * half], k.zero[:, 0:1].broadcast_to([128, half]), ACT.Copy).then_inc(zeroed, 1)

                def step(n, u):
                    act.wait_ge(arrived[u], uses(n, u, ring, 16 * GR))
                    act.copy(idx[:, u, :], k.src[:, bass.ds((n + UNROLL) * GR, GR)]).then_inc(idx_put, 1)

                pipeline(act, NGR, 0, step)

        @block.vector
        def _(dve):
            half = (s.NB + 1) * ACW // 2
            dve.memset(k.big_acc(weighted)[:, 0:half], 0.0).then_inc(zeroed, 1)
            if weighted:
                dve.memset(k.big1[:, 0:half], 0.0).then_inc(zeroed, 1)
            accs = (k.nodes, k.query) if weighted else (k.acc(weighted),)
            dve.wait_ge(zeroed, 2 * len(accs))

            def step(n, u):
                if live(n):
                    if reached(n, 2):
                        dve.wait_ge(summed, n - 1)
                    dve.tensor_tensor(onehot[:, u % 2, :, 0:NP], k.node_iota[:, :].unsqueeze(1).broadcast_to([128, GR, NP]),
                                      k.local[:, bass.ds(n * GR, GR)].unsqueeze(2).broadcast_to([128, GR, NP]),
                                      ALU.is_equal).then_inc(onehot_made, 1)
                if reached(n, 2):
                    m, g = n - 2, (u - 2) % 4
                    _, blocks = nc.values_load_multi_w_load_instructions(
                        k.block_row[0:1, bass.ds(m * GR, GR)], engines=[mybir.EngineType.DVE], min_val=0, max_val=s.NB,
                        skip_runtime_bounds_check_because="item_tables holds the blocks in 0 .. NB")
                    dve.wait_ge(summed, m + 1)

                    for i in range(GR):
                        row = accs[i % len(accs)][0:NP, bass.ds(blocks[i], 1), 0:W].rearrange("p a d -> p (a d)")
                        at_least(dve, added, m * GR + i + 1 - len(accs))
                        dve.tensor_tensor(row, row, ps[g][i // 2][0:NP, i % 2, 0:W], ALU.add).then_inc(added, 1)

            pipeline(dve, NGR, 2, step)
            dve.wait_ge(added, NGR * GR)

        @block.tensor
        def _(pe):
            if not weighted:
                pe.wait_ge(ones_put, 1)

            def step(n, u):
                pe.wait_ge(onehot_made, n + 1)
                if weighted:
                    pe.wait_ge(scaled, n + 1)
                    pe.wait_ge(weight_put, n + 1)
                else:
                    pe.wait_ge(arrived[u], uses(n, u, ring, 16 * GR))
                if reached(n, 4):
                    pe.wait_ge(added, (n - 3) * GR)
                for i in range(GR):
                    last = pe.matmul(ps[u % 4][i // 2][0:NP, i % 2, 0:W], onehot[:, u % 2, i, 0:NP], rows[:, u % ring, i, 0:W],
                                     start=True, stop=True)
                last.then_inc(summed, 1)

            pipeline(pe, NGR, 0, step)


def finish_conv(nc, k, s, a, residual):
    NB = s.NB
    with phase(nc, k) as (c, sem):
        def sb(name, shape, dt=F32):
            return c.enter_context(nc.sbuf_tensor(k.tag + name, shape, dt))

        share = sb("fc_share", [128, NB, HEADS])
        skip = sb("fc_skip", [128, 4, D])
        x = sb("fc_x", [128, 4, D])
        norm = sb("fc_norm", [128, 2, D])
        own, normed, out_made, x_made, final = map(sem, ["fc_own", "fc_normed", "fc_out", "fc_xm", "fc_final"])
        skip_in = [sem(f"fc_skip_in{i}") for i in range(4)]
        x_in = [sem(f"fc_x_in{i}") for i in range(4)]
        stored = sem("fc_stored")
        block = c.enter_context(nc.Block())

        def steps(engine, step):
            for b in range(4):
                step(b, b)
            if NB > 4:
                with engine.Fori(1, NB // 4) as it:
                    for u in range(4):
                        step(it * 4 + u, u)

        def uses(b, u):
            return (b // 4 + 1) * 16 if isinstance(b, int) else (b - u + 4) * 4

        @block.sync
        def _(sp):
            def step(b, u):
                if reached(b, 4):
                    sp.wait_ge(final, b - 3)
                sp.dma_start(skip[0:NP, u, :], k.d_skip[bass.ds(b * NP, NP), :]).then_inc(skip_in[u], 16)
                if residual:
                    sp.dma_start(x[0:NP, u, :], a.x[bass.ds(b * NP, NP), :]).then_inc(x_in[u], 16)

            steps(sp, step)
            if residual:
                sp.wait_ge(final, NB)
                sp.dma_start(k.d_x1.rearrange("(b p) d -> p b d", p=NP), k.nodes[0:NP, 0:NB, 0:D]).then_inc(stored, 16)
                sp.wait_ge(stored, 16)

        @block.vector
        def _(dve):
            ch = Chain(dve, own)
            ch.link(dve.tensor_tensor(k.nodes[0:NP, 0:NB, :], k.nodes[0:NP, 0:NB, :], k.query[0:NP, 0:NB, :], ALU.add))
            ch.link(dve.tensor_scalar(share[0:NP, :, :], k.nodes[0:NP, 0:NB, D:ACW], 1e-16, None, ALU.add))
            ch.link(dve.reciprocal(share[0:NP, :, :], share[0:NP, :, :]))

            def step(b, u):
                row = k.nodes[0:NP, bass.ds(b, 1), 0:D].rearrange("p a d -> p (a d)")
                dve.tensor_tensor(norm[0:NP, u % 2, :].rearrange("p (h c) -> p h c", c=C),
                                  row.rearrange("p (h c) -> p h c", c=C),
                                  share[0:NP, bass.ds(b, 1), :].rearrange("p a h -> p (a h)").unsqueeze(2).broadcast_to([NP, HEADS, C]),
                                  ALU.mult).then_inc(normed, 1)
                if residual:
                    dve.wait_ge(x_in[u], uses(b, u))
                    dve.wait_ge(skip_in[u], uses(b, u))
                    dve.tensor_tensor(skip[0:NP, u, :], skip[0:NP, u, :], x[0:NP, u, :], ALU.add).then_inc(x_made, 1)
                    dve.wait_ge(x_made, b + 1)
                dve.wait_ge(skip_in[u], uses(b, u))
                dve.wait_ge(normed, b + 1)
                dve.tensor_tensor(row, norm[0:NP, u % 2, :], skip[0:NP, u, :], ALU.add).then_inc(final, 1)

            steps(dve, step)
            dve.wait_ge(final, NB)


def store_node_table(nc, k, s):
    with phase(nc, k) as (c, sem):
        stored = sem("st_stored")
        block = c.enter_context(nc.Block())


        @block.sync
        def _(sp):
            sp.dma_start(k.d_node.rearrange("(b p) d -> p b d", p=NP), k.nodes[0:NP, 0:s.NB, 0:D]).then_inc(stored, 16)
            sp.wait_ge(stored, 16)


def finish_mean_layer(nc, k, s, a, layer, layers, out):
    NB = s.NB
    last_layer = layer == layers - 1
    with phase(nc, k) as (c, sem):
        def sb(name, shape, dt=F32):
            return c.enter_context(nc.sbuf_tensor(k.tag + name, shape, dt))

        wl = sb("fm_wl", [128, D])
        wr = sb("fm_wr", [128, D])
        bl = sb("fm_bl", [128, D])
        inv = sb("fm_inv", [128, NB])
        mean = sb("fm_mean", [128, PR, D])
        still = sb("fm_still", [128, PR, D])
        turned_sb = sb("fm_turned", [128, PR, 2, NP])
        raw = sb("fm_raw", [128, PR, D])
        x1 = sb("fm_x1", [128, PR, D])
        res = sb("fm_res", [128, PR, D])
        ps_t = [c.enter_context(nc.psum_tensor(k.tag + f"fm_ps_t{i}", [128, 2, 128], F32)) for i in range(PR)]
        ps_o = [c.enter_context(nc.psum_tensor(k.tag + f"fm_ps_o{i}", [128, D], F32)) for i in range(PR)]
        loaded, own, meaned, stilled, turned, copied, multiplied, biased, made = map(
            sem, ["fm_loaded", "fm_own", "fm_meaned", "fm_stilled", "fm_turned_s", "fm_copied", "fm_multiplied", "fm_biased", "fm_made"])
        x1_in = [sem(f"fm_x1_in{i}") for i in range(PR)]
        stored = [sem(f"fm_stored{i}") for i in range(PR)]
        block = c.enter_context(nc.Block())
        acc = k.acc(False)

        def steps(engine, lag, step):
            for b in range(2 * PR):
                step(b, b % PR)
            with engine.Fori(2, NB // PR) as it:
                for u in range(PR):
                    step(it * PR + u, u)
            for b in range(NB, NB + lag):
                step(b, b % PR)

        def live(b):
            return not isinstance(b, int) or b < NB

        @block.sync
        def _(sp):
            sp.dma_start(wl[:, :], a.wl[layer]).then_inc(loaded, 16)
            sp.dma_start(wr[:, :], a.wr[layer]).then_inc(loaded, 16)
            sp.dma_start(bl[:, :], a.bl[layer:layer + 1, :].broadcast_to([128, D])).then_inc(loaded, 16)

            def step(b, u):
                if live(b) and last_layer:
                    if reached(b, PR):
                        sp.wait_ge(made, b - PR + 1)
                    sp.dma_start(x1[0:NP, u, :], k.d_x1[bass.ds(b * NP, NP), :]).then_inc(x1_in[u], 16)
                if reached(b, 3):
                    m, v = b - 3, (u - 3) % PR
                    sp.wait_ge(made, m + 1)
                    target = out if last_layer else k.d_node
                    source = res[0:NP, v, :] if last_layer else k.nodes[0:NP, bass.ds(m, 1), 0:D].rearrange("p a d -> p (a d)")
                    sp.dma_start(target[bass.ds(m * NP, NP), :], source).then_inc(stored[v], 16)

            steps(sp, 3, step)
            for u in range(PR):
                sp.wait_ge(stored[u], 16 * (NB // PR))

        @block.vector
        def _(dve):
            ch = Chain(dve, own)
            ch.link(dve.tensor_scalar(inv[0:NP, :], acc[0:NP, 0:NB, D], 1.0, None, ALU.max))
            ch.link(dve.reciprocal(inv[0:NP, :], inv[0:NP, :]))
            dve.wait_ge(loaded, 48)

            def step(b, u):
                if live(b):
                    if reached(b, PR):
                        dve.wait_ge(turned, b - PR + 1)
                    dve.tensor_scalar(mean[0:NP, u, :], acc[0:NP, bass.ds(b, 1), 0:D].rearrange("p a d -> p (a d)"),
                                      inv[0:NP, bass.ds(b, 1)], None, ALU.mult).then_inc(meaned, 1)
                if reached(b, 3):
                    m, v = b - 3, (u - 3) % PR
                    dve.wait_ge(multiplied, m + 1)
                    if reached(m, PR):
                        dve.wait_ge(made, m - PR + 1)
                    dve.tensor_tensor(raw[0:NP, v, :], ps_o[v][0:NP, :], bl[0:NP, :], ALU.add).then_inc(biased, 1)
                    if last_layer:
                        dve.wait_ge(x1_in[v], uses(m, v, PR, 16))
                        dve.wait_ge(biased, m + 1)
                        if reached(m, PR):
                            dve.wait_ge(stored[v], uses(m - PR, v, PR, 16))
                        dve.tensor_tensor(res[0:NP, v, :], raw[0:NP, v, :], x1[0:NP, v, :], ALU.add).then_inc(made, 1)

            steps(dve, 3, step)

        @block.tensor
        def _(pe):
            pe.wait_ge(loaded, 48)

            def step(b, u):
                if live(b):
                    pe.wait_ge(meaned, b + 1)
                    pe.wait_ge(stilled, b + 1)
                    if reached(b, PR):
                        pe.wait_ge(copied, b - PR + 1)
                    pe.transpose(ps_t[u][:, 0, 0:NP], mean[0:NP, u, :], k.ident[0:NP, 0:NP])
                    pe.transpose(ps_t[u][:, 1, 0:NP], still[0:NP, u, :],
                                 k.ident[0:NP, 0:NP]).then_inc(turned, 1)
                if reached(b, 1):
                    m, v = b - 1, (u - 1) % PR
                    pe.wait_ge(copied, m + 1)
                    if reached(m, PR):
                        pe.wait_ge(biased, m - PR + 1)
                    pe.matmul(ps_o[v][0:NP, :], turned_sb[:, v, 0, :], wl[:, :], start=True, stop=False)
                    pe.matmul(ps_o[v][0:NP, :], turned_sb[:, v, 1, :], wr[:, :], start=False, stop=True).then_inc(multiplied, 1)

            steps(pe, 1, step)

        @block.gpsimd
        def _(pool):
            def step(b, u):
                if reached(b, PR):
                    pool.wait_ge(turned, b - PR + 1)
                pool.tensor_copy(still[0:NP, u, :], k.nodes[0:NP, bass.ds(b, 1), 0:D].rearrange("p a d -> p (a d)")).then_inc(stilled, 1)

            steps(pool, 0, step)

        @block.scalar
        def _(act):
            def step(b, u):
                if live(b):
                    act.wait_ge(turned, b + 1)
                    if reached(b, PR):
                        act.wait_ge(multiplied, b - PR + 1)
                    act.copy(turned_sb[:, u, :, :], ps_t[u][:, :, 0:NP]).then_inc(copied, 1)
                if reached(b, 3) and not last_layer:
                    m, v = b - 3, (u - 3) % PR
                    act.wait_ge(biased, m + 1)
                    act.activation(k.nodes[0:NP, bass.ds(m, 1), 0:D].rearrange("p a d -> p (a d)"), raw[0:NP, v, :],
                                   ACT.Relu).then_inc(made, 1)

            steps(act, 3, step)


def graph_kernel(nc, a, out):
    s = Shapes(a.x, a.src)
    k = Store()
    k.tag = "prepare_"

    def dram(name, shape, dt=F32):
        return nc.dram_tensor(name, shape, dt, kind="Internal").ap()

    k.d_tile_of = dram("d_tile_of", [s.I], I32)
    k.d_block_of = dram("d_block_of", [s.I], I32)
    k.d_kv = dram("d_kv", [s.N, KVW])
    k.d_skip = dram("d_skip", [s.N, D])
    k.d_attr = dram("d_attr", [s.G, 128, GR * EP])
    k.d_value = dram("d_value", [s.G, EP, GR * D])
    k.d_x1 = dram("d_x1", [s.N, D])
    k.d_node = dram("d_node", [s.N, D])
    with ExitStack() as c:
        def sb(name, shape, dt=F32):
            return c.enter_context(nc.sbuf_tensor(name, shape, dt))

        k.ident = sb("ident", [128, 128])
        k.ident_b = sb("ident_b", [128, 128], BF16)
        k.node_iota_i = sb("node_iota_i", [128, NP], I32)
        k.node_iota = sb("node_iota", [128, NP])
        k.node_iota_b = sb("node_iota_b", [128, NP], BF16)
        k.ones = sb("ones", [128, 128])
        k.zero = sb("zero", [128, 1])
        k.eps = sb("eps", [128, 1])
        walk = sb("walk", [2, s.I], I32)
        k.tile_row, k.block_row = walk[0:1, :], walk[1:2, :]
        k.local = sb("local_t", [128, s.I])
        k.local_b = sb("local_b", [128, s.I], BF16)
        k.src = sb("src_t", [128, s.I + UNROLL * GR], I32)
        k.weight = sb("weight_t", [128, s.I])
        k.key = sb("key", [128, NG * EP])
        k.vec = sb("vec", [128, s.NB])
        constants(nc, k)
        item_tables(nc, k, s, a)

        k.score = sb("score", [128, s.I * HEADS])
        big = max((s.NB + 1) * ACW, (HEADS + 2) * NG * EP, GR * (UNROLL * KVW + 2 * RING * D))
        k.big1 = sb("big1", [128, big])
        k.big2 = sb("big2", [128, big])
        k.query = k.big1[:, 0:(s.NB + 1) * ACW].rearrange("p (b d) -> p b d", d=ACW)
        k.nodes = k.big2[:, 0:(s.NB + 1) * ACW].rearrange("p (b d) -> p b d", d=ACW)
        k.acc = lambda weighted: k.nodes if weighted else k.query
        k.big_acc = lambda weighted: k.big2 if weighted else k.big1

        load_nodes(nc, k, s, a)
        layer_norm(nc, k, s)
        for n in range(2):
            k.tag = f"conv{n}_"
            project_nodes(nc, k, s, a.convs[n])
            edge_scores(nc, k, s, a, a.convs[n], first=n == 0)
            softmax_weights(nc, k, s)
            add_up(nc, k, s, weighted=True)
            finish_conv(nc, k, s, a, residual=n == 1)
        k.tag = "between_"
        layer_norm(nc, k, s)
        store_node_table(nc, k, s)
        layers = a.wl.shape[0]
        for n in range(layers):
            k.tag = f"mean{n}_"
            add_up(nc, k, s, weighted=False)
            finish_mean_layer(nc, k, s, a, n, layers, out)


def layout(inputs):
    import numpy as np

    N = inputs["x"].shape[0]
    pad = -inputs["src"].shape[0] % EP
    edge = lambda v, fill: np.concatenate([np.asarray(v), np.full((pad,) + v.shape[1:], fill, v.dtype)])
    arrays = {
        "x": inputs["x"], "vec": inputs["node_vec"],
        "src": edge(inputs["src"], 0).reshape(-1, EP),
        "dst": edge(inputs["dst"], N).reshape(-1, EP),
        "weight": edge(inputs["edge_weight"], 0).reshape(-1, EP),
        "message": edge(inputs["edge_attr_64"], 0).reshape(-1, EP, MSG),
        "wt": inputs["L0_gnn_Wt"], "bt": inputs["L0_gnn_bt"], "bl": inputs["L1_gnn_bl"],
        "wl": np.swapaxes(np.asarray(inputs["L1_gnn_Wl"]), 1, 2),
        "wr": np.swapaxes(np.asarray(inputs["L1_gnn_Wr"]), 1, 2),
    }
    for n in "12":
        arrays["we" + n] = inputs["L0_gnn_We" + n]
        for name in ("q", "k", "v", "skip"):
            arrays[f"w{name}{n}"] = inputs[f"L0_gnn_W{name}{n}"]
            arrays[f"b{name}{n}"] = inputs[f"L0_gnn_b{name}{n}"]
    return {name: np.ascontiguousarray(v) for name, v in arrays.items()}


def build(nc, arrays):
    def tensor(name):
        v = arrays[name]
        return nc.dram_tensor(f"in_{name}", v.shape, mybir.dt.from_np(v.dtype), kind="ExternalInput").ap()

    a = Store()
    a.x, a.vec = tensor("x"), tensor("vec")
    a.src, a.dst, a.weight, a.message = tensor("src"), tensor("dst"), tensor("weight"), tensor("message")
    a.wt, a.bt = tensor("wt"), tensor("bt")
    a.wl, a.wr, a.bl = tensor("wl"), tensor("wr"), tensor("bl")
    a.convs = []
    for n in "12":
        conv = Store()
        conv.edge = tensor("we" + n)
        conv.weights = [tensor(f"w{p}{n}") for p in ("q", "k", "v", "skip")]
        conv.biases = [tensor(f"b{p}{n}") for p in ("q", "k", "v", "skip")]
        a.convs.append(conv)
    out = nc.dram_tensor("out_0_dram", arrays["x"].shape, F32, kind="ExternalOutput").ap()
    graph_kernel(nc, a, out)


def kernel(**inputs):
    import concourse.bacc as _bacc
    from concourse.bass_utils import run_bass_kernel_spmd as _run

    nc = _bacc.Bacc("TRN2", target_bir_lowering=False, num_devices=1)
    arrays = layout(inputs)
    build(nc, arrays)
    r = _run(nc, [{f"in_{name}": v for name, v in arrays.items()}], core_ids=[0])
    return r.results[0]["out_0_dram"]
```

```python
from contextlib import ExitStack, contextmanager

import concourse.bass as bass
from concourse import mybir

F32 = mybir.dt.float32
BF16 = mybir.dt.bfloat16
I32 = mybir.dt.int32
ALU = mybir.AluOpType
ACT = mybir.ActivationFunctionType
AX = mybir.AxisListType

D = 128
HEADS = 4
C = D // HEADS
MSG = 64
EP = 128
NP = 125
GR = 4
NG = 16
UNROLL = 8
RING = 4
PR = 4
KVW = 2 * D + 4
ACW = D + HEADS
BIG = 1.0e30
ROUND = 12582912.0
TWO_PI = 6.283185
INV_TWO_PI = 0.15915494309189535


class Shapes:

    def __init__(self, x, src):
        self.N = x.shape[0]
        self.NB = self.N // NP
        self.T = src.shape[0]
        self.NQ = -(-(self.T + self.NB) // NG)
        self.NQ += self.NQ % 2
        self.I = NG * self.NQ
        self.G = self.I // GR
        assert self.N % NP == 0 and self.NB % 4 == 0 and self.NQ <= 128
        self.CH = max(n for n in range(1, 11) if self.NB % (2 * n) == 0)


class Store:
    pass


class Chain:

    def __init__(self, engine, sem):
        self.engine, self.sem, self.n = engine, sem, 0

    def link(self, instruction):
        self.n += 1
        instruction.then_inc(self.sem, 1)
        self.engine.wait_ge(self.sem, self.n)


def at_least(engine, sem, value):
    if not isinstance(value, int) or value > 0:
        engine.wait_ge(sem, value)


def reached(n, back=0):
    return not isinstance(n, int) or n - back >= 0


def pipeline(engine, count, lag, step, period=UNROLL):
    for n in range(period):
        step(n, n)
    if count > period:
        with engine.Fori(1, count // period) as it:
            for u in range(period):
                step(it * period + u, u)
    for n in range(count, count + lag):
        step(n, n % period)


def uses(n, u, ring, per):
    return (n // ring + 1) * per if isinstance(n, int) else (n - u % ring + ring) * (per // ring)


@contextmanager
def phase(nc, k):
    made = []

    def sem(name):
        made.append(nc.alloc_semaphore(name=k.tag + name))
        return made[-1]

    with ExitStack() as c:
        yield c, sem
    nc.clear_and_free_semaphores(made)
    nc.all_engine_barrier()


def constants(nc, k):
    with phase(nc, k) as (c, sem):
        made, cast = sem("const_made"), sem("const_cast")
        block = c.enter_context(nc.Block())


        @block.gpsimd
        def _(pool):
            pool.memset(k.ident[:, :], 0.0).then_inc(made, 1)
            pool.wait_ge(made, 1)
            pool.affine_select(out=k.ident[:, :], in_=k.ident[:, :], compare_op=ALU.not_equal, fill=1.0,
                               base=0, pattern=[[-1, 128]], channel_multiplier=1).then_inc(made, 1)
            pool.iota(k.node_iota_i[:, :], pattern=[[1, NP]], base=0, channel_multiplier=0).then_inc(made, 1)
            pool.memset(k.zero[:, :], 0.0)
            pool.memset(k.ones[:, :], 1.0)
            pool.memset(k.eps[:, :], 1e-5).then_inc(made, 1)

        @block.vector
        def _(dve):
            dve.wait_ge(made, 4)
            dve.tensor_copy(k.ident_b[:, :], k.ident[:, :])
            dve.tensor_copy(k.node_iota[:, :], k.node_iota_i[:, :]).then_inc(cast, 1)
            dve.wait_ge(cast, 1)
            dve.tensor_copy(k.node_iota_b[:, :], k.node_iota[:, :]).then_inc(cast, 1)
            dve.wait_ge(cast, 2)


def item_tables(nc, k, s, a):
    NQ, T, I = s.NQ, s.T, s.I
    COUNTED = NG * 5 // 8
    SL = NG * EP
    with phase(nc, k) as (c, sem):
        def sb(name, shape, dt=F32):
            return c.enter_context(nc.sbuf_tensor(k.tag + name, shape, dt))

        last_i = sb("last_i", [1, T], I32)
        tile_i = sb("tile_i", [1, T], I32)
        last_f = sb("last_f", [1, T])
        tile_f = sb("tile_f", [1, T])
        leave = sb("leave", [1, T])
        leave_all = sb("leave_all", [128, T])
        junk = sb("junk", [128, 2, T])
        junk_act = sb("junk_act", [128, 2, T])
        item_less = sb("item_less", [128, NG])
        item_i = sb("item_i", [128, NG], I32)
        item_f = sb("item_f", [128, NG])
        tile_of = sb("tile_of", [128, NG])
        block_of = sb("block_of", [128, NG])
        tile_of_i = sb("tile_of_i", [128, NG], I32)
        block_of_i = sb("block_of_i", [128, NG], I32)
        base = sb("base", [128, NG])
        src_q = sb("src_q", [128, NG, EP], I32)
        dst_q = sb("dst_q", [128, NG, EP], I32)
        weight_q = sb("weight_q", [128, NG, EP])
        src_f = sb("src_f", [128, NG, EP])
        dst_f = sb("dst_f", [128, NG, EP])
        local = sb("local", [128, NG, EP])
        valid = sb("valid", [128, NG, EP])
        ps_row = c.enter_context(nc.psum_tensor("ps_row", [128, 4, 512], F32))
        ps_t = [c.enter_context(nc.psum_tensor(k.tag + f"ps_t{i}", [128, 4, 128], F32)) for i in range(2)]

        loaded, iotas, leave_done, row_ready, row_copied = map(sem, ["loaded", "iotas", "leave_done", "row_ready", "row_copied"])
        tiles_known, tiles_stored, tiles_back = map(sem, ["tiles_known", "tiles_stored", "tiles_back"])
        items_cast, counted, signs_summed = map(sem, ["items_cast", "counted", "signs_summed"])
        src_in, dst_in, weight_in = map(sem, ["src_in", "dst_in", "weight_in"])
        src_cast, local_done, own, turned, placed = map(sem, ["src_cast", "local_done", "own", "turned", "placed"])
        block = c.enter_context(nc.Block())

        @block.sync
        def _(sp):
            sp.dma_start(last_i[:, :], a.dst[:, EP - 1:EP].rearrange("t o -> o t"),
                         allow_slow_non_contiguous=True).then_inc(loaded, 16)
            sp.wait_ge(tiles_known, 1)
            sp.dma_start(k.d_tile_of.rearrange("(q g) -> q g", g=NG), tile_of_i[0:NQ, :]).then_inc(tiles_stored, 16)
            sp.dma_start(k.d_block_of.rearrange("(q g) -> q g", g=NG), block_of_i[0:NQ, :]).then_inc(tiles_stored, 16)
            sp.wait_ge(tiles_stored, 32)
            sp.dma_start(k.tile_row[:, :], k.d_tile_of.rearrange("(o i) -> o i", o=1)).then_inc(tiles_back, 16)
            sp.dma_start(k.block_row[:, :], k.d_block_of.rearrange("(o i) -> o i", o=1)).then_inc(tiles_back, 16)
            sp.wait_ge(tiles_back, 32)

        @block.gpsimd
        def _(pool):
            pool.memset(k.src[:, I:I + UNROLL * GR], 0)
            pool.iota(tile_i[:, :], pattern=[[1, T]], base=0, channel_multiplier=0)
            pool.iota(item_i[:, :], pattern=[[1, NG]], base=0, channel_multiplier=NG).then_inc(iotas, 1)
            pool.wait_ge(tiles_known, 1)
            for table, out, done in ((a.dst, dst_q, dst_in), (a.src, src_q, src_in), (a.weight, weight_q, weight_in)):
                for g in range(NG):
                    pool.indirect_dma_start(out[0:NQ, g, :], None, table,
                                            bass.IndirectOffsetOnAxis(ap=tile_of_i[0:NQ, g:g + 1], axis=0)).then_inc(done, 16)

        @block.vector
        def _(dve):
            ch = Chain(dve, own)
            dve.wait_ge(iotas, 1)
            dve.tensor_copy(tile_f[:, :], tile_i[:, :])
            dve.tensor_copy(item_f[:, :], item_i[:, :]).then_inc(items_cast, 1)
            dve.wait_ge(items_cast, 1)
            dve.tensor_scalar(item_less[:, :], item_f[:, :], -0.5, None, ALU.add).then_inc(items_cast, 1)
            dve.wait_ge(loaded, 16)
            ch.link(dve.tensor_copy(last_f[:, :], last_i[:, :]))
            ch.link(dve.tensor_scalar(last_f[:, :], last_f[:, :], 1.0 / NP, 0.5 / NP - 0.5, ALU.mult, ALU.add))
            ch.link(dve.tensor_scalar(last_f[:, :], last_f[:, :], ROUND, ROUND, ALU.add, ALU.subtract))
            dve.tensor_tensor(leave[:, :], last_f[:, :], tile_f[:, :], ALU.add).then_inc(leave_done, 1)
            dve.wait_ge(row_copied, 1)
            for g in range(COUNTED):
                last = dve.tensor_scalar(junk[0:NQ, g % 2, :], leave_all[0:NQ, :], item_f[0:NQ, g:g + 1], 0.0,
                                         ALU.is_lt, ALU.add, accum_out=tile_of[0:NQ, g:g + 1])
                last.then_inc(counted, 1)
                if g > 0:
                    dve.wait_ge(counted, g)
            dve.wait_ge(counted, COUNTED)
            dve.wait_ge(signs_summed, NG - COUNTED)
            ch.link(dve.tensor_scalar(tile_of[0:NQ, COUNTED:NG], tile_of[0:NQ, COUNTED:NG], 0.5, 0.5 * T, ALU.mult, ALU.add))
            ch.link(dve.tensor_scalar(tile_of[0:NQ, :], tile_of[0:NQ, :], float(T - 1), None, ALU.min))
            ch.link(dve.tensor_tensor(block_of[0:NQ, :], item_f[0:NQ, :], tile_of[0:NQ, :], ALU.subtract))
            ch.link(dve.tensor_scalar(block_of[0:NQ, :], block_of[0:NQ, :], float(s.NB), None, ALU.min))
            dve.tensor_copy(tile_of_i[0:NQ, :], tile_of[0:NQ, :])
            dve.tensor_copy(block_of_i[0:NQ, :], block_of[0:NQ, :]).then_inc(tiles_known, 1)
            ch.link(dve.tensor_scalar(base[0:NQ, :], block_of[0:NQ, :], float(NP), None, ALU.mult))
            dve.wait_ge(dst_in, 16 * NG)
            ch.link(dve.tensor_copy(dst_f[0:NQ, :, :], dst_q[0:NQ, :, :]))
            ch.link(dve.tensor_tensor(local[0:NQ, :, :], dst_f[0:NQ, :, :],
                                      base[0:NQ, :].unsqueeze(2).broadcast_to([NQ, NG, EP]), ALU.subtract))
            ch.link(dve.tensor_scalar(valid[0:NQ, :, :], local[0:NQ, :, :], 0.0, None, ALU.is_ge))
            ch.link(dve.scalar_tensor_tensor(valid[0:NQ, :, :], local[0:NQ, :, :], float(NP), valid[0:NQ, :, :],
                                             ALU.is_lt, ALU.mult))
            ch.link(dve.scalar_tensor_tensor(local[0:NQ, :, :], local[0:NQ, :, :], 1.0, valid[0:NQ, :, :],
                                             ALU.add, ALU.mult))
            dve.tensor_scalar(local[0:NQ, :, :], local[0:NQ, :, :], -1.0, None, ALU.add).then_inc(local_done, 1)
            dve.wait_ge(src_in, 16 * NG)
            dve.tensor_copy(src_f[0:NQ, :, :], src_q[0:NQ, :, :]).then_inc(src_cast, 1)
            ch.link(dve.scalar_tensor_tensor(dst_f[0:NQ, :, :], dst_f[0:NQ, :, :], 1.0, valid[0:NQ, :, :],
                                             ALU.add, ALU.mult))
            ch.link(dve.tensor_scalar(k.key[0:NQ, :], dst_f[0:NQ, :, :].rearrange("q g e -> q (g e)"), -1.0, None, ALU.add))
            dve.wait_ge(src_cast, 1)
            dve.wait_ge(placed, NG // 4)
            ch.link(dve.tensor_copy(k.local_b[:, :], k.local[:, :]))

        order = [(t, g4) for t in range(3) for g4 in range(NG // 4)]

        @block.tensor
        def _(pe):
            pe.wait_ge(leave_done, 1)
            for i in range(-(-T // 512)):
                w = min(512, T - 512 * i)
                last = pe.matmul(ps_row[0:NQ, i, 0:w], k.ones[0:1, 0:NQ], leave[:, 512 * i:512 * i + w], start=True, stop=True)
            last.then_inc(row_ready, 1)
            pe.wait_ge(local_done, 1)
            for j, (t, g4) in enumerate(order):
                table = (local, src_f, weight_q)[t]
                if g4 == 0 and t == 1:
                    pe.wait_ge(src_cast, 1)
                if g4 == 0 and t == 2:
                    pe.wait_ge(weight_in, 16 * NG)
                at_least(pe, placed, j - 1)
                for g in range(4):
                    last = pe.transpose(ps_t[j % 2][:, g, 0:NQ], table[0:NQ, 4 * g4 + g, :], k.ident[0:NQ, 0:NQ])
                last.then_inc(turned, 1)

        @block.scalar
        def _(act):
            act.wait_ge(row_ready, 1)
            for i in range(-(-T // 512)):
                w = min(512, T - 512 * i)
                last = act.copy(leave_all[0:NQ, 512 * i:512 * i + w], ps_row[0:NQ, i, 0:w])
            last.then_inc(row_copied, 1)
            act.wait_ge(row_copied, 1)
            act.wait_ge(items_cast, 2)
            for g in range(COUNTED, NG):
                act.activation(junk_act[0:NQ, g % 2, :], leave_all[0:NQ, :], ACT.Sign, bias=item_less[0:NQ, g:g + 1], scale=-1.0,
                               accum_out=tile_of[0:NQ, g:g + 1]).then_inc(signs_summed, 1)
                if g > COUNTED:
                    act.wait_ge(signs_summed, g - COUNTED)
            for j, (t, g4) in enumerate(order):
                table = (k.local, k.src, k.weight)[t]
                act.wait_ge(turned, j + 1)
                act.copy(table[:, 0:I].rearrange("p (q g) -> p g q", g=NG)[:, 4 * g4:4 * g4 + 4, :],
                         ps_t[j % 2][:, :, 0:NQ]).then_inc(placed, 1)
            act.wait_ge(placed, len(order))


def layer_norm(nc, k, s, load=None, store=None):
    NB, CH = s.NB, s.CH
    NCH = NB // CH
    with phase(nc, k) as (c, sem):
        def sb(name, shape, dt=F32):
            return c.enter_context(nc.sbuf_tensor(k.tag + name, shape, dt))

        stats = sb("ln_stats", [128, 2, CH, 6])
        moments = sb("ln_moments", [128, 2, CH, 2])
        std = sb("ln_std", [128, 2, CH])
        rstd = sb("ln_rstd", [128, 2, CH])
        shift = sb("ln_shift", [128, 2, CH])
        stats_done, var_done, std_done, rstd_done, scale_done, applied = map(
            sem, ["ln_stats_done", "ln_var_done", "ln_std_done", "ln_rstd_done", "ln_scale_done", "ln_applied"])
        stats_turn = sem("ln_stats_turn")
        rows_in = [sem(f"ln_rows_in{i}") for i in range(2)]
        rows_out = [sem(f"ln_rows_out{i}") for i in range(2)]
        block = c.enter_context(nc.Block())

        def live(n):
            return not isinstance(n, int) or n < NCH

        def on_chip(n):
            return k.nodes[0:NP, bass.ds(n * CH, CH), 0:D]

        def in_dram(table, n):
            return table.rearrange("(b p) d -> p b d", p=NP)[:, bass.ds(n * CH, CH), :]

        @block.sync
        def _(sp):
            def step(n, u):
                if load is not None and live(n):
                    if reached(n, 2):
                        sp.wait_ge(stats_done, n - 1)
                    sp.dma_start(on_chip(n), in_dram(load, n)).then_inc(rows_in[u], 16)
                if store is not None and reached(n, 1):
                    sp.wait_ge(applied, n)
                    sp.dma_start(in_dram(store, n - 1), on_chip(n - 1)).then_inc(rows_out[1 - u], 16)

            if load is not None or store is not None:
                pipeline(sp, NCH, 0 if store is None else 1, step, 2)
            if store is not None:
                for out in rows_out:
                    sp.wait_ge(out, 16 * (NCH // 2))

        @block.vector
        def _(dve):
            def step(n, u):
                if live(n):
                    if load is not None:
                        dve.wait_ge(rows_in[u], uses(n, u, 2, 16))
                        dve.sem_inc(stats_turn, 1)
                    rows = on_chip(n)
                    for b in range(CH):
                        last = dve.bn_stats(stats[0:NP, u, b, :], rows[:, b, :])
                    last.then_inc(stats_done, 1)
                if reached(n, 1):
                    v = 1 - u
                    dve.wait_ge(std_done, n)
                    if reached(n, 3):
                        dve.wait_ge(applied, n - 2)
                    dve.reciprocal(rstd[0:NP, v, :], std[0:NP, v, :]).then_inc(rstd_done, 1)
                    dve.wait_ge(rstd_done, n)
                    dve.scalar_tensor_tensor(shift[0:NP, v, :], moments[0:NP, v, :, 0], -1.0, rstd[0:NP, v, :],
                                             ALU.mult, ALU.mult).then_inc(scale_done, 1)
                if live(n):
                    dve.wait_ge(stats_done, n + 1)
                    if reached(n, 2):
                        dve.wait_ge(scale_done, n - 1)
                    dve.sem_inc(stats_turn, 1)
                    for b in range(CH):
                        last = dve.bn_aggr(moments[0:NP, u, b, :], stats[0:NP, u, b, :])
                    last.then_inc(var_done, 1)

            pipeline(dve, NCH, 1, step, 2)

        @block.scalar
        def _(act):
            def step(n, u):
                if live(n):
                    act.wait_ge(var_done, n + 1)
                    if reached(n, 2):
                        act.wait_ge(rstd_done, n - 1)
                    act.activation(std[0:NP, u, :], moments[0:NP, u, :, 1], ACT.Sqrt, bias=k.eps[0:NP, :]).then_inc(std_done, 1)
                if reached(n, 1):
                    v = 1 - u
                    act.wait_ge(scale_done, n)
                    rows = on_chip(n - 1)
                    for b in range(CH):
                        last = act.activation(rows[:, b, :], rows[:, b, :], ACT.Relu, bias=shift[0:NP, v, b:b + 1],
                                              scale=rstd[0:NP, v, b:b + 1])
                    last.then_inc(applied, 1)

            pipeline(act, NCH, 1, step, 2)
            act.wait_ge(applied, NCH)


def load_vec(nc, k, s, a):
    with phase(nc, k) as (c, sem):
        vec_rows = c.enter_context(nc.sbuf_tensor("vec_rows", [128, NP], F32))
        ps = c.enter_context(nc.psum_tensor("ps_vec", [128, 128], F32))
        vec_in, turned, copied = [sem(n) for n in ("vec_in", "vec_turned", "vec_copied")]
        block = c.enter_context(nc.Block())

        @block.sync
        def _(sp):
            sp.dma_start(vec_rows[0:s.NB, :], a.vec.rearrange("(b p) -> b p", p=NP)).then_inc(vec_in, 16)

        @block.tensor
        def _(pe):
            pe.wait_ge(vec_in, 16)
            pe.transpose(ps[0:NP, 0:s.NB], vec_rows[0:s.NB, :], k.ident[0:s.NB, 0:s.NB]).then_inc(turned, 1)

        @block.vector
        def _(dve):
            dve.wait_ge(turned, 1)
            dve.tensor_copy(k.vec[0:NP, :], ps[0:NP, 0:s.NB]).then_inc(copied, 1)
            dve.wait_ge(copied, 1)


def project_nodes(nc, k, s, w, residual):
    NB = s.NB
    with phase(nc, k) as (c, sem):
        def sb(name, shape, dt=F32):
            return c.enter_context(nc.sbuf_tensor(k.tag + name, shape, dt))

        weights = sb("pr_weights", [128, 4 * D])
        bias = sb("pr_bias", [128, 4 * D])
        turned_sb = sb("pr_turned", [128, PR, NP])
        still = sb("pr_still", [128, PR, D])
        kv = sb("pr_kv", [128, PR, KVW])
        skip = sb("pr_skip", [128, PR, D])
        x = sb("pr_x", [128, PR, D])
        ps_t = [c.enter_context(nc.psum_tensor(k.tag + f"pr_ps_t{i}", [128, 512], F32)) for i in range(PR)]
        ps_p = [c.enter_context(nc.psum_tensor(k.tag + f"pr_ps_p{i}", [128, 512], F32)) for i in range(PR)]
        loaded, stilled, turned, copied, projected, added, vec_put, zeroed = map(
            sem, ["pr_loaded", "pr_stilled", "pr_turned_s", "pr_copied", "pr_projected", "pr_added", "pr_vec_put", "pr_zeroed"])
        kv_out = [sem(f"pr_kv_out{i}") for i in range(PR)]
        skip_out = [sem(f"pr_skip_out{i}") for i in range(PR)]
        x_in = [sem(f"pr_x_in{i}") for i in range(PR)]
        x_added = sem("pr_x_added")
        block = c.enter_context(nc.Block())

        def steps(engine, step):
            for b in range(2 * PR):
                step(b, b % PR)
            with engine.Fori(2, NB // PR) as it:
                for u in range(PR):
                    step(it * PR + u, u)

        def live(b):
            return not isinstance(b, int) or b < NB

        @block.sync
        def _(sp):
            for i in range(4):
                sp.dma_start(weights[:, D * i:D * i + D], w.weights[i]).then_inc(loaded, 16)
                sp.dma_start(bias[:, D * i:D * i + D], w.biases[i].rearrange("(o d) -> o d", o=1).broadcast_to([128, D])).then_inc(loaded, 16)

            def step(b, u):
                if reached(b, 2):
                    store(b - 2, (u - 2) % PR)

            def store(b, u):
                sp.wait_ge(added, b + 1)
                sp.wait_ge(vec_put, b + 1)
                if residual is not None:
                    sp.wait_ge(x_added, b + 1)
                sp.dma_start(k.d_kv.rearrange("(b p) d -> p b d", p=NP)[:, bass.ds(b, 1), :].rearrange("p a d -> p (a d)"),
                             kv[0:NP, u, :]).then_inc(kv_out[u], 16)
                sp.dma_start(k.d_skip.rearrange("(b p) d -> p b d", p=NP)[:, bass.ds(b, 1), :].rearrange("p a d -> p (a d)"),
                             skip[0:NP, u, :]).then_inc(skip_out[u], 16)

            steps(sp, step)
            for b in (NB - 2, NB - 1):
                store(b, b % PR)
            for u in range(PR):
                sp.wait_ge(kv_out[u], 16 * (NB // PR))
                sp.wait_ge(skip_out[u], 16 * (NB // PR))

        @block.tensor
        def _(pe):
            pe.wait_ge(loaded, 128)

            def step(b, u):
                if live(b):
                    pe.wait_ge(stilled, b + 1)
                    if reached(b, PR):
                        pe.wait_ge(copied, b - PR + 1)
                    pe.transpose(ps_t[u][:, 0:NP], still[0:NP, u, :],
                                 k.ident[0:NP, 0:NP]).then_inc(turned, 1)
                if reached(b, 1):
                    m, v = b - 1, (u - 1) % PR
                    pe.wait_ge(copied, m + 1)
                    if reached(m, PR):
                        pe.wait_ge(added, m - PR + 1)
                    pe.matmul(ps_p[v][0:NP, :], turned_sb[:, v, :], weights[:, :], start=True, stop=True).then_inc(projected, 1)

            steps(pe, step)
            step(NB, NB % PR)

        @block.gpsimd
        def _(pool):
            def step(b, u):
                if reached(b, PR):
                    pool.wait_ge(turned, b - PR + 1)
                pool.tensor_copy(still[0:NP, u, :], k.nodes[0:NP, bass.ds(b, 1), 0:D].rearrange("p a d -> p (a d)")).then_inc(stilled, 1)
                if residual is not None and reached(b, 3):
                    add_x(b - 3, (u - 3) % PR)

            def add_x(b, u):
                pool.wait_ge(added, b + 1)
                pool.wait_ge(x_in[u], uses(b, u, PR, 16))
                pool.tensor_tensor(skip[0:NP, u, :], skip[0:NP, u, :], x[0:NP, u, :], ALU.add).then_inc(x_added, 1)

            steps(pool, step)
            if residual is not None:
                for b in range(NB - 3, NB):
                    add_x(b, b % PR)

        @block.scalar
        def _(act):
            def step(b, u):
                if residual is not None:
                    if reached(b, PR):
                        act.wait_ge(x_added, b - PR + 1)
                    act.dma_start(x[0:NP, u, :], residual[bass.ds(b * NP, NP), :]).then_inc(x_in[u], 16)
                act.wait_ge(turned, b + 1)
                if reached(b, PR):
                    act.wait_ge(projected, b - PR + 1)
                act.copy(turned_sb[:, u, :], ps_t[u][:, 0:NP]).then_inc(copied, 1)
                if reached(b, PR):
                    act.wait_ge(kv_out[u], uses(b - PR, u, PR, 16))
                act.copy(kv[0:NP, u, 2 * D:2 * D + 1], k.vec[0:NP, bass.ds(b, 1)]).then_inc(vec_put, 1)

            act.wait_ge(zeroed, 1)
            steps(act, step)

        @block.vector
        def _(dve):
            dve.memset(kv[:, :, :], 0.0)
            dve.memset(k.query[:, NB, :], 0.0).then_inc(zeroed, 1)
            dve.wait_ge(loaded, 128)
            dve.wait_ge(zeroed, 1)

            def step(b, u):
                dve.wait_ge(projected, b + 1)
                if reached(b, PR):
                    dve.wait_ge(kv_out[u], uses(b - PR, u, PR, 16))
                    dve.wait_ge(skip_out[u], uses(b - PR, u, PR, 16))
                dve.tensor_tensor(k.query[0:NP, bass.ds(b, 1), 0:D].rearrange("p a d -> p (a d)"), ps_p[u][0:NP, 0:D], bias[0:NP, 0:D], ALU.add)
                dve.tensor_tensor(kv[0:NP, u, 0:2 * D], ps_p[u][0:NP, D:3 * D], bias[0:NP, D:3 * D], ALU.add)
                dve.tensor_tensor(skip[0:NP, u, :], ps_p[u][0:NP, 3 * D:4 * D], bias[0:NP, 3 * D:4 * D],
                                  ALU.add).then_inc(added, 1)

            steps(dve, step)


def edge_scores(nc, k, s, a, w, first):
    NGR = s.G
    lag = 3 if first else 2
    with phase(nc, k) as (c, sem):
        def sb(name, shape, dt=F32):
            return c.enter_context(nc.sbuf_tensor(k.tag + name, shape, dt))

        def psums(name, shape, dt=F32):
            return [c.enter_context(nc.psum_tensor(k.tag + f"{name}{i}", shape, dt)) for i in range(2)]

        taken = [0]

        def carve(ring, width):
            part = k.big2[:, taken[0]:taken[0] + ring * GR * width]
            taken[0] += ring * GR * width
            return part.rearrange("p (r i d) -> p r i d", r=ring, i=GR)

        kv = carve(UNROLL, KVW)
        attr_t = carve(RING, EP)
        both = carve(RING, D)
        idx = sb("es_idx", [128, UNROLL, GR], I32)
        onehot = sb("es_onehot", [128, 2, GR, 128], BF16)
        onehot_t = sb("es_onehot_t", [128, RING, GR, EP])
        key_e = sb("es_key", [128, 2, GR, D])
        prod = sb("es_prod", [128, 2, GR, D])
        we = sb("es_we", [128, D])
        ps_oh = psums("es_ps_oh", [128, GR, 256], BF16)
        ps_at = psums("es_ps_at", [128, GR, EP])
        ps_e = psums("es_ps_e", [128, GR, D])
        ps_q = psums("es_ps_q", [128, GR, D])
        if first:
            attr = sb("es_attr", [128, RING, GR, D])
            rel = sb("es_rel", [128, 2, GR])
            arg = sb("es_arg", [128, 2, GR, MSG])
            part = sb("es_part", [128, 2, GR, MSG])
            wt = sb("es_wt", [128, MSG])
            bt = sb("es_bt", [128, MSG])

        loaded = sem("es_loaded")
        idx_put, gather_turn = sem("es_idx_put"), sem("es_gather_turn")
        gathered = [sem(f"es_gathered{i}") for i in range(UNROLL)]
        onehot_made, onehot_turned, onehot_copied = sem("es_oh_made"), sem("es_oh_turned"), sem("es_oh_copied")
        turns_ready = sem("es_turns_ready")
        rel_made, product_made, arg_made = sem("es_rel_made"), sem("es_product_made"), sem("es_arg_made")
        whole_made, angle_made, code_made = sem("es_whole_made"), sem("es_angle_made"), sem("es_code_made")
        attr_turned, attr_copied = sem("es_attr_turned"), sem("es_attr_copied")
        e_done, q_done, key_made = sem("es_e_done"), sem("es_q_done"), sem("es_key_made")
        value_made, prod_made, score_made = sem("es_value_made"), sem("es_prod_made"), sem("es_score_made")
        message_in = [sem(f"es_message_in{i}") for i in range(RING)]
        attr_in = [sem(f"es_attr_in{i}") for i in range(RING)]
        attr_out = [sem(f"es_attr_out{i}") for i in range(RING)]
        value_out = [sem(f"es_value_out{i}") for i in range(RING)]
        block = c.enter_context(nc.Block())

        def live(n):
            return not isinstance(n, int) or n < NGR

        def ended(n, back):
            return reached(n, back) and live(n - back)

        @block.gpsimd
        def _(pool):
            def step(n, u):
                pool.wait_ge(idx_put, n + 1)
                if reached(n, UNROLL):
                    pool.wait_ge(value_made, n - UNROLL + 1)
                pool.sem_inc(gather_turn, 1)
                for i in range(GR):
                    pool.indirect_dma_start(kv[:, u, i, :], None, k.d_kv,
                                            bass.IndirectOffsetOnAxis(ap=idx[:, u, i:i + 1], axis=0)).then_inc(gathered[u], 16)

            pipeline(pool, NGR, 0, step)

        @block.sync
        def _(sp):
            sp.dma_start(we[:, :], w.edge).then_inc(loaded, 16)
            if first:
                sp.dma_start(wt[:, :], a.wt.broadcast_to([128, MSG])).then_inc(loaded, 16)
                sp.dma_start(bt[:, :], a.bt.rearrange("(o d) -> o d", o=1).broadcast_to([128, MSG])).then_inc(loaded, 16)

            def step(n, u):
                if live(n):
                    v = u % RING
                    if first:
                        if reached(n, RING):
                            sp.wait_ge(attr_turned, n - RING + 1)
                        _, tiles = nc.values_load_multi_w_load_instructions(
                            k.tile_row[0:1, bass.ds(n * GR, GR)], engines=[mybir.EngineType.SP], min_val=0, max_val=s.T - 1,
                            skip_runtime_bounds_check_because="item_tables holds the tiles in 0 .. T - 1")
                        for i in range(GR):
                            sp.dma_start(attr[:, v, i, MSG:D],
                                         a.message[bass.ds(tiles[i], 1), :, :].rearrange("a p d -> (a p) d")).then_inc(message_in[v], 16)
                    else:
                        if reached(n, RING):
                            sp.wait_ge(e_done, n - RING + 1)
                        sp.dma_start(attr_t[:, v, :, :].rearrange("p a e -> p (a e)"),
                                     k.d_attr[bass.ds(n, 1), :, :].rearrange("a p d -> (a p) d")).then_inc(attr_in[v], 16)
                if ended(n, lag + 1):
                    m, v = n - lag - 1, (u - lag - 1) % RING
                    if first:
                        sp.wait_ge(attr_copied, m + 1)
                        sp.dma_start(k.d_attr[bass.ds(m, 1), :, :].rearrange("a p d -> (a p) d"),
                                     attr_t[:, v, :, :].rearrange("p a e -> p (a e)")).then_inc(attr_out[v], 16)
                    sp.wait_ge(value_made, m + 1)
                    sp.dma_start(k.d_value[bass.ds(m, 1), :, :].rearrange("a p d -> (a p) d"),
                                 both[:, v, :, :].rearrange("p a d -> p (a d)")).then_inc(value_out[v], 16)

            pipeline(sp, NGR, lag + 1, step)
            for v in range(RING):
                if first:
                    sp.wait_ge(attr_out[v], 16 * (NGR // RING))
                sp.wait_ge(value_out[v], 16 * (NGR // RING))

        @block.vector
        def _(dve):
            dve.wait_ge(loaded, 48 if first else 16)
            if first:
                dve.tensor_scalar(wt[:, :], wt[:, :], INV_TWO_PI, None, ALU.mult).then_inc(turns_ready, 1)
                dve.tensor_scalar(bt[:, :], bt[:, :], INV_TWO_PI, 0.25, ALU.mult, ALU.add).then_inc(turns_ready, 1)
                dve.wait_ge(turns_ready, 2)

            def step(n, u):
                h = u % 2
                if live(n):
                    if reached(n, 2):
                        dve.wait_ge(onehot_turned, n - 1)
                    dve.tensor_tensor(onehot[:, h, :, 0:NP], k.node_iota_b[:, :].unsqueeze(1).broadcast_to([128, GR, NP]),
                                      k.local_b[:, bass.ds(n * GR, GR)].unsqueeze(2).broadcast_to([128, GR, NP]),
                                      ALU.is_equal).then_inc(onehot_made, 1)
                    if first:
                        dve.wait_ge(gathered[u], uses(n, u, UNROLL, 16 * GR))
                        if reached(n, 2):
                            dve.wait_ge(product_made, n - 1)
                        dve.tensor_tensor(rel[:, h, :], kv[:, u, :, 2 * D], k.weight[:, bass.ds(n * GR, GR)],
                                          ALU.subtract).then_inc(rel_made, 1)
                m, v, g = n - lag, (u - lag) % UNROLL, (u - lag) % 2
                r, o = n - 1, 1 - h
                score, reduce = ended(n, lag), first and ended(n, 1)
                if score:
                    if not first:
                        dve.wait_ge(gathered[v], uses(m, v, UNROLL, 16 * GR))
                    dve.wait_ge(e_done, m + 1)
                    dve.tensor_tensor(key_e[:, g, :, :], kv[:, v, :, 0:D], ps_e[g][:, :, :], ALU.add).then_inc(key_made, 1)
                if reduce:
                    dve.wait_ge(arg_made, r + 1)
                    dve.tensor_scalar(part[:, o, :, :], arg[:, o, :, :], ROUND, ROUND, ALU.add, ALU.subtract).then_inc(whole_made, 1)
                if score:
                    if reached(m, RING):
                        dve.wait_ge(value_out[v % RING], uses(m - RING, v, RING, 16))
                    dve.tensor_tensor(both[:, v % RING, :, :], kv[:, v, :, D:2 * D], ps_e[g][:, :, :], ALU.add).then_inc(value_made, 1)
                if reduce:
                    dve.wait_ge(whole_made, r + 1)
                    dve.tensor_tensor(arg[:, o, :, :], arg[:, o, :, :], part[:, o, :, :], ALU.subtract).then_inc(angle_made, 1)
                if score:
                    dve.wait_ge(q_done, m + 1)
                    dve.wait_ge(key_made, m + 1)
                    dve.tensor_tensor(prod[:, g, :, :], key_e[:, g, :, :], ps_q[g][:, :, :], ALU.mult).then_inc(prod_made, 1)
                if first and live(n):
                    dve.wait_ge(product_made, n + 1)
                    if reached(n, 2):
                        dve.wait_ge(code_made, n - 1)
                    dve.tensor_tensor(arg[:, h, :, :], part[:, h, :, :],
                                      bt[:, :].unsqueeze(1).broadcast_to([128, GR, MSG]), ALU.add).then_inc(arg_made, 1)
                if score:
                    dve.wait_ge(prod_made, m + 1)
                    dve.tensor_reduce(k.score[:, bass.ds(m * (GR * HEADS), GR * HEADS)],
                                      prod[:, g, :, :].rearrange("p i (h c) -> p (i h) c", c=C), AX.X, ALU.add).then_inc(score_made, 1)

            pipeline(dve, NGR, lag, step)
            dve.wait_ge(score_made, NGR)

        @block.scalar
        def _(act):
            if first:
                act.wait_ge(turns_ready, 2)
            act.copy(idx[:, :, :], k.src[:, 0:UNROLL * GR].rearrange("p (r i) -> p r i", i=GR)).then_inc(idx_put, UNROLL)

            def step(n, u):
                h = u % 2
                if first and ended(n, 2):
                    m, v, g = n - 2, (u - 2) % RING, h
                    act.wait_ge(attr_turned, m + 1)
                    if reached(m, RING):
                        act.wait_ge(attr_out[v], uses(m - RING, v, RING, 16))
                        act.wait_ge(e_done, m - RING + 1)
                    act.copy(attr_t[:, v, :, :], ps_at[g][:, :, :]).then_inc(attr_copied, 1)
                if first and live(n):
                    act.wait_ge(rel_made, n + 1)
                    if reached(n, 2):
                        act.wait_ge(angle_made, n - 1)
                    for i in range(GR):
                        last = act.activation(part[:, h, i, :], wt[:, :], ACT.Identity, bias=k.zero[:, :], scale=rel[:, h, i:i + 1])
                    last.then_inc(product_made, 1)
                if live(n):
                    act.wait_ge(onehot_turned, n + 1)
                    if reached(n, RING):
                        act.wait_ge(q_done, n - RING + 1)
                    act.copy(onehot_t[0:NP, u % RING, :, :], ps_oh[h][0:NP, :, 0:EP]).then_inc(onehot_copied, 1)
                if first and ended(n, 1):
                    m, v, g = n - 1, (u - 1) % RING, 1 - h
                    act.wait_ge(angle_made, m + 1)
                    if reached(m, RING):
                        act.wait_ge(attr_turned, m - RING + 1)
                    act.activation(attr[:, v, :, 0:MSG], arg[:, g, :, :], ACT.Sin, bias=k.zero[:, :], scale=TWO_PI).then_inc(code_made, 1)
                if live(n):
                    act.wait_ge(gathered[u], uses(n, u, UNROLL, 16 * GR))
                    act.copy(idx[:, u, :], k.src[:, bass.ds((n + UNROLL) * GR, GR)]).then_inc(idx_put, 1)

            pipeline(act, NGR, 2 if first else 0, step)

        @block.tensor
        def _(pe):
            pe.wait_ge(loaded, 48 if first else 16)

            def step(n, u):
                h = u % 2
                if live(n):
                    pe.wait_ge(onehot_made, n + 1)
                    if reached(n, 2):
                        pe.wait_ge(onehot_copied, n - 1)
                    for i in range(GR):
                        last = pe.transpose(ps_oh[h][0:NP, i, 0:EP], onehot[:, h, i, 0:NP], k.ident_b[:, :])
                    last.then_inc(onehot_turned, 1)
                if ended(n, lag - 1):
                    m, v, g = n - lag + 1, (u - lag + 1) % RING, (u - lag + 1) % 2
                    if first:
                        pe.wait_ge(attr_copied, m + 1)
                    else:
                        pe.wait_ge(attr_in[v], uses(m, v, RING, 16))
                    if reached(m, 2):
                        pe.wait_ge(value_made, m - 1)
                        pe.wait_ge(key_made, m - 1)
                    for i in range(GR):
                        last = pe.matmul(ps_e[g][:, i, :], attr_t[:, v, i, :], we[:, :], start=True, stop=True)
                    last.then_inc(e_done, 1)
                    _, blocks = nc.values_load_multi_w_load_instructions(
                        k.block_row[0:1, bass.ds(m * GR, GR)], engines=[mybir.EngineType.PE], min_val=0, max_val=s.NB,
                        skip_runtime_bounds_check_because="item_tables holds the blocks in 0 .. NB")
                    pe.wait_ge(onehot_copied, m + 1)
                    if reached(m, 2):
                        pe.wait_ge(prod_made, m - 1)
                    for i in range(GR):
                        last = pe.matmul(ps_q[g][:, i, :], onehot_t[0:NP, v, i, :],
                                         k.query[0:NP, bass.ds(blocks[i], 1), 0:D].rearrange("p a d -> p (a d)"),
                                         start=True, stop=True)
                    last.then_inc(q_done, 1)
                if first and ended(n, 1):
                    m, v, g = n - 1, (u - 1) % RING, 1 - h
                    pe.wait_ge(message_in[v], uses(m, v, RING, 16 * GR))
                    pe.wait_ge(code_made, m + 1)
                    if reached(m, 2):
                        pe.wait_ge(attr_copied, m - 1)
                    for i in range(GR):
                        last = pe.transpose(ps_at[g][:, i, :], attr[:, v, i, :], k.ident[:, :])
                    last.then_inc(attr_turned, 1)

            pipeline(pe, NGR, lag - 1, step)


def softmax_weights(nc, k, s):
    NQ, SL = s.NQ, NG * EP
    with phase(nc, k) as (c, sem):
        def sb(name, shape, dt=F32):
            return c.enter_context(nc.sbuf_tensor(k.tag + name, shape, dt))

        alpha = k.big1[:, 0:HEADS * SL].rearrange("p (h s) -> p h s", h=HEADS)
        peak = k.big2[:, 0:HEADS * SL].rearrange("p (h s) -> p h s", h=HEADS)
        cut = k.big1[:, HEADS * SL:HEADS * SL + SL + 1]
        other = k.big2[:, HEADS * SL:HEADS * SL + 2 * SL].rearrange("p (a s) -> p a s", a=2)
        edge = sb("sm_edge", [128, 10])
        diag = sb("sm_diag", [128, 10, 128])
        rows = sb("sm_rows", [128, 10, 128])
        apart = sb("sm_apart", [128, 2, 2, 128])
        cand = sb("sm_cand", [128, 2, 128])
        joined = sb("sm_joined", [128, 2, HEADS])
        ps_f = [c.enter_context(nc.psum_tensor(k.tag + f"sm_ps_f{i}", [128, HEADS, 128], F32)) for i in range(2)]
        ps_r = [c.enter_context(nc.psum_tensor(k.tag + f"sm_ps_r{i}", [128, 4, 128], F32)) for i in range(3)]
        turned, put, own, peaks, ran, seam, seam_rows, diff, expd, back, done = map(
            sem, ["sm_turned", "sm_put", "sm_own", "sm_peaks", "sm_ran", "sm_seam", "sm_seam_rows", "sm_diff", "sm_expd",
                  "sm_back", "sm_done"])
        block = c.enter_context(nc.Block())

        order = [(h, g) for h in range(HEADS) for g in range(0, NG, 4)]

        @block.tensor
        def _(pe):
            for j, (h, g) in enumerate(order):
                at_least(pe, put, j - 1)
                for i in range(4):
                    v = k.score[:, :].rearrange("p (q g h) -> p g h q", g=NG, h=HEADS)[:, g + i, h, :]
                    last = pe.transpose(ps_f[j % 2][0:NQ, i, :], v, k.ident[:, :])
                last.then_inc(turned, 1)
            pe.wait_ge(seam, 1)
            for i in range(3):
                w = min(4, 10 - 4 * i)
                last = pe.matmul(ps_r[i][0:NQ, 0:w, :], k.ones[0:NQ, 0:NQ], diag[0:NQ, 4 * i:4 * i + w, :], start=True, stop=True)
            last.then_inc(seam_rows, 1)
            for j, (h, g) in enumerate(order):
                if g == 0:
                    pe.wait_ge(expd, h + 1)
                at_least(pe, back, j - 1)
                for i in range(4):
                    last = pe.transpose(ps_f[j % 2][:, i, 0:NQ], peak[0:NQ, h, EP * (g + i):EP * (g + i + 1)], k.ident[0:NQ, 0:NQ])
                last.then_inc(done, 1)

        @block.scalar
        def _(act):
            for j, (h, g) in enumerate(order):
                act.wait_ge(turned, j + 1)
                act.copy(alpha[0:NQ, h, EP * g:EP * (g + 4)].rearrange("p (g e) -> p g e", g=4), ps_f[j % 2][0:NQ, :, :]).then_inc(put, 1)

            def place(j, h, g):
                act.wait_ge(done, j + 1)
                act.copy(k.score[:, :].rearrange("p (q g h) -> p g h q", g=NG, h=HEADS)[:, g:g + 4, h, :],
                         ps_f[j % 2][:, :, 0:NQ]).then_inc(back, 1)

            for h in range(HEADS):
                act.wait_ge(diff, h + 1)
                act.activation(peak[0:NQ, h, :], peak[0:NQ, h, :], ACT.Exp, scale=float(C) ** -0.5).then_inc(expd, 1)
                for j in range(NG // 4 * h, NG // 4 * (h + 1)):
                    place(j, *order[j])
            act.wait_ge(back, len(order))

        @block.vector
        def _(dve):
            ch = Chain(dve, own)
            dve.memset(cut[0:NQ, 0:1], -BIG)
            dve.memset(cut[0:NQ, SL:SL + 1], -BIG)
            dve.memset(diag[:, :, :], 0.0)
            ch.link(dve.scalar_tensor_tensor(cut[0:NQ, 1:SL], k.key[0:NQ, 1:SL], 0.0, k.key[0:NQ, 0:SL - 1],
                                             ALU.add, ALU.not_equal))
            ch.link(dve.tensor_scalar(cut[0:NQ, 1:SL], cut[0:NQ, 1:SL], -BIG, None, ALU.mult))
            for h in range(HEADS):
                dve.wait_ge(put, NG // 4 * (h + 1))
                dve.tensor_tensor_scan(peak[0:NQ, h, :], cut[0:NQ, 0:SL], alpha[0:NQ, h, :], 0.0, ALU.add, ALU.max).then_inc(peaks, 1)
            for h in range(HEADS):
                dve.wait_ge(peaks, h + 1)
                last = dve.tensor_tensor_scan(peak[0:NQ, h, ::-1], cut[0:NQ, SL:0:-1], peak[0:NQ, h, ::-1], 0.0, ALU.add, ALU.max)
            ch.link(last)
            for end, slot in ((0, 0), (1, SL - 1)):
                dve.tensor_copy(edge[0:NQ, end:end + 1], k.key[0:NQ, slot:slot + 1])
                last = dve.tensor_copy(edge[0:NQ, 2 + HEADS * end:2 + HEADS * end + HEADS], peak[0:NQ, :, slot])
            ch.link(last)
            dve.tensor_tensor(diag[0:NQ, :, 0:NQ], edge[0:NQ, :].unsqueeze(2).broadcast_to([NQ, 10, NQ]),
                              k.ident[0:NQ, 0:NQ].unsqueeze(1).broadcast_to([NQ, 10, NQ]), ALU.mult).then_inc(seam, 1)
            for end in range(2):
                slot = (0, SL - 1)[end]
                last = dve.tensor_scalar(other[0:NQ, end, :], k.key[0:NQ, :], k.key[0:NQ, slot:slot + 1], -BIG,
                                         ALU.not_equal, ALU.mult)
            ch.link(last)
            dve.wait_ge(seam_rows, 1)
            for i in range(3):
                w = min(4, 10 - 4 * i)
                last = dve.tensor_copy(rows[0:NQ, 4 * i:4 * i + w, :], ps_r[i][0:NQ, 0:w, :])
            ch.link(last)
            for end in range(2):
                last = dve.tensor_scalar(apart[0:NQ, end, :, 0:NQ], rows[0:NQ, 0:2, 0:NQ], edge[0:NQ, end:end + 1], -BIG,
                                         ALU.not_equal, ALU.mult)
            ch.link(last)
            for end in range(2):
                for h in range(HEADS):
                    ch.link(dve.tensor_tensor(cand[0:NQ, :, 0:NQ], rows[0:NQ, 2 + h:7 + h:HEADS, 0:NQ], apart[0:NQ, end, :, 0:NQ], ALU.add))
                    ch.link(dve.tensor_reduce(joined[0:NQ, end, h:h + 1], cand[0:NQ, :, 0:NQ], AX.XY, ALU.max))
            for h in range(HEADS):
                for end in range(2):
                    ch.link(dve.scalar_tensor_tensor(peak[0:NQ, h, :], other[0:NQ, end, :], joined[0:NQ, end, h:h + 1],
                                                     peak[0:NQ, h, :], ALU.add, ALU.max))
                dve.tensor_tensor(peak[0:NQ, h, :], alpha[0:NQ, h, :], peak[0:NQ, h, :], ALU.subtract).then_inc(diff, 1)


def add_up(nc, k, s, weighted):
    NGR = s.G
    W = ACW if weighted else D + 1
    SPLIT = GR // 2
    ring = RING if weighted else UNROLL
    with phase(nc, k) as (c, sem):
        def sb(name, shape, dt=F32):
            return c.enter_context(nc.sbuf_tensor(k.tag + name, shape, dt))

        rows = sb("au_rows", [128, ring, GR, ACW])
        onehot = sb("au_onehot", [128, RING, GR, 128])
        apart = sb("au_apart", [128, 2, GR, 128])
        if weighted:
            value = sb("au_value", [128, ring, GR, D])
        else:
            idx = sb("au_idx", [128, UNROLL, GR], I32)
        ps = [[c.enter_context(nc.psum_tensor(k.tag + f"au_ps{i}{j}", [128, 2, 256], F32)) for j in range(2)] for i in range(4)]
        arrived = [sem(f"au_arrived{i}") for i in range(ring)]
        ones_put, zeroed, idx_put, gather_turn = sem("au_ones_put"), sem("au_zeroed"), sem("au_idx_put"), sem("au_gather_turn")
        apart_made, onehot_act = sem("au_apart_made"), sem("au_onehot_act")
        onehot_made, scaled, weight_put = sem("au_onehot_made"), sem("au_scaled"), sem("au_weight_put")
        summed = sem("au_summed")
        added = [sem(f"au_added{i}") for i in range(GR)]
        block = c.enter_context(nc.Block())

        def live(n):
            return not isinstance(n, int) or n < NGR

        @block.sync
        def _(sp):
            if weighted:
                def step(n, u):
                    if reached(n, ring):
                        sp.wait_ge(scaled, n - ring + 1)
                    sp.dma_start(value[:, u % ring, :, :].rearrange("p a d -> p (a d)"),
                                 k.d_value[bass.ds(n, 1), :, :].rearrange("a p d -> (a p) d")).then_inc(arrived[u % ring], 16)

                pipeline(sp, NGR, 0, step)

        @block.gpsimd
        def _(pool):
            if not weighted:
                pool.memset(rows[:, :, :, D:ACW], 1.0).then_inc(ones_put, 1)

            def step(n, u):
                if weighted:
                    pool.wait_ge(arrived[u % ring], uses(n, u, ring, 16))
                    if reached(n, ring):
                        pool.wait_ge(summed, n - ring + 1)
                    pool.tensor_tensor(rows[:, u % ring, :, 0:D].rearrange("p i (h c) -> p i h c", c=C),
                                       value[:, u % ring, :, :].rearrange("p i (h c) -> p i h c", c=C),
                                       k.score[:, bass.ds(n * (GR * HEADS), GR * HEADS)].rearrange("p (i h) -> p i h", h=HEADS)
                                       .unsqueeze(3).broadcast_to([128, GR, HEADS, C]), ALU.mult).then_inc(scaled, 1)
                else:
                    pool.wait_ge(idx_put, n + 1)
                    if reached(n, ring):
                        pool.wait_ge(summed, n - ring + 1)
                    pool.sem_inc(gather_turn, 1)
                    for i in range(GR):
                        pool.indirect_dma_start(rows[:, u, i, 0:D], None, k.d_node,
                                                bass.IndirectOffsetOnAxis(ap=idx[:, u, i:i + 1], axis=0)).then_inc(arrived[u], 16)

            pipeline(pool, NGR, 0, step)

        @block.scalar
        def _(act):
            def onehots(n, u):
                h = u % 2
                if reached(n, 2):
                    act.wait_ge(onehot_act, n - 1)
                for i in range(SPLIT, GR):
                    last = act.activation(apart[:, h, i, 0:NP], k.node_iota[:, :], ACT.Abs,
                                          bias=k.local[:, bass.ds(n * GR + i, 1)], scale=-1.0)
                last.then_inc(apart_made, 1)
                if reached(n, RING):
                    act.wait_ge(summed, n - RING + 1)
                act.wait_ge(apart_made, n + 1)
                act.activation(onehot[:, u % RING, SPLIT:GR, 0:NP], apart[:, h, SPLIT:GR, 0:NP], ACT.Relu,
                               bias=k.ones[:, 0:1], scale=-1.0).then_inc(onehot_act, 1)

            half = (s.NB + 1) * ACW // 2
            if weighted:
                for big in (k.big1, k.big2):
                    act.activation(big[:, half:2 * half], k.zero[:, 0:1].broadcast_to([128, half]), ACT.Copy).then_inc(zeroed, 1)

                def step(n, u):
                    if reached(n, ring):
                        act.wait_ge(summed, n - ring + 1)
                    act.copy(rows[:, u % ring, :, D:ACW],
                             k.score[:, bass.ds(n * (GR * HEADS), GR * HEADS)].rearrange("p (i h) -> p i h", h=HEADS)).then_inc(weight_put, 1)
                    onehots(n, u)

                pipeline(act, NGR, 0, step)
            else:
                act.copy(idx[:, :, :], k.src[:, 0:UNROLL * GR].rearrange("p (r i) -> p r i", i=GR)).then_inc(idx_put, UNROLL)
                act.activation(k.big_acc(weighted)[:, half:2 * half], k.zero[:, 0:1].broadcast_to([128, half]), ACT.Copy).then_inc(zeroed, 1)

                def step(n, u):
                    onehots(n, u)
                    act.wait_ge(arrived[u], uses(n, u, ring, 16 * GR))
                    act.copy(idx[:, u, :], k.src[:, bass.ds((n + UNROLL) * GR, GR)]).then_inc(idx_put, 1)

                pipeline(act, NGR, 0, step)

        @block.vector
        def _(dve):
            half = (s.NB + 1) * ACW // 2
            dve.memset(k.big_acc(weighted)[:, 0:half], 0.0).then_inc(zeroed, 1)
            if weighted:
                dve.memset(k.big1[:, 0:half], 0.0).then_inc(zeroed, 1)
            accs = (k.nodes, k.query) if weighted else (k.acc(weighted),)
            dve.wait_ge(zeroed, 2 * len(accs))

            found = [None]

            def step(n, u):
                if u % 2 == 0 and live(n):
                    if reached(n, RING):
                        dve.wait_ge(summed, n - RING + 2)
                    dve.tensor_tensor(onehot[:, u % RING:u % RING + 2, 0:SPLIT, 0:NP],
                                      k.node_iota[:, :].unsqueeze(1).unsqueeze(1).broadcast_to([128, 2, SPLIT, NP]),
                                      k.local[:, bass.ds(n * GR, 2 * GR)].rearrange("p (g i) -> p g i", i=GR)[:, :, 0:SPLIT]
                                      .unsqueeze(3).broadcast_to([128, 2, SPLIT, NP]), ALU.is_equal).then_inc(onehot_made, 2)
                if reached(n, 2):
                    m, g = n - 2, (u - 2) % 4
                    if u % 2 == 0:
                        _, found[0] = nc.values_load_multi_w_load_instructions(
                            k.block_row[0:1, bass.ds(m * GR, 2 * GR)], engines=[mybir.EngineType.DVE], min_val=0, max_val=s.NB,
                            skip_runtime_bounds_check_because="item_tables holds the blocks in 0 .. NB")
                    dve.wait_ge(summed, m + 1)
                    for i in range(GR):
                        row = accs[i % len(accs)][0:NP, bass.ds(found[0][GR * (u % 2) + i], 1), 0:W].rearrange("p a d -> p (a d)")
                        before = i - len(accs)
                        if before >= 0:
                            dve.wait_ge(added[before], m + 1)
                        else:
                            at_least(dve, added[before + GR], m)
                        dve.tensor_tensor(row, row, ps[g][i // 2][0:NP, i % 2, 0:W], ALU.add).then_inc(added[i], 1)

            pipeline(dve, NGR, 2, step)
            for i in range(GR):
                dve.wait_ge(added[i], NGR)

        @block.tensor
        def _(pe):
            if not weighted:
                pe.wait_ge(ones_put, 1)

            def step(n, u):
                pe.wait_ge(onehot_made, n + 1)
                pe.wait_ge(onehot_act, n + 1)
                if weighted:
                    pe.wait_ge(scaled, n + 1)
                    pe.wait_ge(weight_put, n + 1)
                else:
                    pe.wait_ge(arrived[u], uses(n, u, ring, 16 * GR))
                if reached(n, 4):
                    for i in range(GR - (2 if weighted else 1), GR):
                        pe.wait_ge(added[i], n - 3)
                for i in range(GR):
                    last = pe.matmul(ps[u % 4][i // 2][0:NP, i % 2, 0:W], onehot[:, u % RING, i, 0:NP], rows[:, u % ring, i, 0:W],
                                     start=True, stop=True)
                last.then_inc(summed, 1)

            pipeline(pe, NGR, 0, step)


def finish_conv(nc, k, s, store=None):
    NB, CH = s.NB, s.CH
    NCH = NB // CH
    with phase(nc, k) as (c, sem):
        def sb(name, shape, dt=F32):
            return c.enter_context(nc.sbuf_tensor(k.tag + name, shape, dt))

        share = sb("fc_share", [128, NB, HEADS])
        skip = sb("fc_skip", [128, 2, CH, D])
        own, summed, normed, final = map(sem, ["fc_own", "fc_summed", "fc_normed", "fc_final"])
        skip_in = [sem(f"fc_skip_in{i}") for i in range(2)]
        rows_out = [sem(f"fc_rows_out{i}") for i in range(2)]
        block = c.enter_context(nc.Block())

        def live(n):
            return not isinstance(n, int) or n < NCH

        def on_chip(table, n):
            return table[0:NP, bass.ds(n * CH, CH), 0:D]

        def in_dram(table, n):
            return table.rearrange("(b p) d -> p b d", p=NP)[:, bass.ds(n * CH, CH), :]

        @block.sync
        def _(sp):
            def step(n, u):
                if live(n):
                    if reached(n, 2):
                        sp.wait_ge(final, n - 1)
                    sp.dma_start(skip[0:NP, u, :, :], in_dram(k.d_skip, n)).then_inc(skip_in[u], 16)
                if store is not None and reached(n, 2):
                    sp.wait_ge(final, n - 1)
                    sp.dma_start(in_dram(store, n - 2), on_chip(k.nodes, n - 2)).then_inc(rows_out[u], 16)

            pipeline(sp, NCH, 0 if store is None else 2, step, 2)
            if store is not None:
                for out in rows_out:
                    sp.wait_ge(out, 16 * (NCH // 2))

        @block.vector
        def _(dve):
            ch = Chain(dve, own)
            ch.link(dve.tensor_tensor(share[0:NP, :, :], k.nodes[0:NP, 0:NB, D:ACW], k.query[0:NP, 0:NB, D:ACW], ALU.add))
            ch.link(dve.tensor_scalar(share[0:NP, :, :], share[0:NP, :, :], 1e-16, None, ALU.add))
            ch.link(dve.reciprocal(share[0:NP, :, :], share[0:NP, :, :]))

            def step(n, u):
                if live(n):
                    dve.tensor_tensor(on_chip(k.nodes, n), on_chip(k.nodes, n), on_chip(k.query, n), ALU.add).then_inc(summed, 1)
                if reached(n, 1):
                    dve.wait_ge(skip_in[1 - u], uses(n - 1, 1 - u, 2, 16))
                    dve.wait_ge(normed, n)
                    dve.tensor_tensor(on_chip(k.nodes, n - 1), on_chip(k.nodes, n - 1), skip[0:NP, 1 - u, :, :], ALU.add).then_inc(final, 1)
                if live(n):
                    dve.wait_ge(summed, n + 1)
                    rows = on_chip(k.nodes, n).rearrange("p b (h c) -> p b h c", c=C)
                    dve.tensor_tensor(rows, rows, share[0:NP, bass.ds(n * CH, CH), :].unsqueeze(3).broadcast_to([NP, CH, HEADS, C]),
                                      ALU.mult).then_inc(normed, 1)

            pipeline(dve, NCH, 1, step, 2)
            dve.wait_ge(final, NCH)


def finish_mean_layer(nc, k, s, a, layer, layers, out):
    NB = s.NB
    last_layer = layer == layers - 1
    with phase(nc, k) as (c, sem):
        def sb(name, shape, dt=F32):
            return c.enter_context(nc.sbuf_tensor(k.tag + name, shape, dt))

        wl = sb("fm_wl", [128, D])
        wr = sb("fm_wr", [128, D])
        bl = sb("fm_bl", [128, D])
        inv = sb("fm_inv", [128, NB])
        mean = sb("fm_mean", [128, PR, D])
        still = sb("fm_still", [128, PR, D])
        turned_sb = sb("fm_turned", [128, PR, 2, NP])
        raw = sb("fm_raw", [128, PR, D])
        x1 = sb("fm_x1", [128, PR, D])
        res = sb("fm_res", [128, PR, D])
        ps_t = [c.enter_context(nc.psum_tensor(k.tag + f"fm_ps_t{i}", [128, 2, 128], F32)) for i in range(PR)]
        ps_o = [c.enter_context(nc.psum_tensor(k.tag + f"fm_ps_o{i}", [128, D], F32)) for i in range(PR)]
        loaded, own, meaned, stilled, turned, copied, multiplied, biased, made = map(
            sem, ["fm_loaded", "fm_own", "fm_meaned", "fm_stilled", "fm_turned_s", "fm_copied", "fm_multiplied", "fm_biased", "fm_made"])
        x1_in = [sem(f"fm_x1_in{i}") for i in range(PR)]
        stored = [sem(f"fm_stored{i}") for i in range(PR)]
        block = c.enter_context(nc.Block())
        acc = k.acc(False)

        def steps(engine, lag, step):
            for b in range(2 * PR):
                step(b, b % PR)
            with engine.Fori(2, NB // PR) as it:
                for u in range(PR):
                    step(it * PR + u, u)
            for b in range(NB, NB + lag):
                step(b, b % PR)

        def live(b):
            return not isinstance(b, int) or b < NB

        @block.sync
        def _(sp):
            sp.dma_start(wl[:, :], a.wl[layer]).then_inc(loaded, 16)
            sp.dma_start(wr[:, :], a.wr[layer]).then_inc(loaded, 16)
            sp.dma_start(bl[:, :], a.bl[layer:layer + 1, :].broadcast_to([128, D])).then_inc(loaded, 16)

            back = 4 if last_layer else 3

            def step(b, u):
                if reached(b, back):
                    m, v = b - back, (u - back) % PR
                    sp.wait_ge(made, m + 1)
                    target = out if last_layer else k.d_node
                    source = res[0:NP, v, :] if last_layer else k.nodes[0:NP, bass.ds(m, 1), 0:D].rearrange("p a d -> p (a d)")
                    sp.dma_start(target[bass.ds(m * NP, NP), :], source).then_inc(stored[v], 16)

            steps(sp, back, step)
            for u in range(PR):
                sp.wait_ge(stored[u], 16 * (NB // PR))

        @block.vector
        def _(dve):
            ch = Chain(dve, own)
            ch.link(dve.tensor_scalar(inv[0:NP, :], acc[0:NP, 0:NB, D], 1.0, None, ALU.max))
            ch.link(dve.reciprocal(inv[0:NP, :], inv[0:NP, :]))
            dve.wait_ge(loaded, 48)

            def step(b, u):
                if live(b):
                    if reached(b, PR):
                        dve.wait_ge(turned, b - PR + 1)
                    dve.tensor_scalar(mean[0:NP, u, :], acc[0:NP, bass.ds(b, 1), 0:D].rearrange("p a d -> p (a d)"),
                                      inv[0:NP, bass.ds(b, 1)], None, ALU.mult).then_inc(meaned, 1)
                if reached(b, 3) and live(b - 3):
                    m, v = b - 3, (u - 3) % PR
                    dve.wait_ge(multiplied, m + 1)
                    if reached(m, PR):
                        dve.wait_ge(made, m - PR + 1)
                    dve.tensor_tensor(raw[0:NP, v, :], ps_o[v][0:NP, :], bl[0:NP, :], ALU.add).then_inc(biased, 1)
                if last_layer and reached(b, 4):
                    m, v = b - 4, u
                    dve.wait_ge(x1_in[v], uses(m, v, PR, 16))
                    dve.wait_ge(biased, m + 1)
                    if reached(m, PR):
                        dve.wait_ge(stored[v], uses(m - PR, v, PR, 16))
                    dve.tensor_tensor(res[0:NP, v, :], raw[0:NP, v, :], x1[0:NP, v, :], ALU.add).then_inc(made, 1)

            steps(dve, 4 if last_layer else 3, step)

        @block.tensor
        def _(pe):
            pe.wait_ge(loaded, 48)

            def step(b, u):
                if live(b):
                    pe.wait_ge(meaned, b + 1)
                    pe.wait_ge(stilled, b + 1)
                    if reached(b, PR):
                        pe.wait_ge(copied, b - PR + 1)
                    pe.transpose(ps_t[u][:, 0, 0:NP], mean[0:NP, u, :], k.ident[0:NP, 0:NP])
                    pe.transpose(ps_t[u][:, 1, 0:NP], still[0:NP, u, :],
                                 k.ident[0:NP, 0:NP]).then_inc(turned, 1)
                if reached(b, 1):
                    m, v = b - 1, (u - 1) % PR
                    pe.wait_ge(copied, m + 1)
                    if reached(m, PR):
                        pe.wait_ge(biased, m - PR + 1)
                    pe.matmul(ps_o[v][0:NP, :], turned_sb[:, v, 0, :], wl[:, :], start=True, stop=False)
                    pe.matmul(ps_o[v][0:NP, :], turned_sb[:, v, 1, :], wr[:, :], start=False, stop=True).then_inc(multiplied, 1)

            steps(pe, 1, step)

        @block.gpsimd
        def _(pool):
            def step(b, u):
                if reached(b, PR):
                    pool.wait_ge(turned, b - PR + 1)
                pool.tensor_copy(still[0:NP, u, :], k.nodes[0:NP, bass.ds(b, 1), 0:D].rearrange("p a d -> p (a d)")).then_inc(stilled, 1)

            steps(pool, 0, step)

        @block.scalar
        def _(act):
            def step(b, u):
                if live(b):
                    act.wait_ge(turned, b + 1)
                    if reached(b, PR):
                        act.wait_ge(multiplied, b - PR + 1)
                    act.copy(turned_sb[:, u, :, :], ps_t[u][:, :, 0:NP]).then_inc(copied, 1)
                if live(b) and last_layer:
                    if reached(b, PR):
                        act.wait_ge(made, b - PR + 1)
                    act.dma_start(x1[0:NP, u, :], k.d_x1[bass.ds(b * NP, NP), :]).then_inc(x1_in[u], 16)
                if reached(b, 3) and not last_layer:
                    m, v = b - 3, (u - 3) % PR
                    act.wait_ge(biased, m + 1)
                    act.activation(k.nodes[0:NP, bass.ds(m, 1), 0:D].rearrange("p a d -> p (a d)"), raw[0:NP, v, :],
                                   ACT.Relu).then_inc(made, 1)

            steps(act, 3, step)


def graph_kernel(nc, a, out):
    s = Shapes(a.x, a.src)
    k = Store()
    k.tag = "prepare_"

    def dram(name, shape, dt=F32):
        return nc.dram_tensor(name, shape, dt, kind="Internal").ap()

    k.d_tile_of = dram("d_tile_of", [s.I], I32)
    k.d_block_of = dram("d_block_of", [s.I], I32)
    k.d_kv = dram("d_kv", [s.N, KVW])
    k.d_skip = dram("d_skip", [s.N, D])
    k.d_attr = dram("d_attr", [s.G, 128, GR * EP])
    k.d_value = dram("d_value", [s.G, EP, GR * D])
    k.d_x1 = dram("d_x1", [s.N, D])
    k.d_node = dram("d_node", [s.N, D])
    with ExitStack() as c:
        def sb(name, shape, dt=F32):
            return c.enter_context(nc.sbuf_tensor(name, shape, dt))

        k.ident = sb("ident", [128, 128])
        k.ident_b = sb("ident_b", [128, 128], BF16)
        k.node_iota_i = sb("node_iota_i", [128, NP], I32)
        k.node_iota = sb("node_iota", [128, NP])
        k.node_iota_b = sb("node_iota_b", [128, NP], BF16)
        k.ones = sb("ones", [128, 128])
        k.zero = sb("zero", [128, 1])
        k.eps = sb("eps", [128, 1])
        walk = sb("walk", [2, s.I], I32)
        k.tile_row, k.block_row = walk[0:1, :], walk[1:2, :]
        k.local = sb("local_t", [128, s.I])
        k.local_b = sb("local_b", [128, s.I], BF16)
        k.src = sb("src_t", [128, s.I + UNROLL * GR], I32)
        k.weight = sb("weight_t", [128, s.I])
        k.key = sb("key", [128, NG * EP])
        k.vec = sb("vec", [128, s.NB])
        constants(nc, k)
        item_tables(nc, k, s, a)

        k.score = sb("score", [128, s.I * HEADS])
        big = max((s.NB + 1) * ACW, (HEADS + 2) * NG * EP, GR * (UNROLL * KVW + 2 * RING * D))
        k.big1 = sb("big1", [128, big])
        k.big2 = sb("big2", [128, big])
        k.query = k.big1[:, 0:(s.NB + 1) * ACW].rearrange("p (b d) -> p b d", d=ACW)
        k.nodes = k.big2[:, 0:(s.NB + 1) * ACW].rearrange("p (b d) -> p b d", d=ACW)
        k.acc = lambda weighted: k.nodes if weighted else k.query
        k.big_acc = lambda weighted: k.big2 if weighted else k.big1

        load_vec(nc, k, s, a)
        layer_norm(nc, k, s, load=a.x)
        for n in range(2):
            k.tag = f"conv{n}_"
            project_nodes(nc, k, s, a.convs[n], residual=a.x if n == 1 else None)
            edge_scores(nc, k, s, a, a.convs[n], first=n == 0)
            softmax_weights(nc, k, s)
            add_up(nc, k, s, weighted=True)
            finish_conv(nc, k, s, store=k.d_x1 if n == 1 else None)
        k.tag = "between_"
        layer_norm(nc, k, s, store=k.d_node)
        layers = a.wl.shape[0]
        for n in range(layers):
            k.tag = f"mean{n}_"
            add_up(nc, k, s, weighted=False)
            finish_mean_layer(nc, k, s, a, n, layers, out)


def layout(inputs):
    import numpy as np

    N = inputs["x"].shape[0]
    pad = -inputs["src"].shape[0] % EP
    edge = lambda v, fill: np.concatenate([np.asarray(v), np.full((pad,) + v.shape[1:], fill, v.dtype)])
    arrays = {
        "x": inputs["x"], "vec": inputs["node_vec"],
        "src": edge(inputs["src"], 0).reshape(-1, EP),
        "dst": edge(inputs["dst"], N).reshape(-1, EP),
        "weight": edge(inputs["edge_weight"], 0).reshape(-1, EP),
        "message": edge(inputs["edge_attr_64"], 0).reshape(-1, EP, MSG),
        "wt": inputs["L0_gnn_Wt"], "bt": inputs["L0_gnn_bt"], "bl": inputs["L1_gnn_bl"],
        "wl": np.swapaxes(np.asarray(inputs["L1_gnn_Wl"]), 1, 2),
        "wr": np.swapaxes(np.asarray(inputs["L1_gnn_Wr"]), 1, 2),
    }
    for n in "12":
        arrays["we" + n] = inputs["L0_gnn_We" + n]
        for name in ("q", "k", "v", "skip"):
            arrays[f"w{name}{n}"] = inputs[f"L0_gnn_W{name}{n}"]
            arrays[f"b{name}{n}"] = inputs[f"L0_gnn_b{name}{n}"]
    return {name: np.ascontiguousarray(v) for name, v in arrays.items()}


def build(nc, arrays):
    def tensor(name):
        v = arrays[name]
        return nc.dram_tensor(f"in_{name}", v.shape, mybir.dt.from_np(v.dtype), kind="ExternalInput").ap()

    a = Store()
    a.x, a.vec = tensor("x"), tensor("vec")
    a.src, a.dst, a.weight, a.message = tensor("src"), tensor("dst"), tensor("weight"), tensor("message")
    a.wt, a.bt = tensor("wt"), tensor("bt")
    a.wl, a.wr, a.bl = tensor("wl"), tensor("wr"), tensor("bl")
    a.convs = []
    for n in "12":
        conv = Store()
        conv.edge = tensor("we" + n)
        conv.weights = [tensor(f"w{p}{n}") for p in ("q", "k", "v", "skip")]
        conv.biases = [tensor(f"b{p}{n}") for p in ("q", "k", "v", "skip")]
        a.convs.append(conv)
    out = nc.dram_tensor("out_0_dram", arrays["x"].shape, F32, kind="ExternalOutput").ap()
    graph_kernel(nc, a, out)


def kernel(**inputs):
    import concourse.bacc as _bacc
    from concourse.bass_utils import run_bass_kernel_spmd as _run

    nc = _bacc.Bacc("TRN2", target_bir_lowering=False, num_devices=1)
    arrays = layout(inputs)
    build(nc, arrays)
    r = _run(nc, [{f"in_{name}": v for name, v in arrays.items()}], core_ids=[0])
    return r.results[0]["out_0_dram"]
```
